# Optimizing a Trainium2 kernel written in Bass

```python
import numpy as np
import jax
import jax.numpy as jnp

def _softmax(x, axis=-1):
    return jax.nn.softmax(x, axis=axis)

def _gelu(x):
    return jax.nn.gelu(x, approximate=True)

def _silu(x):
    return jax.nn.silu(x)

def _sigmoid(x):
    return jax.nn.sigmoid(x)

def _layernorm(x, axis=-1, eps=1e-05):
    m = jnp.mean(x, axis=axis, keepdims=True)
    v = jnp.var(x, axis=axis, keepdims=True)
    return (x - m) / jnp.sqrt(v + eps)

def _scatter_add(tgt, idx, src, axis=0):
    return tgt.at[idx].add(src)

def _segment_sum(src, seg, n):
    return jax.ops.segment_sum(src, seg, n)
kernel_name = 'mk_conv_attn_hybrid_d4_conv_nchw256_r2_224a0c'

def setup_inputs(seed: int=0):
    np.random.seed(seed)
    _w = jnp.asarray

    def _rec_inputs():
        import jax
        import jax.numpy as jnp
        _gk = jax.random.key(seed)
        x = -0.0002928 + 1 * jax.random.normal(jax.random.fold_in(_gk, 1), (4, 128, 32, 32), jnp.float32)
        return x
    x = _rec_inputs()

    def _L0_conv_setup():
        import jax, jax.numpy as jnp
        import numpy as np
        B, C, CI, H, W = (4, 128, 64, 32, 32)
        BN_EPS = 1e-05
        key = jax.random.key(seed)
        ks = jax.random.split(key, 11)
        s_in = 1.0 / np.sqrt(C)
        s_mid = 1.0 / np.sqrt(CI)
        return {'x': jax.random.normal(ks[0], (B, C, H, W), jnp.float32), 'theta_w': jax.random.normal(ks[1], (CI, C), jnp.float32) * s_in, 'theta_b': jax.random.normal(ks[2], (CI,), jnp.float32) * s_in, 'phi_w': jax.random.normal(ks[3], (CI, C), jnp.float32) * s_in, 'phi_b': jax.random.normal(ks[4], (CI,), jnp.float32) * s_in, 'g_w': jax.random.normal(ks[5], (CI, C), jnp.float32) * s_in, 'g_b': jax.random.normal(ks[6], (CI,), jnp.float32) * s_in, 'w_w': jax.random.normal(ks[7], (C, CI), jnp.float32) * s_mid, 'w_b': jax.random.normal(ks[8], (C,), jnp.float32) * s_mid, 'gamma': jax.random.normal(ks[9], (C,), jnp.float32) * 0.1 + 1.0, 'beta': jax.random.normal(ks[10], (C,), jnp.float32) * 0.1}
    _L0_conv_all = _L0_conv_setup()
    _L0_conv_in = {k: v for k, v in _L0_conv_all.items() if k in ('theta_w', 'theta_b', 'phi_w', 'phi_b', 'g_w', 'g_b', 'w_w', 'w_b', 'gamma', 'beta')}
    del _L0_conv_all

    def _L1_conv_setup():
        import jax, jax.numpy as jnp
        import numpy as np
        POOL = 16
        LOW = 4
        KS = 3
        PAD = 1
        GROUPS = 1

        def _dct_matrix(size):
            n = jnp.arange(size, dtype=jnp.float32)
            k = n[:, None]
            return jnp.cos((2.0 * k + 1.0) * n * jnp.pi / (2.0 * size)) / size
        key = jax.random.key(seed)
        ks = jax.random.split(key, 10)
        B, C, H, W = (16, 128, 32, 32)
        E, O = (8, 128)
        hidden = max(32, C // 16)
        x = jax.random.normal(ks[0], (B, C, H, W), jnp.float32)
        experts = jax.random.normal(ks[1], (E, O, C // GROUPS, KS, KS), jnp.float32) * np.sqrt(2.0 / (O * KS * KS))
        w_r1 = jax.random.normal(ks[2], (C, hidden), jnp.float32) * 0.05
        b_r1 = jnp.zeros((hidden,), jnp.float32)
        w_r2 = jax.random.normal(ks[3], (hidden, E), jnp.float32) * 0.05
        b_r2 = jnp.zeros((E,), jnp.float32)
        w_f1 = jax.random.normal(ks[4], (LOW * LOW, 32), jnp.float32) * 0.1
        b_f1 = jnp.zeros((32,), jnp.float32)
        w_f2 = jax.random.normal(ks[5], (32, 1), jnp.float32) * 0.1
        b_f2 = jnp.zeros((1,), jnp.float32)
        return {'x': x, 'experts': experts, 'w_r1': w_r1, 'b_r1': b_r1, 'w_r2': w_r2, 'b_r2': b_r2, 'w_f1': w_f1, 'b_f1': b_f1, 'w_f2': w_f2, 'b_f2': b_f2}
    _L1_conv_all = _L1_conv_setup()
    _L1_conv_in = {k: v for k, v in _L1_conv_all.items() if k in ('experts', 'w_r1', 'b_r1', 'w_r2', 'b_r2', 'w_f1', 'b_f1', 'w_f2', 'b_f2')}
    del _L1_conv_all

    def _L2_attn_setup():
        import jax, jax.numpy as jnp
        import numpy as np
        N_HEAD = 4
        key = jax.random.key(seed)
        k1, k2, k3 = jax.random.split(key, 3)
        B, T, C = (8, 1024, 128)
        x = jax.random.normal(k1, (B, T, C), dtype=jnp.float32)
        W_attn = jax.random.normal(k2, (C, 3 * C), dtype=jnp.float32) / np.sqrt(C)
        W_proj = jax.random.normal(k3, (C, C), dtype=jnp.float32) / np.sqrt(C)
        return {'x': x, 'W_attn': W_attn, 'W_proj': W_proj}
    _L2_attn_all = _L2_attn_setup()
    _L2_attn_in = {k: v for k, v in _L2_attn_all.items() if k in ('W_attn', 'W_proj')}
    del _L2_attn_all

    def _L2_ffn_setup():
        import jax, jax.numpy as jnp
        import numpy as np
        B, S, D = (8, 2048, 128)
        H = 4 * D
        CAPACITY = 0.5
        key = jax.random.key(seed)
        ks = jax.random.split(key, 6)
        x = jax.random.normal(ks[0], (B, S, D), dtype=jnp.float32)
        attention_mask = jnp.zeros((B, 1, 1, S), dtype=jnp.float32)
        wr = jax.random.normal(ks[1], (D, 1), dtype=jnp.float32) * 0.02
        br = jnp.zeros((1,), dtype=jnp.float32)
        w1 = jax.random.normal(ks[2], (D, H), dtype=jnp.float32) * 0.02
        b1 = jnp.zeros((H,), dtype=jnp.float32)
        w2 = jax.random.normal(ks[3], (H, D), dtype=jnp.float32) * 0.02
        b2 = jnp.zeros((D,), dtype=jnp.float32)
        return {'x': x, 'attention_mask': attention_mask, 'wr': wr, 'br': br, 'w1': w1, 'b1': b1, 'w2': w2, 'b2': b2}
    _L2_ffn_all = _L2_ffn_setup()
    _L2_ffn_in = {k: v for k, v in _L2_ffn_all.items() if k in ('attention_mask', 'wr', 'br', 'w1', 'b1', 'w2', 'b2')}
    del _L2_ffn_all

    def _L3_attn_setup():
        import jax, jax.numpy as jnp
        import numpy as np
        N_HEAD = 16
        NOPE = 32
        ROPE = 32
        VDIM = 32
        HD = NOPE + ROPE
        WINDOW = 64
        KEEP = 256
        EPS = 1e-06

        def _freqs(T, dim=ROPE, theta=10000.0):
            f = 1.0 / theta ** (np.arange(0, dim, 2, dtype=np.float32) / dim)
            ang = np.outer(np.arange(T, dtype=np.float32), f)
            return (jnp.asarray(np.cos(ang)), jnp.asarray(np.sin(ang)))

        def _rms(x, w):
            return x * jax.lax.rsqrt(jnp.mean(x * x, -1, keepdims=True) + EPS) * w

        def _rope(x, cos, sin):
            T = x.shape[-2]
            c = cos[:T][None, None]
            s = sin[:T][None, None]
            xr, xi = jnp.split(x, 2, -1)
            return jnp.concatenate([xr * c - xi * s, xr * s + xi * c], -1)

        def _attn(q, k, v, mask=None):
            s = jnp.einsum('bhqd,bhkd->bhqk', q, k) / np.float32(np.sqrt(HD))
            if mask is not None:
                s = jnp.where(mask, s, jnp.float32(-1000000000.0))
            return jnp.einsum('bhqk,bhkd->bhqd', jax.nn.softmax(s, -1), v)
        key = jax.random.key(seed)
        ks = jax.random.split(key, 16)
        w = lambda k, shape: jax.random.normal(k, shape, jnp.float32) * 0.02
        B, T, C = (2, 1024, 128)
        return {'x': jax.random.normal(ks[0], (B, T, C), jnp.float32), 'Wcq': w(ks[1], (C, 48)), 'q_norm_w': jnp.ones((48,), jnp.float32), 'Wq_nope': w(ks[2], (48, N_HEAD * NOPE)), 'Wq_rope': w(ks[3], (48, N_HEAD * ROPE)), 'Wckv': w(ks[4], (C, 32)), 'kv_norm_w': jnp.ones((32,), jnp.float32), 'Wk_nope': w(ks[5], (32, N_HEAD * NOPE)), 'Wv': w(ks[6], (32, N_HEAD * VDIM)), 'Wk_rope': w(ks[7], (C, ROPE)), 'W_imp': w(ks[8], (C, 1)), 'Wsel_k': w(ks[9], (C, N_HEAD * HD)), 'Wsel_v': w(ks[10], (C, N_HEAD * VDIM)), 'Wwin_k': w(ks[11], (C, N_HEAD * HD)), 'Wwin_v': w(ks[12], (C, N_HEAD * VDIM)), 'Wgate': w(ks[13], (C, 3)), 'Wproj': w(ks[14], (N_HEAD * VDIM, C))}
    _L3_attn_all = _L3_attn_setup()
    _L3_attn_in = {k: v for k, v in _L3_attn_all.items() if k in ('Wcq', 'q_norm_w', 'Wq_nope', 'Wq_rope', 'Wckv', 'kv_norm_w', 'Wk_nope', 'Wv', 'Wk_rope', 'W_imp', 'Wsel_k', 'Wsel_v', 'Wwin_k', 'Wwin_v', 'Wgate', 'Wproj')}
    del _L3_attn_all

    def _L3_ffn_setup():
        import math
        import jax, jax.numpy as jnp
        import numpy as np
        CAPACITY_FACTOR = 1.25
        key = jax.random.key(seed)
        ks = jax.random.split(key, 5)
        B, L, D, F, E = (8, 4096, 128, 512, 8)
        h = jax.random.normal(ks[0], (B, L, D), dtype=jnp.float32)
        gate_w = jax.random.normal(ks[1], (D, E), dtype=jnp.float32) * 0.02
        gate_b = jnp.zeros((E,), dtype=jnp.float32)
        w1 = jax.random.normal(ks[2], (E, D, F), dtype=jnp.float32) * (1.0 / math.sqrt(D))
        b1 = jnp.zeros((E, F), dtype=jnp.float32)
        w2 = jax.random.normal(ks[3], (E, F, D), dtype=jnp.float32) * (1.0 / math.sqrt(F))
        b2 = jnp.zeros((E, D), dtype=jnp.float32)
        return {'h': h, 'gate_w': gate_w, 'gate_b': gate_b, 'w1': w1, 'b1': b1, 'w2': w2, 'b2': b2}
    _L3_ffn_all = _L3_ffn_setup()
    _L3_ffn_in = {k: v for k, v in _L3_ffn_all.items() if k in ('gate_w', 'gate_b', 'w1', 'b1', 'w2', 'b2')}
    del _L3_ffn_all
    return {'x': x, 'L0_conv_theta_w': _L0_conv_in['theta_w'], 'L0_conv_theta_b': _L0_conv_in['theta_b'], 'L0_conv_phi_w': _L0_conv_in['phi_w'], 'L0_conv_phi_b': _L0_conv_in['phi_b'], 'L0_conv_g_w': _L0_conv_in['g_w'], 'L0_conv_g_b': _L0_conv_in['g_b'], 'L0_conv_w_w': _L0_conv_in['w_w'], 'L0_conv_w_b': _L0_conv_in['w_b'], 'L0_conv_gamma': _L0_conv_in['gamma'], 'L0_conv_beta': _L0_conv_in['beta'], 'L1_conv_experts': _L1_conv_in['experts'], 'L1_conv_w_r1': _L1_conv_in['w_r1'], 'L1_conv_b_r1': _L1_conv_in['b_r1'], 'L1_conv_w_r2': _L1_conv_in['w_r2'], 'L1_conv_b_r2': _L1_conv_in['b_r2'], 'L1_conv_w_f1': _L1_conv_in['w_f1'], 'L1_conv_b_f1': _L1_conv_in['b_f1'], 'L1_conv_w_f2': _L1_conv_in['w_f2'], 'L1_conv_b_f2': _L1_conv_in['b_f2'], 'L2_attn_W_attn': _L2_attn_in['W_attn'], 'L2_attn_W_proj': _L2_attn_in['W_proj'], 'L2_ffn_attention_mask': _L2_ffn_in['attention_mask'], 'L2_ffn_wr': _L2_ffn_in['wr'], 'L2_ffn_br': _L2_ffn_in['br'], 'L2_ffn_w1': _L2_ffn_in['w1'], 'L2_ffn_b1': _L2_ffn_in['b1'], 'L2_ffn_w2': _L2_ffn_in['w2'], 'L2_ffn_b2': _L2_ffn_in['b2'], 'L3_attn_Wcq': _L3_attn_in['Wcq'], 'L3_attn_q_norm_w': _L3_attn_in['q_norm_w'], 'L3_attn_Wq_nope': _L3_attn_in['Wq_nope'], 'L3_attn_Wq_rope': _L3_attn_in['Wq_rope'], 'L3_attn_Wckv': _L3_attn_in['Wckv'], 'L3_attn_kv_norm_w': _L3_attn_in['kv_norm_w'], 'L3_attn_Wk_nope': _L3_attn_in['Wk_nope'], 'L3_attn_Wv': _L3_attn_in['Wv'], 'L3_attn_Wk_rope': _L3_attn_in['Wk_rope'], 'L3_attn_W_imp': _L3_attn_in['W_imp'], 'L3_attn_Wsel_k': _L3_attn_in['Wsel_k'], 'L3_attn_Wsel_v': _L3_attn_in['Wsel_v'], 'L3_attn_Wwin_k': _L3_attn_in['Wwin_k'], 'L3_attn_Wwin_v': _L3_attn_in['Wwin_v'], 'L3_attn_Wgate': _L3_attn_in['Wgate'], 'L3_attn_Wproj': _L3_attn_in['Wproj'], 'L3_ffn_gate_w': _L3_ffn_in['gate_w'], 'L3_ffn_gate_b': _L3_ffn_in['gate_b'], 'L3_ffn_w1': _L3_ffn_in['w1'], 'L3_ffn_b1': _L3_ffn_in['b1'], 'L3_ffn_w2': _L3_ffn_in['w2'], 'L3_ffn_b2': _L3_ffn_in['b2']}

def reference(x, L0_conv_theta_w, L0_conv_theta_b, L0_conv_phi_w, L0_conv_phi_b, L0_conv_g_w, L0_conv_g_b, L0_conv_w_w, L0_conv_w_b, L0_conv_gamma, L0_conv_beta, L1_conv_experts, L1_conv_w_r1, L1_conv_b_r1, L1_conv_w_r2, L1_conv_b_r2, L1_conv_w_f1, L1_conv_b_f1, L1_conv_w_f2, L1_conv_b_f2, L2_attn_W_attn, L2_attn_W_proj, L2_ffn_attention_mask, L2_ffn_wr, L2_ffn_br, L2_ffn_w1, L2_ffn_b1, L2_ffn_w2, L2_ffn_b2, L3_attn_Wcq, L3_attn_q_norm_w, L3_attn_Wq_nope, L3_attn_Wq_rope, L3_attn_Wckv, L3_attn_kv_norm_w, L3_attn_Wk_nope, L3_attn_Wv, L3_attn_Wk_rope, L3_attn_W_imp, L3_attn_Wsel_k, L3_attn_Wsel_v, L3_attn_Wwin_k, L3_attn_Wwin_v, L3_attn_Wgate, L3_attn_Wproj, L3_ffn_gate_w, L3_ffn_gate_b, L3_ffn_w1, L3_ffn_b1, L3_ffn_w2, L3_ffn_b2):
    import jax
    import jax.numpy as jnp

    def _L0_conv_ref(x, theta_w, theta_b, phi_w, phi_b, g_w, g_b, w_w, w_b, gamma, beta):
        import jax, jax.numpy as jnp
        import numpy as np
        B, C, CI, H, W = (4, 128, 64, 32, 32)
        BN_EPS = 1e-05
        b, c, h, w = x.shape
        n = h * w
        xf = x.reshape(b, c, n)
        theta_x = jnp.einsum('ic,bcn->bni', theta_w, xf) + theta_b
        phi_x = jnp.einsum('ic,bcn->bin', phi_w, xf) + phi_b[None, :, None]
        g_x = jnp.einsum('ic,bcn->bni', g_w, xf) + g_b
        f = jnp.einsum('bni,bim->bnm', theta_x, phi_x) / n
        y = jnp.einsum('bnm,bmi->bni', f, g_x)
        y = y.transpose(0, 2, 1).reshape(b, theta_w.shape[0], h, w)
        wy = jnp.einsum('ci,bihw->bchw', w_w, y) + w_b[None, :, None, None]
        mean = jnp.mean(wy, axis=(0, 2, 3), keepdims=True)
        var = jnp.var(wy, axis=(0, 2, 3), keepdims=True)
        wy_bn = (wy - mean) * jax.lax.rsqrt(var + BN_EPS)
        wy_bn = wy_bn * gamma[None, :, None, None] + beta[None, :, None, None]
        return wy_bn + x

    def _L1_conv_ref(x, experts, w_r1, b_r1, w_r2, b_r2, w_f1, b_f1, w_f2, b_f2):
        import jax, jax.numpy as jnp
        import numpy as np
        POOL = 16
        LOW = 4
        KS = 3
        PAD = 1
        GROUPS = 1

        def _dct_matrix(size):
            n = jnp.arange(size, dtype=jnp.float32)
            k = n[:, None]
            return jnp.cos((2.0 * k + 1.0) * n * jnp.pi / (2.0 * size)) / size
        B, C, H, W = x.shape
        xp = x.reshape(B, C, POOL, H // POOL, POOL, W // POOL).mean(axis=(3, 5))
        M = _dct_matrix(POOL)
        dct_low = jnp.einsum('bchw,hi,wj->bcij', xp, M, M)[..., :LOW, :LOW]
        freq = dct_low.reshape(B, C, LOW * LOW)
        f = jax.nn.sigmoid(jax.nn.relu(freq @ w_f1 + b_f1) @ w_f2 + b_f2)[..., 0]
        route = jax.nn.softmax(jax.nn.relu(f @ w_r1 + b_r1) @ w_r2 + b_r2, axis=-1)
        dyn_k = jnp.einsum('be,eoihw->boihw', route, experts)

        def conv_one(xi, ki):
            out = jax.lax.conv_general_dilated(xi[None], ki, window_strides=(1, 1), padding=[(PAD, PAD), (PAD, PAD)], dimension_numbers=('NCHW', 'OIHW', 'NCHW'), feature_group_count=GROUPS)
            return out[0]
        return jax.vmap(conv_one)(x, dyn_k)

    def _L2_attn_ref(x, W_attn, W_proj):
        import jax, jax.numpy as jnp
        import numpy as np
        N_HEAD = 4
        B, T, C = x.shape
        hs = C // N_HEAD
        qkv = x @ W_attn
        q, k, v = jnp.split(qkv, 3, axis=2)

        def to_heads(t):
            return t.reshape(B, T, N_HEAD, hs).transpose(0, 2, 1, 3)
        q, k, v = (to_heads(q), to_heads(k), to_heads(v))
        scale = 1.0 / np.sqrt(hs).astype(np.float32)
        att = jnp.einsum('bhqd,bhkd->bhqk', q, k) * scale
        causal = jnp.tril(jnp.ones((T, T), dtype=bool))
        att = jnp.where(causal, att, jnp.finfo(att.dtype).min)
        att = jax.nn.softmax(att, axis=-1)
        y = jnp.einsum('bhqk,bhkd->bhqd', att, v)
        y = y.transpose(0, 2, 1, 3).reshape(B, T, C)
        return y @ W_proj

    def _L2_ffn_ref(x, attention_mask, wr, br, w1, b1, w2, b2):
        import jax, jax.numpy as jnp
        import numpy as np
        B, S, D = (8, 2048, 128)
        H = 4 * D
        CAPACITY = 0.5
        b, s, d = x.shape
        weights = (jnp.einsum('bsd,do->bso', x, wr) + br)[..., 0]
        k = max(1, int(CAPACITY * s))
        kk = k - 1 if k > 1 else 1
        _, idx = jax.lax.top_k(weights, k)
        sel_idx = idx[:, :kk]
        sel = jnp.take_along_axis(x, sel_idx[:, :, None], axis=1)
        h = jax.nn.gelu(jnp.einsum('bkd,dh->bkh', sel, w1) + b1)
        y = jnp.einsum('bkh,hd->bkd', h, w2) + b2
        w_sel = jnp.take_along_axis(weights, sel_idx, axis=1)
        y = y * w_sel[..., None]
        batch_idx = jnp.arange(b)[:, None]
        processed = jnp.zeros_like(x).at[batch_idx, sel_idx].set(y)
        return processed + x

    def _L3_attn_ref(x, Wcq, q_norm_w, Wq_nope, Wq_rope, Wckv, kv_norm_w, Wk_nope, Wv, Wk_rope, W_imp, Wsel_k, Wsel_v, Wwin_k, Wwin_v, Wgate, Wproj):
        import jax, jax.numpy as jnp
        import numpy as np
        N_HEAD = 16
        NOPE = 32
        ROPE = 32
        VDIM = 32
        HD = NOPE + ROPE
        WINDOW = 64
        KEEP = 256
        EPS = 1e-06

        def _freqs(T, dim=ROPE, theta=10000.0):
            f = 1.0 / theta ** (np.arange(0, dim, 2, dtype=np.float32) / dim)
            ang = np.outer(np.arange(T, dtype=np.float32), f)
            return (jnp.asarray(np.cos(ang)), jnp.asarray(np.sin(ang)))

        def _rms(x, w):
            return x * jax.lax.rsqrt(jnp.mean(x * x, -1, keepdims=True) + EPS) * w

        def _rope(x, cos, sin):
            T = x.shape[-2]
            c = cos[:T][None, None]
            s = sin[:T][None, None]
            xr, xi = jnp.split(x, 2, -1)
            return jnp.concatenate([xr * c - xi * s, xr * s + xi * c], -1)

        def _attn(q, k, v, mask=None):
            s = jnp.einsum('bhqd,bhkd->bhqk', q, k) / np.float32(np.sqrt(HD))
            if mask is not None:
                s = jnp.where(mask, s, jnp.float32(-1000000000.0))
            return jnp.einsum('bhqk,bhkd->bhqd', jax.nn.softmax(s, -1), v)
        B, T, C = x.shape
        cos, sin = _freqs(T)
        cq = _rms(x @ Wcq, q_norm_w)
        qn = (cq @ Wq_nope).reshape(B, T, N_HEAD, NOPE).transpose(0, 2, 1, 3)
        qr = _rope((cq @ Wq_rope).reshape(B, T, N_HEAD, ROPE).transpose(0, 2, 1, 3), cos, sin)
        q = jnp.concatenate([qn, qr], -1)
        gate = jax.nn.softmax((x @ Wgate).mean(1), -1)
        ckv = _rms(x @ Wckv, kv_norm_w)
        kn = (ckv @ Wk_nope).reshape(B, T, N_HEAD, NOPE).transpose(0, 2, 1, 3)
        v1 = (ckv @ Wv).reshape(B, T, N_HEAD, VDIM).transpose(0, 2, 1, 3)
        kr = (x @ Wk_rope / N_HEAD).reshape(B, T, 1, ROPE).transpose(0, 2, 1, 3)
        kr = _rope(kr, cos, sin)
        k1 = jnp.concatenate([kn, jnp.broadcast_to(kr, (B, N_HEAD, T, ROPE))], -1)
        ii = jnp.arange(T)
        causal = ii[:, None] >= ii[None, :]
        o1 = _attn(q, k1, v1, causal[None, None])
        scores = (x @ W_imp)[..., 0]
        _, idx = jax.lax.top_k(scores, KEEP)
        idx = jnp.sort(idx, 1)
        sel = jnp.take_along_axis(x, idx[..., None], 1)
        ks = (sel @ Wsel_k).reshape(B, KEEP, N_HEAD, HD).transpose(0, 2, 1, 3)
        vs = (sel @ Wsel_v).reshape(B, KEEP, N_HEAD, VDIM).transpose(0, 2, 1, 3)
        ks = jnp.concatenate([ks[..., :NOPE], _rope(ks[..., NOPE:], cos, sin)], -1)
        o2 = _attn(q, ks, vs)
        kw = (x @ Wwin_k).reshape(B, T, N_HEAD, HD).transpose(0, 2, 1, 3)
        vw = (x @ Wwin_v).reshape(B, T, N_HEAD, VDIM).transpose(0, 2, 1, 3)
        kw = jnp.concatenate([kw[..., :NOPE], _rope(kw[..., NOPE:], cos, sin)], -1)
        winmask = causal & (ii[:, None] - ii[None, :] < WINDOW)
        o3 = _attn(q, kw, vw, winmask[None, None])
        g = gate[:, :, None, None, None]
        o = g[:, 0] * o1 + g[:, 1] * o2 + g[:, 2] * o3
        o = o.transpose(0, 2, 1, 3).reshape(B, T, N_HEAD * VDIM)
        return o @ Wproj

    def _L3_ffn_ref(h, gate_w, gate_b, w1, b1, w2, b2):
        import math
        import jax, jax.numpy as jnp
        import numpy as np
        CAPACITY_FACTOR = 1.25
        B, L, D = h.shape
        E = gate_w.shape[1]
        T = B * L
        C = max(1, math.ceil(CAPACITY_FACTOR * T / E))
        x = h.reshape(T, D)
        logits = x @ gate_w + gate_b
        probs = jax.nn.softmax(logits, axis=-1)
        idx = jnp.argmax(probs, axis=-1)
        prb = jnp.take_along_axis(probs, idx[:, None], axis=1)[:, 0]
        one_hot = jax.nn.one_hot(idx, E, dtype=jnp.float32)
        pos = (jnp.cumsum(one_hot, axis=0) * one_hot).sum(-1).astype(jnp.int32) - 1
        kept = pos < C
        pos_safe = jnp.where(kept, pos, C)
        buf = jnp.zeros((E, C, D), dtype=h.dtype).at[idx, pos_safe].set(x, mode='drop')
        hmid = jax.nn.relu(jnp.einsum('ecd,edf->ecf', buf, w1) + b1[:, None, :])
        ybuf = jnp.einsum('ecf,efd->ecd', hmid, w2) + b2[:, None, :]
        pos_g = jnp.minimum(pos, C - 1)
        y_tok = ybuf[idx, pos_g] * (prb * kept)[:, None]
        y = y_tok.reshape(B, L, D)
        y = jnp.nan_to_num(y, nan=0.0, posinf=10000.0, neginf=-10000.0)
        return y

    def _gn(v, G=32, eps=1e-05):
        B_, C_, H_, W_ = v.shape
        g = v.reshape(B_, G, C_ // G, H_, W_)
        m = jnp.mean(g, axis=(2, 3, 4), keepdims=True)
        s = jnp.var(g, axis=(2, 3, 4), keepdims=True)
        return ((g - m) / jnp.sqrt(s + eps)).reshape(v.shape)

    def _ln_c(v, eps=1e-06):
        m = jnp.mean(v, axis=1, keepdims=True)
        s = jnp.var(v, axis=1, keepdims=True)
        return (v - m) / jnp.sqrt(s + eps)

    def _ln_t(v, eps=1e-05):
        m = jnp.mean(v, axis=-1, keepdims=True)
        s = jnp.var(v, axis=-1, keepdims=True)
        return (v - m) / jnp.sqrt(s + eps)

    def _to_tokens(v):
        B_, C_, H_, W_ = v.shape
        return v.reshape(B_, C_, H_ * W_).transpose(0, 2, 1)

    def _from_tokens(t, like):
        B_, C_, H_, W_ = like.shape
        return t.transpose(0, 2, 1).reshape(B_, C_, H_, W_)
    x = _L0_conv_ref(x, L0_conv_theta_w, L0_conv_theta_b, L0_conv_phi_w, L0_conv_phi_b, L0_conv_g_w, L0_conv_g_b, L0_conv_w_w, L0_conv_w_b, L0_conv_gamma, L0_conv_beta)
    x = x + _L1_conv_ref(_gn(x), L1_conv_experts, L1_conv_w_r1, L1_conv_b_r1, L1_conv_w_r2, L1_conv_b_r2, L1_conv_w_f1, L1_conv_b_f1, L1_conv_w_f2, L1_conv_b_f2)
    t = _to_tokens(x)
    t = t + _L2_attn_ref(_ln_t(t), L2_attn_W_attn, L2_attn_W_proj)
    t = t + _L2_ffn_ref(_ln_t(t), L2_ffn_attention_mask, L2_ffn_wr, L2_ffn_br, L2_ffn_w1, L2_ffn_b1, L2_ffn_w2, L2_ffn_b2)
    t = t + _L3_attn_ref(_ln_t(t), L3_attn_Wcq, L3_attn_q_norm_w, L3_attn_Wq_nope, L3_attn_Wq_rope, L3_attn_Wckv, L3_attn_kv_norm_w, L3_attn_Wk_nope, L3_attn_Wv, L3_attn_Wk_rope, L3_attn_W_imp, L3_attn_Wsel_k, L3_attn_Wsel_v, L3_attn_Wwin_k, L3_attn_Wwin_v, L3_attn_Wgate, L3_attn_Wproj)
    t = t + _L3_ffn_ref(_ln_t(t), L3_ffn_gate_w, L3_ffn_gate_b, L3_ffn_w1, L3_ffn_b1, L3_ffn_w2, L3_ffn_b2)
    x = _from_tokens(t, x)
    return x

_drawn_inputs = setup_inputs


def setup_inputs(seed=0):
    import zlib

    import numpy as np

    out = dict(_drawn_inputs(seed))
    spreads = {'L1_conv_b_r1': (0.0, 0.8),
     'L1_conv_b_r2': (0.0, 0.1),
     'L1_conv_b_f1': (0.0, 0.8),
     'L2_ffn_b1': (0.0, 0.8),
     'L2_ffn_b2': (0.0, 0.8),
     'L3_attn_q_norm_w': (1.0, 0.6),
     'L3_attn_kv_norm_w': (1.0, 0.6),
     'L3_ffn_gate_b': (0.0, 0.363),
     'L3_ffn_b1': (0.0, 2.0),
     'L3_ffn_b2': (0.0, 2.0)}
    factors = {'L0_conv_theta_b': 2.806,
     'L0_conv_w_b': 64.0,
     'L1_conv_w_f1': 64.0,
     'L1_conv_w_f2': 8.0,
     'L2_ffn_wr': 8.0,
     'L2_ffn_w1': 8.0,
     'L2_ffn_w2': 8.0,
     'L3_attn_Wcq': 8.0,
     'L3_attn_Wq_nope': 8.0,
     'L3_attn_Wq_rope': 8.0,
     'L3_attn_Wckv': 8.0,
     'L3_attn_Wk_nope': 8.0,
     'L3_attn_Wv': 8.0,
     'L3_attn_Wk_rope': 64.0,
     'L3_attn_W_imp': 8.0,
     'L3_attn_Wsel_k': 8.0,
     'L3_attn_Wsel_v': 8.0,
     'L3_attn_Wwin_k': 8.0,
     'L3_attn_Wwin_v': 8.0,
     'L3_attn_Wgate': 8.0,
     'L3_attn_Wproj': 8.0,
     'L3_ffn_w1': 4.232,
     'L3_ffn_w2': 2.868}
    for name, (base, spread) in spreads.items():
        noise = np.random.default_rng([zlib.crc32(name.encode()), seed]).standard_normal(out[name].shape)
        drawn = base * np.exp(spread * noise) if base else spread * noise
        out[name] = jnp.asarray(drawn.astype(out[name].dtype))
    for name, factor in factors.items():
        out[name] = (out[name] * factor).astype(out[name].dtype)
    return out
```

```python
import numpy as np
import concourse.bass as bass
from concourse import mybir
from contextlib import ExitStack

F32 = mybir.dt.float32
F32R = mybir.dt.float32r
BF16 = mybir.dt.bfloat16
U32 = mybir.dt.uint32
ALU = mybir.AluOpType
ACT = mybir.ActivationFunctionType
AX = mybir.AxisListType

B, C, HW, N = 4, 128, 32, 1024
NT = N // 128
TT = B * NT
HALF = 512
CI = 64
E1 = 8
GH = 32
LOW = 16
PADW = HW + 2
TAPS = 9


class Semaphores:

    def __init__(self, nc):
        self.nc, self.stack, self.taken = nc, ExitStack(), []

    def enter_context(self, manager):
        self.taken.append(self.stack.enter_context(manager))
        return self.taken[-1]

    def release(self):
        numbers = sorted(sem.num for sem in self.taken)
        with self.nc.Block() as block:
            @block.gpsimd
            def _(pool):
                start = end = numbers[0]
                for n in numbers + [None]:
                    if n is not None and n <= end:
                        end = n + 1
                        continue
                    pool.sem_clear(range(start, end))
                    start, end = n, (n or 0) + 1
        self.stack.close()


class Chain:

    def __init__(self, eng, sem):
        self.eng, self.sem, self.n = eng, sem, 0

    def __call__(self, ins):
        self.n += 1
        ins.then_inc(self.sem, 1)
        self.eng.wait_ge(self.sem, self.n)


def stage_conv(nc, keep, P, T, ident, d):
    with ExitStack() as ctx:
        def sb(name, shape, dt=F32):
            return ctx.enter_context(nc.sbuf_tensor("c_" + name, shape, dt))

        def sem(name):
            return keep.enter_context(nc.semaphore(name))

        X = sb("X", [C, B * N])
        WY = sb("WY", [C, B * N])
        PG = sb("PG", [C, 2 * CI])
        PGb = sb("PGb", [128, 2 * CI])
        thw = sb("thw", [CI, C])
        thb = sb("thb", [CI, 1])
        wwT = sb("wwT", [CI, C])
        vec = sb("vec", [C, 3])
        PT = sb("PT", [128, NT, 2 * CI])
        KVT = sb("KVT", [CI, CI])
        M = sb("M", [CI, C])
        WE = sb("WE", [C, C])
        be = sb("be", [C, 1])
        st = sb("st", [C, B * 2, 6])
        mv = sb("mv", [C, 2])
        sc = sb("sc", [C, 4])
        gst = sb("gst", [C, B * 2, 6])
        gmv = sb("gmv", [C, B, 2])
        gq = sb("gq", [C, B])
        gg = sb("gg", [C, B, 2])
        gr = sb("gr", [C, B])
        blk4 = sb("blk4", [C, C])
        XP = sb("XP", [C, B, PADW, PADW])
        pr = sb("pr", [C, B, HW // 2, HW])
        pp = sb("pp", [C, B, 256])
        ppT = sb("ppT", [128, 2, B, C])
        dct = sb("dct", [128, 2, LOW])
        fq = sb("fq", [LOW, B * C])
        wf1 = sb("wf1", [LOW, GH])
        bf1 = sb("bf1", [GH, 1])
        h1 = sb("h1", [GH, B * C])
        wf2 = sb("wf2", [GH, 1])
        bf2 = sb("bf2", [C, 1])
        fs = sb("fs", [C, B])
        wr1 = sb("wr1", [C, GH])
        br1 = sb("br1", [GH, 1])
        rh = sb("rh", [GH, B])
        rhb = sb("rhb", [GH, B, C])
        wr2 = sb("wr2", [GH, E1])
        br2 = sb("br2", [C, E1])
        lg = sb("lg", [C, B, E1])
        lm = sb("lm", [C, B])
        EX = sb("EX", [C, E1, TAPS * C])
        KD = sb("KD", [C, 2, TAPS * C])

        ld_x, ld_w, ld_e, zeroed = sem("ld_x"), sem("ld_w"), sem("ld_e"), sem("zeroed")
        pg_ready, pg_biased = sem("pg_ready"), sem("pg_biased")
        kvt_ready, kvt_copied = sem("kvt_ready"), sem("kvt_copied")
        m_ready, m_copied = sem("m_ready"), sem("m_copied")
        we_ready, we_copied, be_ready = sem("we_ready"), sem("we_copied"), sem("be_ready")
        wy_ready, wy_copied = sem("wy_ready"), sem("wy_copied")
        var_ready, std_ready, bn_scale = sem("var_ready"), sem("std_ready"), sem("bn_scale")
        bn_done, dch = sem("bn_done"), sem("dch")
        gstat, ggrp, gvar, gstd = sem("gstat"), sem("ggrp"), sem("gvar"), sem("gstd")

        nld = 14
        with nc.Block() as block:
            @block.sync
            def _(sp):
                for b in range(B):
                    sp.dma_start(X[:, b * N:(b + 1) * N], d["x"][:, b * N:(b + 1) * N]).then_inc(ld_x, 16)
                sp.dma_start(EX[:, :, :].rearrange("p e n -> p (e n)"), d["experts"]).then_inc(ld_e, 16)

            @block.scalar
            def _(act):
                for dst, src in ((PG, d["pg_w"]), (PGb, d["pg_b"].broadcast_to([128, 2 * CI])), (thw, d["theta_w"]),
                                 (thb, d["theta_b"]), (wwT, d["w_wT"]), (vec, d["vec"]), (blk4, d["blk4"]),
                                 (wf1, d["w_f1"]), (bf1, d["b_f1"]), (wf2, d["w_f2"]),
                                 (bf2, d["b_f2"].broadcast_to([128, 1])), (wr1, d["w_r1"]), (br1, d["b_r1"]),
                                 (wr2, d["w_r2"])):
                    act.dma_start(dst[:, :], src).then_inc(ld_w, 16)
                for b in range(B):
                    act.wait_ge(we_ready, b + 1)
                    nc.scalar.activation(WE[:, :], P[4][:, 0:C], ACT.Copy).then_inc(we_copied, 1)
                    act.wait_ge(be_ready, b + 1)
                    for h in range(2):
                        act.wait_ge(wy_ready, 2 * b + h + 1)
                        nc.scalar.activation(WY[:, b * N + h * HALF:b * N + (h + 1) * HALF], P[6 + h][:, :],
                                             ACT.Identity, bias=be[:, 0:1]).then_inc(wy_copied, 1)
                act.wait_ge(var_ready, 1)
                nc.scalar.activation(sc[:, 1:2], sc[:, 0:1], ACT.Sqrt).then_inc(std_ready, 1)
                act.wait_ge(gvar, 1)
                nc.scalar.activation(gr[:, :], gq[:, :], ACT.Sqrt).then_inc(gstd, 1)

            @block.gpsimd
            def _(pool):
                nc.gpsimd.memset(XP[:, :, :, :], 0.0).then_inc(zeroed, 1)

            @block.tensor
            def _(pe):
                pe.wait_ge(ld_x, 16 * B)
                pe.wait_ge(ld_w, 16 * nld)
                for b in range(B):
                    for h in range(2):
                        for t in range(4):
                            k = b * N + (4 * h + t) * 128
                            last = nc.tensor.matmul(P[h][:, t * 128:(t + 1) * 128], X[:, k:k + 128], PG[:, :],
                                                    start=True, stop=True)
                        last.then_inc(pg_ready, 1)
                    pe.wait_ge(pg_biased, 2 * b + 2)
                    for t in range(NT):
                        last = nc.tensor.matmul(P[2][0:CI, 0:CI], PT[:, t, CI:], PT[:, t, 0:CI],
                                                start=(t == 0), stop=(t == NT - 1))
                    last.then_inc(kvt_ready, 1)
                    pe.wait_ge(kvt_copied, b + 1)
                    nc.tensor.matmul(P[3][0:CI, 0:C], KVT[:, :], wwT[:, :], start=True, stop=True).then_inc(m_ready, 1)
                    pe.wait_ge(m_copied, b + 1)
                    nc.tensor.matmul(P[5][:, 0:1], M[:, :], thb[:, :], start=True, stop=True)
                    nc.tensor.matmul(P[4][:, 0:C], thw[:, :], M[:, :], start=True, stop=True).then_inc(we_ready, 1)
                    pe.wait_ge(we_copied, b + 1)
                    for h in range(2):
                        k = b * N + h * HALF
                        nc.tensor.matmul(P[6 + h][:, :], WE[:, :], X[:, k:k + HALF],
                                         start=True, stop=True).then_inc(wy_ready, 1)
                    pe.wait_ge(wy_copied, 2 * b + 2)
                pe.wait_ge(gstat, 1)
                nc.tensor.matmul(P[2][:, 0:2 * B], blk4[:, :], gg[:, :, :].rearrange("p b s -> p (b s)"),
                                 start=True, stop=True).then_inc(ggrp, 1)

            @block.vector
            def _(dve):
                link = Chain(dve, dch)
                dve.wait_ge(ld_w, 16 * nld)
                for b in range(B):
                    for h in range(2):
                        dve.wait_ge(pg_ready, 2 * b + h + 1)
                        nc.vector.tensor_tensor(PT[:, 4 * h:4 * h + 4, :],
                                                P[h][:, :].rearrange("p (t n) -> p t n", t=4),
                                                PGb[:, None, :].broadcast_to([128, 4, 2 * CI]), ALU.add)\
                            .then_inc(pg_biased, 1)
                    dve.wait_ge(kvt_ready, b + 1)
                    nc.vector.tensor_copy(KVT[:, :], P[2][0:CI, 0:CI]).then_inc(kvt_copied, 1)
                    dve.wait_ge(m_ready, b + 1)
                    nc.vector.tensor_scalar(M[:, :], P[3][0:CI, 0:C], 1.0 / N, None, ALU.mult).then_inc(m_copied, 1)
                    dve.wait_ge(we_ready, b + 1)
                    nc.vector.tensor_tensor(be[:, :], P[5][:, 0:1], vec[:, 0:1], ALU.add).then_inc(be_ready, 1)
                    for h in range(2):
                        k = b * N + h * HALF
                        dve.wait_ge(wy_copied, 2 * b + h + 1)
                        ins = nc.vector.bn_stats(st[:, 2 * b + h, :], WY[:, k:k + HALF])
                link(ins)
                link(nc.vector.bn_aggr(mv[:, :], st[:, :, :].rearrange("p a s -> p (a s)")))
                nc.vector.tensor_scalar(sc[:, 0:1], mv[:, 1:2], 1e-5, None, ALU.add).then_inc(var_ready, 1)
                dve.wait_ge(std_ready, 1)
                link(nc.vector.reciprocal(sc[:, 2:3], sc[:, 1:2]))
                link(nc.vector.tensor_tensor(sc[:, 0:1], sc[:, 2:3], vec[:, 1:2], ALU.mult))
                link(nc.vector.tensor_tensor(sc[:, 1:2], mv[:, 0:1], sc[:, 0:1], ALU.mult))
                link(nc.vector.tensor_tensor(sc[:, 3:4], vec[:, 2:3], sc[:, 1:2], ALU.subtract))
                for k in range(0, B * N, N):
                    nc.vector.tensor_scalar(WY[:, k:k + N], WY[:, k:k + N], sc[:, 0:1], sc[:, 3:4],
                                            ALU.mult, ALU.add).then_inc(bn_done, 1)
                for i, k in enumerate(range(0, B * N, N)):
                    dve.wait_ge(bn_done, i + 1)
                    nc.vector.tensor_tensor(X[:, k:k + N], X[:, k:k + N], WY[:, k:k + N], ALU.add).then_inc(bn_done, 1)
                dve.wait_ge(bn_done, 2 * B)
                for j in range(2 * B):
                    ins = nc.vector.bn_stats(gst[:, j, :], X[:, j * HALF:(j + 1) * HALF])
                link(ins)
                for b in range(B):
                    ins = nc.vector.bn_aggr(gmv[:, b, :], gst[:, 2 * b:2 * b + 2, :].rearrange("p a s -> p (a s)"))
                link(ins)
                link(nc.vector.tensor_tensor(gq[:, :], gmv[:, :, 0], gmv[:, :, 0], ALU.mult))
                link(nc.vector.tensor_copy(gg[:, :, 0], gmv[:, :, 0]))
                nc.vector.tensor_tensor(gg[:, :, 1], gmv[:, :, 1], gq[:, :], ALU.add).then_inc(gstat, 1)
                dve.wait_ge(ggrp, 1)
                link(nc.vector.tensor_copy(gg[:, :, :].rearrange("p b s -> p (b s)"), P[2][:, 0:2 * B]))
                link(nc.vector.tensor_tensor(gr[:, :], gg[:, :, 0], gg[:, :, 0], ALU.mult))
                link(nc.vector.tensor_tensor(gq[:, :], gg[:, :, 1], gr[:, :], ALU.subtract))
                link(nc.vector.tensor_scalar(gq[:, :], gq[:, :], 1e-5, None, ALU.add))
                nc.vector.tensor_copy(gmv[:, :, 0], gg[:, :, 0]).then_inc(gvar, 1)
                dve.wait_ge(gstd, 1)
                link(nc.vector.reciprocal(gq[:, :], gr[:, :]))
                dve.wait_ge(zeroed, 1)
                for b in range(B):
                    ins = nc.vector.tensor_scalar(XP[:, b, 1:1 + HW, 1:1 + HW],
                                                  X[:, b * N:(b + 1) * N].rearrange("p (h w) -> p h w", h=HW),
                                                  gmv[:, b, 0:1], gq[:, b:b + 1], ALU.subtract, ALU.mult)
                link(ins)

        pooled, pT_ready, pT_copied = sem("pooled"), sem("pT_ready"), sem("pT_copied")
        fq_ready, fq_copied, h1_ready, h1_done = sem("fq_ready"), sem("fq_copied"), sem("h1_ready"), sem("h1_done")
        f_ready, f_done, rh_ready, rh_done = sem("f_ready"), sem("f_done"), sem("rh_ready"), sem("rh_done")
        rhb_done, lg_ready, lsub, lexp = sem("rhb_done"), sem("lg_ready"), sem("lsub"), sem("lexp")
        mixed, conv_ready, conv_added, dch2 = sem("mixed"), sem("conv_ready"), sem("conv_added"), sem("dch2")
        t_ready, t_copied, ld_r = sem("t_ready"), sem("t_copied"), sem("ld_r")

        with nc.Block() as block:
            @block.sync
            def _(sp):
                sp.dma_start(dct[:, :, :], d["dct"]).then_inc(ld_r, 16)
                sp.dma_start(br2[:, :], d["b_r2"].broadcast_to([128, E1])).then_inc(ld_r, 16)

            @block.tensor
            def _(pe):
                for b in range(B):
                    pe.wait_ge(pooled, b + 1)
                    for j in range(2):
                        last = nc.tensor.transpose(P[j][:, b * 128:(b + 1) * 128], pp[:, b, j * 128:(j + 1) * 128],
                                                   ident[:, :])
                last.then_inc(pT_ready, 1)
                pe.wait_ge(pT_copied, 2)
                pe.wait_ge(ld_r, 32)
                for j in range(2):
                    last = nc.tensor.matmul(P[2][0:LOW, :], dct[:, j, :], ppT[:, j, :, :].rearrange("p b c -> p (b c)"),
                                            start=(j == 0), stop=(j == 1))
                last.then_inc(fq_ready, 1)
                pe.wait_ge(fq_copied, 1)
                nc.tensor.matmul(P[3][0:GH, :], wf1[:, :], fq[:, :], start=True, stop=True).then_inc(h1_ready, 1)
                pe.wait_ge(h1_done, 1)
                for b in range(B):
                    last = nc.tensor.matmul(P[4][:, b:b + 1], h1[:, b * C:(b + 1) * C], wf2[:, :], start=True, stop=True)
                last.then_inc(f_ready, 1)
                pe.wait_ge(f_done, 1)
                nc.tensor.matmul(P[5][0:GH, 0:B], wr1[:, :], fs[:, :], start=True, stop=True).then_inc(rh_ready, 1)
                pe.wait_ge(rhb_done, 1)
                for b in range(B):
                    last = nc.tensor.matmul(P[6][:, b * E1:(b + 1) * E1], rhb[:, b, :], wr2[:, :], start=True, stop=True)
                last.then_inc(lg_ready, 1)
                for b in range(B):
                    pe.wait_ge(mixed, b + 1)
                    for h in range(2):
                        if b > 0:
                            pe.wait_ge(conv_added, 2 * (b - 1) + h + 1)
                        for tap in range(TAPS):
                            dy, dx = divmod(tap, 3)
                            last = nc.tensor.matmul(P[h][:, :], KD[:, b % 2, tap * C:(tap + 1) * C],
                                                    XP[:, b, 16 * h + dy:16 * h + dy + 16, dx:dx + HW],
                                                    start=(tap == 0), stop=(tap == TAPS - 1))
                        last.then_inc(conv_ready, 1)
                for u in range(2 * B):
                    pe.wait_ge(conv_added, u + 1)
                    if u >= 2:
                        pe.wait_ge(t_copied, u - 1)
                    for t in range(4):
                        k = (4 * u + t) * 128
                        last = nc.tensor.transpose(P[2 + u % 2][:, t * 128:(t + 1) * 128], X[:, k:k + 128], ident[:, :])
                    last.then_inc(t_ready, 1)

            @block.scalar
            def _(act):
                act.wait_ge(pT_ready, 1)
                for j in range(2):
                    nc.scalar.activation(ppT[:, j, :, :].rearrange("p b c -> p (b c)"), P[j][:, :], ACT.Copy)\
                        .then_inc(pT_copied, 1)
                act.wait_ge(fq_ready, 1)
                nc.scalar.activation(fq[:, :], P[2][0:LOW, :], ACT.Copy).then_inc(fq_copied, 1)
                act.wait_ge(h1_ready, 1)
                nc.scalar.activation(h1[:, :], P[3][0:GH, :], ACT.Relu, bias=bf1[:, 0:1]).then_inc(h1_done, 1)
                act.wait_ge(f_ready, 1)
                nc.scalar.activation(fs[:, :], P[4][:, 0:B], ACT.Sigmoid, bias=bf2[:, 0:1]).then_inc(f_done, 1)
                act.wait_ge(rh_ready, 1)
                nc.scalar.activation(rh[:, :], P[5][0:GH, 0:B], ACT.Relu, bias=br1[:, 0:1]).then_inc(rh_done, 1)
                act.wait_ge(lsub, 1)
                nc.scalar.activation(lg[:, :, :], lg[:, :, :], ACT.Exp).then_inc(lexp, 1)
                for u in range(2 * B):
                    act.wait_ge(t_ready, u + 1)
                    nc.scalar.activation(T[:, 4 * u:4 * u + 4, :], P[2 + u % 2][:, :].rearrange("p (t c) -> p t c", t=4),
                                         ACT.Copy).then_inc(t_copied, 1)

            def add_conv(nc, dve, b):
                for h in range(2):
                    k = b * N + h * HALF
                    dve.wait_ge(conv_ready, 2 * b + h + 1)
                    nc.vector.tensor_tensor(X[:, k:k + HALF], X[:, k:k + HALF], P[h][:, :], ALU.add)\
                        .then_inc(conv_added, 1)

            @block.vector
            def _(dve):
                link = Chain(dve, dch2)
                for b in range(B):
                    link(nc.vector.tensor_tensor(pr[:, b, :, :], XP[:, b, 1:1 + HW:2, 1:1 + HW],
                                                 XP[:, b, 2:2 + HW:2, 1:1 + HW], ALU.add))
                    nc.vector.tensor_tensor(pp[:, b, :].rearrange("p (h w) -> p h w", h=16), pr[:, b, :, 0::2],
                                            pr[:, b, :, 1::2], ALU.add).then_inc(pooled, 1)
                dve.wait_ge(rh_done, 1)
                nc.vector.tensor_copy(rhb[:, :, :], rh[:, :, None].broadcast_to([GH, B, C])).then_inc(rhb_done, 1)
                dve.wait_ge(lg_ready, 1)
                dve.wait_ge(ld_r, 32)
                link(nc.vector.tensor_tensor(lg[:, :, :], P[6][:, 0:B * E1].rearrange("p (b e) -> p b e", b=B),
                                             br2[:, None, :].broadcast_to([C, B, E1]), ALU.add))
                link(nc.vector.tensor_reduce(lm[:, :], lg[:, :, :], AX.X, ALU.max))
                nc.vector.tensor_tensor(lg[:, :, :], lg[:, :, :], lm[:, :, None].broadcast_to([C, B, E1]),
                                        ALU.subtract).then_inc(lsub, 1)
                dve.wait_ge(lexp, 1)
                link(nc.vector.tensor_reduce(lm[:, :], lg[:, :, :], AX.X, ALU.add))
                link(nc.vector.reciprocal(lm[:, :], lm[:, :]))
                link(nc.vector.tensor_tensor(lg[:, :, :], lg[:, :, :], lm[:, :, None].broadcast_to([C, B, E1]), ALU.mult))
                dve.wait_ge(ld_e, 16)
                for b in range(B):
                    if b >= 2:
                        dve.wait_ge(conv_ready, 2 * (b - 1))
                    link(nc.vector.tensor_scalar(KD[:, b % 2, :], EX[:, 0, :], lg[:, b, 0:1], None, ALU.mult))
                    for e in range(1, E1):
                        ins = nc.vector.scalar_tensor_tensor(out=KD[:, b % 2, :], in0=EX[:, e, :], scalar=lg[:, b, e:e + 1],
                                                             in1=KD[:, b % 2, :], op0=ALU.mult, op1=ALU.add)
                        if e < E1 - 1:
                            link(ins)
                    ins.then_inc(mixed, 1)
                    if b >= 1:
                        add_conv(nc, dve, b - 1)
                add_conv(nc, dve, B - 1)


def norm_vector(nc, dve, s, b, T, XN, ln):
    for t in range(NT):
        ins = nc.vector.bn_stats(ln["st"][:, t, :], T[:, bass.ds(b * NT + t, 1), :].rearrange("p a c -> p (a c)"))
    ins.then_inc(s["ln_stat"], 1)
    st, va, tmp = ln["st"], ln["va"], ln["tmp"]
    dve.wait_ge(s["ln_stat"], b * 3 + 1)
    nc.vector.tensor_tensor(tmp[:, 0, :], st[:, :, 1], st[:, :, 4], ALU.add)
    nc.vector.tensor_tensor(tmp[:, 1, :], st[:, :, 1], st[:, :, 4], ALU.subtract)
    nc.vector.tensor_tensor(tmp[:, 2, :], st[:, :, 2], st[:, :, 5], ALU.add).then_inc(s["ln_stat"], 1)
    dve.wait_ge(s["ln_stat"], b * 3 + 2)
    nc.vector.tensor_scalar(ln["mv"][:, :], tmp[:, 0, :], 0.5, None, ALU.mult)
    nc.vector.scalar_tensor_tensor(out=tmp[:, 3, :], in0=tmp[:, 1, :], scalar=0.25, in1=tmp[:, 1, :],
                                   op0=ALU.mult, op1=ALU.mult)
    nc.vector.tensor_scalar(va[:, :], tmp[:, 2, :], 1.0 / C, 1e-5, ALU.mult, ALU.add).then_inc(s["ln_stat"], 1)
    dve.wait_ge(s["ln_stat"], b * 3 + 3)
    nc.vector.tensor_tensor(va[:, :], va[:, :], tmp[:, 3, :], ALU.add).then_inc(s["ln_var"], 1)
    dve.wait_ge(s["ln_std"], b + 1)
    nc.vector.reciprocal(ln["rs"][:, :], ln["sd"][:, :]).then_inc(s["ln_rs"], 1)
    dve.wait_ge(s["ln_rs"], b + 1)
    for t in range(NT):
        ins = nc.vector.tensor_scalar(XN[:, t, :], T[:, bass.ds(b * NT + t, 1), :].rearrange("p a c -> p (a c)"),
                                      ln["mv"][:, t:t + 1], ln["rs"][:, t:t + 1], ALU.subtract, ALU.mult)
        if t % 4 == 3:
            ins.then_inc(s["ln_done"], 1)


def norm_scalar(nc, act, s, b, P, XC, ln):
    act.wait_ge(s["ln_var"], b + 1)
    nc.scalar.activation(ln["sd"][:, :], ln["va"][:, :], ACT.Sqrt).then_inc(s["ln_std"], 1)
    for h in range(2):
        act.wait_ge(s["xt_ready"], b * 2 + h + 1)
        nc.scalar.activation(XC[:, h * HALF:(h + 1) * HALF], P[h], ACT.Copy).then_inc(s["xc_ready"], 1)


def norm_tensor(nc, pe, s, b, P, XN, ident):
    for h in range(2):
        pe.wait_ge(s["ln_done"], b * 2 + h + 1)
        for t in range(4):
            last = nc.tensor.transpose(P[h][:, t * 128:(t + 1) * 128], XN[:, 4 * h + t, :], ident[:, :])
        last.then_inc(s["xt_ready"], 1)


def norm_tiles(sb):
    return {"st": sb("ln_st", [128, NT, 6]), "mv": sb("ln_mv", [128, NT]), "tmp": sb("ln_tmp", [128, 4, NT]), "va": sb("ln_va", [128, NT]),
            "sd": sb("ln_sd", [128, NT]), "rs": sb("ln_rs_t", [128, NT])}


NORM_SEMS = ("ln_stat", "ln_var", "ln_std", "ln_rs", "ln_done", "xt_ready", "xc_ready")


H2 = 4
D2 = C // H2
UNITS = NT * H2


def stage_attn2(nc, keep, PS, P, T, ident, identb, cmask, lohi, d):
    with ExitStack() as ctx:
        def sb(name, shape, dt=F32):
            return ctx.enter_context(nc.sbuf_tensor("a2_" + name, shape, dt))

        ln = norm_tiles(sb)
        XN = sb("XN", [128, NT, C])
        XC = sb("XC", [C, N])
        WA = sb("WA", [C, 3 * C])
        WR = sb("WR", [C, 2, H2, 4, D2])
        WP = sb("WP", [C, C])
        R = sb("R", [128, 2, HALF], F32R)
        QS = sb("QS", [128, H2, N], F32R)
        KS = sb("KS", [128, H2, N], F32R)
        V = sb("V", [128, NT, C])
        NM = sb("NM", [128, 2])
        L = sb("L", [128, 2])
        RL = sb("RL", [128, 2])
        PR = sb("PR", [128, 2, N])
        PT = sb("PT", [128, 2, H2, N])
        YT = sb("YT", [C, N])
        names = NORM_SEMS + ("ld", "wr_ready", "qk_ready", "qk_round", "qk_split", "v_ready", "v_copied",
                             "score_ready", "max_ready", "exp_done", "rl_ready", "prob_ready", "pt_ready", "pt_copied",
                             "pv_ready", "yt_copied", "proj_ready", "added")
        s = {n: keep.enter_context(nc.semaphore("a2_" + n)) for n in names}
        jobs = [(w, h, half) for w in range(2) for h in range(H2) for half in range(2)]
        units = [(i, h) for i in range(NT) for h in range(H2)]
        width = lambda i: (i + 1) * 128
        banks = []
        first_bank = []
        for n, (i, h) in enumerate(units):
            first_bank.append(len(banks))
            banks += [(n, j, min(4, i + 1 - j)) for j in range(0, i + 1, 4)]
        first_bank.append(len(banks))
        NB = len(banks)
        slot = lambda n: PS[:, 2 * (n % 2):2 * (n % 2) + 2, :].rearrange("p a n -> p (a n)")

        with nc.Block() as block:
            @block.sync
            def _(sp):
                sp.dma_start(WA[:, :], d["W_attn"]).then_inc(s["ld"], 16)
                sp.dma_start(WP[:, :], d["W_proj2"]).then_inc(s["ld"], 16)

            @block.tensor
            def _(pe):
                def scores(b, n):
                    i, h = units[n]
                    if n >= 2:
                        pe.wait_ge(s["exp_done"], b * UNITS + n - 1)
                    S = slot(n)
                    w = width(i)
                    for c0 in range(0, w, HALF):
                        c1 = min(w, c0 + HALF)
                        diag = c1 == w
                        last = nc.tensor.matmul(S[:, c0:c1], QS[:, h, i * 128:(i + 1) * 128], KS[:, h, c0:c1],
                                                start=True, stop=not diag)
                    last = nc.tensor.matmul(S[:, w - 128:w], identb[:, :], cmask[:, :], start=False, stop=True)
                    last.then_inc(s["score_ready"], 1)

                def transposes(b, n):
                    i, h = units[n]
                    pe.wait_ge(s["prob_ready"], b * UNITS + n + 1)
                    for k in range(first_bank[n], first_bank[n + 1]):
                        if k >= 2:
                            pe.wait_ge(s["pt_copied"], b * NB + k - 1)
                        _, j0, m = banks[k]
                        for j in range(m):
                            last = nc.tensor.transpose(P[4 + k % 2][:, j * 128:(j + 1) * 128],
                                                       PR[:, n % 2, (j0 + j) * 128:(j0 + j + 1) * 128], ident[:, :])
                        last.then_inc(s["pt_ready"], 1)

                def values(b, i):
                    pe.wait_ge(s["pt_copied"], b * NB + first_bank[H2 * (i + 1)])
                    if i >= 2:
                        pe.wait_ge(s["added"], b * NT + i - 1)
                    for j in range(i + 1):
                        for h in range(H2):
                            last = nc.tensor.matmul(P[6 + i % 2][h * D2:(h + 1) * D2, 0:128],
                                                    V[:, j, h * D2:(h + 1) * D2], PT[:, i % 2, h, j * 128:(j + 1) * 128],
                                                    start=(j == 0), stop=(j == i))
                    last.then_inc(s["pv_ready"], 1)

                def project(b, i):
                    pe.wait_ge(s["yt_copied"], b * NT + i + 1)
                    nc.tensor.matmul(P[6 + i % 2][:, 128:256], YT[:, i * 128:(i + 1) * 128], WP[:, :],
                                     start=True, stop=True).then_inc(s["proj_ready"], 1)

                pe.wait_ge(s["wr_ready"], 1)
                with pe.Fori(0, B) as b:
                    norm_tensor(nc, pe, s, b, P, XN, ident)
                    pe.wait_ge(s["xc_ready"], b * 2 + 2)
                    for k, (w, h, half) in enumerate(jobs):
                        if k >= 2:
                            pe.wait_ge(s["qk_split"], b * 16 + k - 1)
                        nc.tensor.matmul(P[2 + k % 2], WR[:, w, h, :, :].rearrange("p r c -> p (r c)"),
                                         XC[:, half * HALF:(half + 1) * HALF], start=True, stop=True)\
                            .then_inc(s["qk_ready"], 1)
                    for half in range(2):
                        for t in range(4):
                            k = (4 * half + t) * 128
                            last = nc.tensor.matmul(P[4 + half][:, t * 128:(t + 1) * 128], XC[:, k:k + 128],
                                                    WA[:, 2 * C:], start=True, stop=True)
                        last.then_inc(s["v_ready"], 1)
                    pe.wait_ge(s["qk_split"], b * 16 + 16)
                    pe.wait_ge(s["v_copied"], b * 2 + 2)
                    scores(b, 0)
                    for n, (i, h) in enumerate(units):
                        if n + 1 < UNITS:
                            scores(b, n + 1)
                        if h == 3 and i > 0:
                            project(b, i - 1)
                        if n >= 1:
                            transposes(b, n - 1)
                        if h == 1 and i > 0:
                            values(b, i - 1)
                    transposes(b, UNITS - 1)
                    values(b, NT - 1)
                    project(b, NT - 1)

            @block.scalar
            def _(act):
                def copy_banks(b, n):
                    i, h = units[n]
                    if h == 0 and i >= 2:
                        act.wait_ge(s["pv_ready"], b * NT + i - 1)
                    for k in range(first_bank[n], first_bank[n + 1]):
                        _, j0, m = banks[k]
                        act.wait_ge(s["pt_ready"], b * NB + k + 1)
                        nc.scalar.activation(PT[:, i % 2, h, j0 * 128:(j0 + m) * 128], P[4 + k % 2][:, 0:m * 128],
                                             ACT.Copy).then_inc(s["pt_copied"], 1)

                with act.Fori(0, B) as b:
                    norm_scalar(nc, act, s, b, P, XC, ln)
                    for k, (w, h, half) in enumerate(jobs):
                        act.wait_ge(s["qk_ready"], b * 16 + k + 1)
                        if k >= 2:
                            act.wait_ge(s["qk_split"], b * 16 + k - 1)
                        nc.scalar.activation(R[:, k % 2, :], P[2 + k % 2], ACT.Copy).then_inc(s["qk_round"], 1)
                    for half in range(2):
                        act.wait_ge(s["v_ready"], b * 2 + half + 1)
                        nc.scalar.activation(V[:, 4 * half:4 * half + 4, :], P[4 + half].rearrange("p (t c) -> p t c", t=4),
                                             ACT.Copy).then_inc(s["v_copied"], 1)
                    for n, (i, h) in enumerate(units):
                        act.wait_ge(s["max_ready"], b * UNITS + n + 1)
                        if n >= 2:
                            act.wait_ge(s["pt_ready"], b * NB + first_bank[n - 1])
                        nc.scalar.activation(PR[:, n % 2, 0:width(i)], slot(n)[:, 0:width(i)], ACT.Exp,
                                             bias=NM[:, n % 2:n % 2 + 1], accum_out=L[:, n % 2:n % 2 + 1])\
                            .then_inc(s["exp_done"], 1)
                        if n >= 1:
                            copy_banks(b, n - 1)
                    copy_banks(b, UNITS - 1)

            @block.vector
            def _(dve):
                def row_max(b, n):
                    dve.wait_ge(s["score_ready"], b * UNITS + n + 1)
                    if n >= 2:
                        dve.wait_ge(s["exp_done"], b * UNITS + n - 1)
                    nc.vector.tensor_reduce(NM[:, n % 2:n % 2 + 1], slot(n)[:, 0:width(units[n][0])], AX.X, ALU.max,
                                            negate=True).then_inc(s["max_ready"], 1)

                def normalise(b, n):
                    i, h = units[n]
                    dve.wait_ge(s["exp_done"], b * UNITS + n + 1)
                    nc.vector.reciprocal(RL[:, n % 2:n % 2 + 1], L[:, n % 2:n % 2 + 1]).then_inc(s["rl_ready"], 1)
                    dve.wait_ge(s["rl_ready"], b * UNITS + n + 1)
                    nc.vector.tensor_scalar(PR[:, n % 2, 0:width(i)], PR[:, n % 2, 0:width(i)], RL[:, n % 2:n % 2 + 1],
                                            None, ALU.mult).then_inc(s["prob_ready"], 1)

                def head_out(b, i):
                    dve.wait_ge(s["pv_ready"], b * NT + i + 1)
                    nc.vector.tensor_copy(YT[:, i * 128:(i + 1) * 128], P[6 + i % 2][:, 0:128]).then_inc(s["yt_copied"], 1)

                def residual(b, i):
                    dve.wait_ge(s["proj_ready"], b * NT + i + 1)
                    t = T[:, bass.ds(b * NT + i, 1), :].rearrange("p a c -> p (a c)")
                    nc.vector.tensor_tensor(t, t, P[6 + i % 2][:, 128:256], ALU.add).then_inc(s["added"], 1)

                dve.wait_ge(s["ld"], 32)
                for w in range(2):
                    for r in range(4):
                        ins = nc.vector.tensor_scalar(WR[:, w, :, r, :],
                                                      WA[:, w * C:(w + 1) * C].rearrange("p (h c) -> p h c", h=H2),
                                                      1.0 if w else float(1.0 / np.sqrt(np.float32(D2))), None, ALU.mult)
                ins.then_inc(s["wr_ready"], 1)
                with dve.Fori(0, B) as b:
                    norm_vector(nc, dve, s, b, T, XN, ln)
                    for k, (w, h, half) in enumerate(jobs):
                        dve.wait_ge(s["qk_round"], b * 16 + k + 1)
                        nc.vector.scalar_tensor_tensor(out=(QS, KS)[w][:, h, half * HALF:(half + 1) * HALF],
                                                       in0=R[:, k % 2, :].bitcast(F32), scalar=lohi[:, w:w + 1],
                                                       in1=P[2 + k % 2], op0=ALU.mult, op1=ALU.add)\
                            .then_inc(s["qk_split"], 1)
                    row_max(b, 0)
                    for n, (i, h) in enumerate(units):
                        if n + 1 < UNITS:
                            row_max(b, n + 1)
                        if h == 2 and i > 0:
                            head_out(b, i - 1)
                        normalise(b, n)
                        if h == 3 and i > 0:
                            residual(b, i - 1)
                    head_out(b, NT - 1)
                    residual(b, NT - 1)
                    dve.wait_ge(s["added"], b * NT + NT)


F = 4 * C
KEEP2 = N // 2 - 1


def rank_tiles(sb):
    return {"row": sb("rk_row", [128, N]), "ex": sb("rk_ex", [128, NT, 128]), "col": sb("rk_col", [128, NT]),
            "cnt": sb("rk_cnt", [128, 3, NT]), "junk": sb("rk_junk", [128, NT, N + 128], BF16), "rank": sb("rk_rank", [128, NT])}


def rank_vector(nc, dve, s, b, rk, ident, below, steps):
    row, col, cnt, junk = rk["row"], rk["col"], rk["cnt"], rk["junk"]
    nc.vector.tensor_tensor(rk["ex"][:, :, :], row[:, :].rearrange("p (t c) -> p t c", t=NT),
                            ident[:, None, :].broadcast_to([128, NT, 128]), ALU.mult).then_inc(s["rk"], 1)
    dve.wait_ge(s["rk"], b * steps + 1)
    nc.vector.tensor_reduce(col[:, :], rk["ex"][:, :, :], AX.X, ALU.add).then_inc(s["rk"], 1)
    dve.wait_ge(s["rk"], b * steps + 2)
    for t in range(NT):
        c = col[:, t:t + 1]
        if t:
            nc.vector.tensor_scalar(junk[:, t, 0:128 * t], row[:, 0:128 * t], c, 0.0, ALU.is_ge, ALU.add,
                                    accum_out=cnt[:, 0, t:t + 1])
        nc.vector.tensor_scalar(junk[:, t, 128 * t:N], row[:, 128 * t:N], c, 0.0, ALU.is_gt, ALU.add,
                                accum_out=cnt[:, 1, t:t + 1])
        ins = nc.vector.scalar_tensor_tensor(out=junk[:, t, N:], in0=row[:, 128 * t:128 * t + 128], scalar=c,
                                             in1=below[:, :], op0=ALU.is_equal, op1=ALU.mult,
                                             accum_out=cnt[:, 2, t:t + 1])
    ins.then_inc(s["rk"], 1)
    dve.wait_ge(s["rk"], b * steps + 3)
    nc.vector.tensor_tensor(rk["rank"][:, :], cnt[:, 0, :], cnt[:, 1, :], ALU.add).then_inc(s["rk"], 1)
    dve.wait_ge(s["rk"], b * steps + 4)
    nc.vector.tensor_tensor(rk["rank"][:, :], rk["rank"][:, :], cnt[:, 2, :], ALU.add).then_inc(s["rk"], 1)
    dve.wait_ge(s["rk"], b * steps + 5)


def stage_ffn2(nc, keep, PS, P, T, ident, below, d):
    with ExitStack() as ctx:
        def sb(name, shape, dt=F32):
            return ctx.enter_context(nc.sbuf_tensor("f2_" + name, shape, dt))

        ln, rk = norm_tiles(sb), rank_tiles(sb)
        XN = sb("XN", [128, NT, C])
        XC = sb("XC", [C, N])
        wr = sb("wr", [C, 1])
        wrr = sb("wrr", [C, 128])
        br = sb("br", [128, 1])
        w1 = sb("w1", [C, F])
        b1 = sb("b1", [128, 4])
        w2 = sb("w2", [128, 4, C])
        b2 = sb("b2", [128, C])
        H = sb("H", [128, 4, N])
        Y = sb("Y", [128, NT, C])
        gate = sb("gate", [128, NT])
        names = NORM_SEMS + ("ld", "wrr_ready", "row_ready", "row_copied", "rk", "gated", "h_ready", "h_done",
                             "y_ready", "y_scaled", "t_plus_x", "t_done")
        s = {n: keep.enter_context(nc.semaphore("f2_" + n)) for n in names}
        jobs = [(m, half) for half in range(2) for m in range(4)]
        with nc.Block() as block:
            @block.sync
            def _(sp):
                for dst, src in ((wr[:, :], d["wr"]), (br[:, :], d["br"].broadcast_to([128, 1])), (w1[:, :], d["w1"]),
                                 (b1[:, :], d["b1"]), (w2[:, :, :], d["w2"]), (b2[:, :], d["b2"].broadcast_to([128, C]))):
                    sp.dma_start(dst, src).then_inc(s["ld"], 16)

            @block.tensor
            def _(pe):
                pe.wait_ge(s["ld"], 96)
                pe.wait_ge(s["wrr_ready"], 1)
                with pe.Fori(0, B) as b:
                    norm_tensor(nc, pe, s, b, P, XN, ident)
                    pe.wait_ge(s["xc_ready"], b * 2 + 2)
                    for h in range(2):
                        nc.tensor.matmul(P[2 + h], wrr[:, :], XC[:, h * HALF:(h + 1) * HALF], start=True, stop=True)\
                            .then_inc(s["row_ready"], 1)
                    for k, (m, half) in enumerate(jobs):
                        if k >= 2:
                            pe.wait_ge(s["h_done"], b * 8 + k - 1)
                        nc.tensor.matmul(P[4 + k % 2], w1[:, m * 128:(m + 1) * 128], XC[:, half * HALF:(half + 1) * HALF],
                                         start=True, stop=True).then_inc(s["h_ready"], 1)
                    for g in range(2):
                        pe.wait_ge(s["h_done"], b * 8 + 4 * g + 4)
                        for t in range(4):
                            for m in range(4):
                                k = (4 * g + t) * 128
                                last = nc.tensor.matmul(P[6 + g][:, t * 128:(t + 1) * 128], H[:, m, k:k + 128],
                                                        w2[:, m, :], start=(m == 0), stop=(m == 3))
                        last.then_inc(s["y_ready"], 1)

            @block.scalar
            def _(act):
                with act.Fori(0, B) as b:
                    norm_scalar(nc, act, s, b, P, XC, ln)
                    for h in range(2):
                        act.wait_ge(s["row_ready"], b * 2 + h + 1)
                        nc.scalar.activation(rk["row"][:, h * HALF:(h + 1) * HALF], P[2 + h], ACT.Identity,
                                             bias=br[:, 0:1]).then_inc(s["row_copied"], 1)
                    for k, (m, half) in enumerate(jobs):
                        act.wait_ge(s["h_ready"], b * 8 + k + 1)
                        nc.scalar.activation(H[:, m, half * HALF:(half + 1) * HALF], P[4 + k % 2], ACT.Gelu_apprx_tanh,
                                             bias=b1[:, m:m + 1]).then_inc(s["h_done"], 1)

            @block.gpsimd
            def _(pool):
                with pool.Fori(0, B) as b:
                    for g in range(2):
                        pool.wait_ge(s["ln_done"], b * 2 + g + 1)
                        t = T[:, bass.ds(b * NT + 4 * g, 4), :]
                        nc.gpsimd.tensor_tensor(t, t, XN[:, 4 * g:4 * g + 4, :], ALU.add).then_inc(s["t_plus_x"], 1)

            @block.vector
            def _(dve):
                dve.wait_ge(s["ld"], 96)
                nc.vector.memset(rk["cnt"][:, 0, 0:1], 0.0)
                nc.vector.tensor_copy(wrr[:, :], wr[:, 0:1].broadcast_to([C, 128])).then_inc(s["wrr_ready"], 1)
                with dve.Fori(0, B) as b:
                    norm_vector(nc, dve, s, b, T, XN, ln)
                    dve.wait_ge(s["row_copied"], b * 2 + 2)
                    rank_vector(nc, dve, s, b, rk, ident, below, 6)
                    nc.vector.tensor_scalar(rk["rank"][:, :], rk["rank"][:, :], float(KEEP2), None, ALU.is_lt)\
                        .then_inc(s["rk"], 1)
                    dve.wait_ge(s["rk"], b * 6 + 6)
                    nc.vector.tensor_tensor(gate[:, :], rk["rank"][:, :], rk["col"][:, :], ALU.mult).then_inc(s["gated"], 1)
                    dve.wait_ge(s["gated"], b + 1)
                    for g in range(2):
                        y = Y[:, 4 * g:4 * g + 4, :]
                        dve.wait_ge(s["y_ready"], b * 2 + g + 1)
                        nc.vector.tensor_tensor(y, P[6 + g].rearrange("p (t c) -> p t c", t=4),
                                                b2[:, None, :].broadcast_to([128, 4, C]), ALU.add).then_inc(s["y_scaled"], 1)
                    for g in range(2):
                        y = Y[:, 4 * g:4 * g + 4, :]
                        dve.wait_ge(s["y_scaled"], b * 4 + g + 1)
                        nc.vector.tensor_tensor(y, y, gate[:, 4 * g:4 * g + 4, None].broadcast_to([128, 4, C]), ALU.mult)\
                            .then_inc(s["y_scaled"], 1)
                    dve.wait_ge(s["t_plus_x"], b * 2 + 2)
                    for g in range(2):
                        dve.wait_ge(s["y_scaled"], b * 4 + g + 3)
                        t = T[:, bass.ds(b * NT + 4 * g, 4), :]
                        nc.vector.tensor_tensor(t, t, Y[:, 4 * g:4 * g + 4, :], ALU.add).then_inc(s["t_done"], 1)


E3 = 8
CAP = -(-5 * B * N // (4 * E3))
SLOTS = E3 * CAP
CT = CAP // 128
F3 = 4 * C


def stage_ffn3(nc, keep, PS, P, T, ident, upto_tri, d):
    with ExitStack() as ctx:
        def sb(name, shape, dt=F32):
            return ctx.enter_context(nc.sbuf_tensor("f3_" + name, shape, dt))

        buf = nc.dram_tensor("slots_in", [SLOTS + B * N, C], F32, kind="Internal").ap()
        ybuf = nc.dram_tensor("slots_out", [SLOTS, C], F32, kind="Internal").ap()
        ln = norm_tiles(sb)
        XN = sb("XN", [128, NT, C])
        XA = sb("XA", [128, TT, C])
        XC = sb("XC", [C, N])
        ZR = sb("ZR", [128, 8 * C])
        gw = sb("gw", [C, E3])
        gb = sb("gb", [128, E3])
        LG = sb("LG", [128, TT, E3])
        A1, A2 = sb("A1", [128, TT, E3]), sb("A2", [128, TT, E3])
        OH = sb("OH", [128, TT, E3])
        RX = sb("RX", [128, 8, TT])
        CU = sb("CU", [128, 2, TT + 16, E3])
        ecol, eslot = sb("ecol", [128, E3]), sb("eslot", [128, E3])
        ones = sb("ones", [128, 128])
        SC, SG = sb("SC", [128, TT], U32), sb("SG", [128, TT], U32)
        tok = sb("tok", [128, TT])
        W1 = sb("W1", [C, 2, F3])
        B1 = sb("B1", [128, 2, 4])
        W2 = sb("W2", [128, 2, 4, C])
        B2 = sb("B2", [128, 2, C])
        XB = sb("XB", [128, 2, CT, C])
        XT = sb("XT", [C, 2, CAP])
        H = sb("H", [128, 2, 4, CAP])
        YB = sb("YB", [128, 2, CT, C])
        YG = sb("YG", [128, TT, C])
        bad = sb("bad", [128, 8, C], U32)
        clamp = sb("clamp", [128, 3, 8 * C])
        names = NORM_SEMS + ("ld", "zero", "zeroed", "kept_x", "lg_ready", "lg_copied", "st", "sub", "exp", "tri_ready",
                             "scattered", "slot_ready", "gathered", "xt3_ready", "xt3_copied", "h_ready", "h_done",
                             "y_ready", "y_done", "fin", "cl")
        s = {n: keep.enter_context(nc.semaphore("f3_" + n)) for n in names}

        with nc.Block() as block:
            @block.sync
            def _(sp):
                for dst, src in ((gw[:, :], d["gate_w"]), (gb[:, :], d["gate_b"].broadcast_to([128, E3])),
                                 (ecol[:, :], d["ecol"].broadcast_to([128, E3])),
                                 (eslot[:, :], d["eslot"].broadcast_to([128, E3])),
                                 (tok[:, :], d["tok"])):
                    sp.dma_start(dst, src).then_inc(s["ld"], 16)
                sp.wait_ge(s["zero"], 1)
                for k in range(CT):
                    sp.dma_start(buf[k * 8 * 128:(k + 1) * 8 * 128, :].rearrange("(p r) c -> p (r c)", r=8), ZR[:, :])\
                        .then_inc(s["zeroed"], 16)

            @block.gpsimd
            def _(pool):
                nc.gpsimd.memset(ZR[:, :], 0.0).then_inc(s["zero"], 1)
                nc.gpsimd.memset(ones[:, :], 1.0)
                nc.gpsimd.memset(CU[:, :, 0:16, :], 0.0).then_inc(s["zero"], 1)
                with pool.Fori(0, B) as b:
                    for g in range(2):
                        pool.wait_ge(s["ln_done"], b * 2 + g + 1)
                        nc.gpsimd.tensor_copy(XA[:, bass.ds(b * NT + 4 * g, 4), :], XN[:, 4 * g:4 * g + 4, :])\
                            .then_inc(s["kept_x"], 1)
                pool.wait_ge(s["zeroed"], 16 * CT)
                pool.wait_ge(s["kept_x"], 2 * B)
                pool.wait_ge(s["slot_ready"], 1)
                for t in range(TT):
                    nc.gpsimd.indirect_dma_start(out=buf, out_offset=bass.IndirectOffsetOnAxis(ap=SC[:, t:t + 1], axis=0),
                                                 in_=XA[:, t, :], in_offset=None).then_inc(s["scattered"], 16)
                pool.wait_ge(s["scattered"], 16 * TT)

            @block.tensor
            def _(pe):
                pe.wait_ge(s["ld"], 80)
                with pe.Fori(0, B) as b:
                    norm_tensor(nc, pe, s, b, P, XN, ident)
                    pe.wait_ge(s["xc_ready"], b * 2 + 2)
                    for t in range(NT):
                        last = nc.tensor.matmul(P[2][:, t * E3:(t + 1) * E3], XC[:, t * 128:(t + 1) * 128], gw[:, :],
                                                start=True, stop=True)
                    last.then_inc(s["lg_ready"], 1)
                pe.wait_ge(s["st"], 6)
                pe.wait_ge(s["zero"], 2)
                oh = OH[:, :, :].rearrange("p t e -> p (t e)")
                nc.tensor.matmul(P[3][:, 0:TT * E3], upto_tri[:, :], oh, start=True, stop=True)
                nc.tensor.matmul(P[4][:, 0:TT * E3], ones[:, :], oh, start=True, stop=True).then_inc(s["tri_ready"], 1)

            @block.scalar
            def _(act):
                with act.Fori(0, B) as b:
                    norm_scalar(nc, act, s, b, P, XC, ln)
                act.wait_ge(s["st"], 1)
                nc.scalar.activation(A1[:, :, :], LG[:, :, :], ACT.Exp).then_inc(s["exp"], 1)

            @block.vector
            def _(dve):
                dve.wait_ge(s["ld"], 80)
                with dve.Fori(0, B) as b:
                    norm_vector(nc, dve, s, b, T, XN, ln)
                    dve.wait_ge(s["lg_ready"], b + 1)
                    nc.vector.tensor_tensor(LG[:, bass.ds(b * NT, NT), :], P[2][:, 0:NT * E3].rearrange("p (t e) -> p t e", e=E3),
                                            gb[:, None, :].broadcast_to([128, NT, E3]), ALU.add).then_inc(s["lg_copied"], 1)
                    dve.wait_ge(s["kept_x"], b * 2 + 2)
                link = Chain(dve, s["sub"])
                bc = lambda a: a[:, :, None].broadcast_to([128, TT, E3])
                dve.wait_ge(s["lg_copied"], B)
                link(nc.vector.tensor_reduce(RX[:, 0, :], LG[:, :, :], AX.X, ALU.max))
                nc.vector.tensor_tensor(LG[:, :, :], LG[:, :, :], bc(RX[:, 0, :]), ALU.subtract).then_inc(s["st"], 1)
                dve.wait_ge(s["exp"], 1)
                nc.vector.tensor_reduce(RX[:, 1, :], A1[:, :, :], AX.X, ALU.add).then_inc(s["st"], 1)
                nc.vector.tensor_reduce(RX[:, 0, :], A1[:, :, :], AX.X, ALU.max).then_inc(s["st"], 1)
                dve.wait_ge(s["st"], 3)
                nc.vector.reciprocal(RX[:, 2, :], RX[:, 1, :])
                link(nc.vector.tensor_tensor(A2[:, :, :], A1[:, :, :], bc(RX[:, 0, :]), ALU.is_ge))
                nc.vector.tensor_tensor(A2[:, :, :], A2[:, :, :], ecol[:, None, :].broadcast_to([128, TT, E3]), ALU.mult)\
                    .then_inc(s["st"], 1)
                dve.wait_ge(s["st"], 4)
                nc.vector.tensor_reduce(RX[:, 3, :], A2[:, :, :], AX.X, ALU.max).then_inc(s["st"], 1)
                dve.wait_ge(s["st"], 5)
                nc.vector.tensor_tensor(OH[:, :, :], A2[:, :, :], bc(RX[:, 3, :]), ALU.is_ge).then_inc(s["st"], 1)
                dve.wait_ge(s["tri_ready"], 1)
                dve.wait_ge(s["zero"], 2)
                n4 = P[4][:, 0:TT * E3].rearrange("p (t e) -> p t e", e=E3)
                link(nc.vector.tensor_copy(CU[:, 0, 16:, :], n4))
                for k, sh in enumerate((1, 2, 4, 8, 16)):
                    a, z = k % 2, (k + 1) % 2
                    link(nc.vector.tensor_tensor(CU[:, z, 16:, :], CU[:, a, 16:, :], CU[:, a, 16 - sh:16 + TT - sh, :], ALU.add))
                link(nc.vector.tensor_tensor(A1[:, :, :], P[3][:, 0:TT * E3].rearrange("p (t e) -> p t e", e=E3),
                                             CU[:, 1, 15:15 + TT, :], ALU.add))
                link(nc.vector.tensor_tensor(A1[:, :, :], A1[:, :, :], OH[:, :, :], ALU.mult))
                link(nc.vector.tensor_reduce(RX[:, 3, :], A1[:, :, :], AX.X, ALU.add))
                link(nc.vector.tensor_tensor(A2[:, :, :], OH[:, :, :], eslot[:, None, :].broadcast_to([128, TT, E3]), ALU.mult))
                link(nc.vector.tensor_reduce(RX[:, 4, :], A2[:, :, :], AX.X, ALU.add))
                link(nc.vector.tensor_scalar(RX[:, 5, :], RX[:, 3, :], float(CAP), None, ALU.is_le))
                link(nc.vector.tensor_scalar(RX[:, 6, :], RX[:, 3, :], float(CAP), None, ALU.min))
                link(nc.vector.tensor_tensor(RX[:, 6, :], RX[:, 6, :], RX[:, 4, :], ALU.add))
                link(nc.vector.tensor_copy(SG[:, :], RX[:, 6, :]))
                link(nc.vector.tensor_tensor(RX[:, 6, :], RX[:, 6, :], tok[:, :], ALU.subtract))
                link(nc.vector.tensor_tensor(RX[:, 6, :], RX[:, 6, :], RX[:, 5, :], ALU.mult))
                link(nc.vector.tensor_tensor(RX[:, 6, :], RX[:, 6, :], tok[:, :], ALU.add))
                link(nc.vector.tensor_tensor(RX[:, 7, :], RX[:, 5, :], RX[:, 2, :], ALU.mult))
                nc.vector.tensor_copy(SC[:, :], RX[:, 6, :]).then_inc(s["slot_ready"], 1)

        w_ld, x_ld, y_stored = [[keep.enter_context(nc.semaphore(f"f3_{n}{k}")) for k in range(2)]
                                for n in ("w_ld", "x_ld", "y_stored")]
        sub = 2
        cols = CAP // sub
        with nc.Block() as block:
            @block.gpsimd
            def _(pool):
                def load(e, k):
                    for dst, src in ((W1[:, k, :], d["w1e"][bass.ds(e * C, C), :]),
                                     (W2[:, k, :, :].rearrange("p m c -> p (m c)"), d["w2e"][bass.ds(e * 128, 128), :]),
                                     (B1[:, k, :], d["b1e"][bass.ds(e * 128, 128), :]),
                                     (B2[:, k, :], d["b2e"][bass.ds(e, 1), :].broadcast_to([128, C]))):
                        pool.dma_start(dst, src).then_inc(w_ld[k], 16)
                    pool.dma_start(XB[:, k, :, :], buf[bass.ds(e * CAP, CAP), :].rearrange("(t p) c -> p t c", p=128))\
                        .then_inc(x_ld[k], 16)

                load(0, 0)
                load(1, 1)
                with pool.Fori(0, E3 // 2 - 1) as h:
                    for k in range(2):
                        pool.wait_ge(s["y_done"], (h * 2 + k) * 2 + 2)
                        load(h * 2 + 2 + k, k)
                for k in range(2):
                    pool.wait_ge(y_stored[k], 16 * (E3 // 2) + 1)
                for t in range(TT):
                    nc.gpsimd.indirect_dma_start(out=YG[:, t, :], out_offset=None, in_=ybuf,
                                                 in_offset=bass.IndirectOffsetOnAxis(ap=SG[:, t:t + 1], axis=0))\
                        .then_inc(s["gathered"], 16)
                pool.wait_ge(s["gathered"], 16 * TT)

            @block.tensor
            def _(pe):
                with pe.Fori(0, E3 // 2) as turn:
                    e = turn * 2
                    for k in range(2):
                        pe.wait_ge(x_ld[k], turn * 16 + 16)
                        pe.wait_ge(w_ld[k], turn * 64 + 64)
                        for t in range(CT):
                            last = nc.tensor.transpose(P[t // 4][:, (t % 4) * 128:(t % 4 + 1) * 128], XB[:, k, t, :], ident[:, :])
                        last.then_inc(s["xt3_ready"], 1)
                        pe.wait_ge(s["xt3_copied"], (e + k) * 2 + 2)
                        for j in range(4 * sub):
                            m, c = divmod(j, sub)
                            if j >= 4:
                                pe.wait_ge(s["h_done"], (e + k) * 4 * sub + j - 3)
                            nc.tensor.matmul(P[2 + j % 4][:, 0:cols], W1[:, k, m * 128:(m + 1) * 128],
                                             XT[:, k, c * cols:(c + 1) * cols], start=True, stop=True).then_inc(s["h_ready"], 1)
                        pe.wait_ge(s["h_done"], (e + k + 1) * 4 * sub)
                        for t in range(CT):
                            for m in range(4):
                                last = nc.tensor.matmul(P[6 + t // 4][:, (t % 4) * 128:(t % 4 + 1) * 128],
                                                        H[:, k, m, t * 128:(t + 1) * 128], W2[:, k, m, :],
                                                        start=(m == 0), stop=(m == 3))
                        last.then_inc(s["y_ready"], 1)
                        pe.wait_ge(s["y_done"], (e + k) * 2 + 2)

            @block.scalar
            def _(act):
                with act.Fori(0, E3 // 2) as turn:
                    e = turn * 2
                    for k in range(2):
                        for j in range(4 * sub):
                            m, c = divmod(j, sub)
                            act.wait_ge(s["h_ready"], (e + k) * 4 * sub + j + 1)
                            nc.scalar.activation(H[:, k, m, c * cols:(c + 1) * cols], P[2 + j % 4][:, 0:cols], ACT.Relu,
                                                 bias=B1[:, k, m:m + 1])\
                                .then_inc(s["h_done"], 1)
                        act.wait_ge(s["y_done"], (e + k) * 2 + 2)
                        act.dma_start(ybuf[bass.ds((e + k) * CAP, CAP), :].rearrange("(t p) c -> p t c", p=128),
                                      YB[:, k, :, :]).then_inc(y_stored[k], 16)

            @block.vector
            def _(dve):
                for j, v in enumerate((0.0, 1e4, -1e4)):
                    ins = nc.vector.memset(clamp[:, j, :], v)
                    if j < 2:
                        ins.then_inc(y_stored[j], 1)
                ins.then_inc(s["cl"], 1)
                with dve.Fori(0, E3 // 2) as turn:
                    e = turn * 2
                    for k in range(2):
                        dve.wait_ge(s["xt3_ready"], e + k + 1)
                        nc.vector.tensor_copy(XT[:, k, 0:HALF], P[0]).then_inc(s["xt3_copied"], 1)
                        nc.vector.tensor_copy(XT[:, k, HALF:], P[1][:, 0:CAP - HALF]).then_inc(s["xt3_copied"], 1)
                        dve.wait_ge(s["y_ready"], e + k + 1)
                        dve.wait_ge(y_stored[k], turn * 16 + 1)
                        nc.vector.tensor_tensor(YB[:, k, 0:4, :], P[6].rearrange("p (t c) -> p t c", t=4),
                                                B2[:, k:k + 1, :].broadcast_to([128, 4, C]), ALU.add).then_inc(s["y_done"], 1)
                        nc.vector.tensor_tensor(YB[:, k, 4:, :], P[7][:, 0:CAP - HALF].rearrange("p (t c) -> p t c", c=C),
                                                B2[:, k:k + 1, :].broadcast_to([128, CT - 4, C]), ALU.add).then_inc(s["y_done"], 1)
                dve.wait_ge(s["cl"], 1)
                dve.wait_ge(s["gathered"], 16 * TT)
                link = Chain(dve, s["fin"])
                for t in range(0, TT, 8):
                    y = YG[:, t:t + 8, :]
                    link(nc.vector.tensor_tensor(y, y, RX[:, 7, t:t + 8, None].broadcast_to([128, 8, C]), ALU.mult))
                    big = float(np.finfo(np.float32).max)
                    for j in range(3):
                        if j == 0:
                            link(nc.vector.tensor_tensor(bad[:, :, :], y, y, ALU.not_equal))
                        else:
                            link(nc.vector.tensor_scalar(bad[:, :, :], y, big if j == 1 else -big, None,
                                                         ALU.is_gt if j == 1 else ALU.is_lt))
                        link(nc.vector.copy_predicated(y, bad[:, :, :], clamp[:, j, :].rearrange("p (a c) -> p a c", a=8)))
                    link(nc.vector.tensor_tensor(T[:, t:t + 8, :], T[:, t:t + 8, :], y, ALU.add))


H3 = 16
QUAD = 4
NQ = H3 // QUAD
DH = 64
VD = 32
QR_, KR_ = 48, 32
KEEP3 = 256
SMALL = QR_ + KR_ + VD + 3
PW = N + KEEP3 + 256


def stage_attn3(nc, keep, PS, P, T, ident, identb, masks, lohi, below, tri, d):
    with ExitStack() as ctx:
        def sb(name, shape, dt=F32):
            return ctx.enter_context(nc.sbuf_tensor("a3_" + name, shape, dt))

        ln = norm_tiles(sb)
        PR = sb("PR", [128, 2, PW])
        PT = sb("PT", [128, 2, QUAD, PW])
        XC = sb("XC", [C, N])
        prf = PR[:, :, :].rearrange("p a n -> p (a n)")
        XN = prf[:, 0:N].rearrange("p (t c) -> p t c", t=NT)
        ptf = PT[:, :, :, :].rearrange("p a h n -> p (a h n)")
        SEL = ptf[:, 0:NT * KEEP3].rearrange("p (t j) -> p t j", t=NT)
        rk = {"row": prf[:, N:2 * N], "ex": prf[:, 2 * N:3 * N].rearrange("p (t c) -> p t c", t=NT),
              "junk": ptf[:, NT * KEEP3:NT * KEEP3 + NT * (N + 128) // 2].bitcast(BF16).rearrange("p (t n) -> p t n", t=NT),
              "col": sb("rk_col", [128, NT]), "cnt": sb("rk_cnt", [128, 3, NT]), "rank": sb("rk_rank", [128, NT])}
        WS = sb("WS", [C, SMALL])
        wimp = sb("wimp", [C, 1])
        wimpr = sb("wimpr", [C, 128])
        SM = sb("SM", [128, NT, SMALL])
        ms = sb("ms", [128, 3, 2, NT])
        nw = sb("nw", [128, QR_ + KR_])
        spare = NT * (KEEP3 + (N + 128) // 2)
        widths = (QR_ + KR_, KR_ + VD + QR_, VD, VD)
        starts = [spare + NT * sum(widths[:k]) for k in range(4)]
        SQ, CK, t1, t2 = [ptf[:, a:a + NT * w].rearrange("p (t c) -> p t c", t=NT) for a, w in zip(starts, widths)]
        gs = sb("gs", [128, 6, 3])
        mean = sb("mean", [128, 128])
        ones = sb("ones", [128, 128])
        iota = sb("iota", [128, KEEP3])
        posn = sb("posn", [128, NT])
        cu = sb("cu", [128, 2, NT + 8])
        cosT, sinT = sb("cosT", [128, NT, VD]), sb("sinT", [128, NT, VD])
        CF = sb("CF", [KR_ + VD + QR_, N])
        CKF, CQF = CF[0:KR_ + VD, :], CF[KR_ + VD:, :]
        XS = sb("XS", [C, KEEP3])
        WQ = sb("WQ", [KR_ + VD + QR_, QUAD * DH])[KR_ + VD:, :]
        WKW, WKS = sb("WKW", [C, QUAD * DH]), sb("WKS", [C, QUAD * DH])
        WK1 = sb("WK1", [KR_ + VD, QUAD, 2, DH])
        WV = sb("WV", [KR_, QUAD * VD])
        WVW, WVS = sb("WVW", [C, QUAD * VD]), sb("WVS", [C, QUAD * VD])
        WP = sb("WP", [128, NQ, C])
        TM = sb("TM", [128, 2, 2 * QUAD, 2, DH])
        RA, RB = sb("RA", [128, 2, 2, QUAD, VD]), sb("RB", [128, 2, 2, QUAD, VD])
        R = sb("R", [128, 2, HALF], F32R)
        QH, QL = sb("QH", [128, QUAD, N], F32R), sb("QL", [128, QUAD, N], F32R)
        K1, KW = sb("K1", [128, QUAD, N], F32R), sb("KW", [128, QUAD, N], F32R)
        KS = sb("KS", [128, QUAD, KEEP3], F32R)
        V1, VW, VS = sb("V1", [128, NT, 128]), sb("VW", [128, NT, 128]), sb("VS", [128, 2, 128])
        NM, L, RL = sb("NM", [128, 2, 3]), sb("L", [128, 2, 3]), sb("RL", [128, 2, 3])
        YT = sb("YT", [128, 2, 128])
        names = NORM_SEMS + (
            "ld", "ready", "sm_ready", "sm_copied", "row_ready", "row_copied", "rk", "sel", "selt_ready", "gsum", "gmean", "gsub",
            "gexp", "gate", "rms", "rms_std", "latent", "lt_ready", "lt_copied", "onehot", "xs_ready", "xs_copied",
            "wk_ld", "prepared", "a_ready", "a_copied", "rope", "rope_added", "tr_ready", "tr_round", "tr_split",
            "b_ready", "b_round", "b_split", "v_copied", "s1_ready", "s23_ready", "max1", "max23", "exp1", "exp23",
            "rl", "pos", "prob_ready", "pt_ready", "pt_copied", "pv_ready", "yt_copied", "proj_ready", "added")
        s = {n: keep.enter_context(nc.semaphore("a3_" + n)) for n in names}

        groups = [("q", g) for g in range(4)] + [("w", g) for g in range(4)] + [("s", 0)]
        NG = len(groups)
        plain = [("k1", h, half) for h in range(QUAD) for half in range(2)] + \
                [("v1", 0, 0), ("v1", 1, 0), ("vw", 0, 0), ("vw", 1, 0), ("vs", 0, 0)]
        nk1 = 2 * QUAD
        LAG = 2
        plan = []
        left = list(range(len(plain)))
        for k in range(NG + LAG):
            plan.append((k if k < NG else None, [left.pop(0) for _ in range(2) if left], k - LAG if k >= LAG else None))
        assert not left

        units = [(i, h) for i in range(NT) for h in range(QUAD)]
        NU = len(units)
        win = lambda i: 256 if i else 128
        tiles = lambda i: i + 1 + KEEP3 // 128 + win(i) // 128
        first_bank, banks = [], []
        for n, (i, h) in enumerate(units):
            first_bank.append(len(banks))
            banks += [(n, j, min(4, tiles(i) - j)) for j in range(0, tiles(i), 4)]
        first_bank.append(len(banks))
        NB = len(banks)
        slot = lambda n: PS[:, 2 * (n % 2):2 * (n % 2) + 2, :].rearrange("p a n -> p (a n)")
        S23 = P[4]

        with nc.Block() as block:
            @block.sync
            def _(sp):
                for dst, src in ((WS[:, :], d["w_small"]), (wimp[:, :], d["w_imp"]), (nw[:, :], d["norm_w"].broadcast_to([128, 80])),
                                 (cosT[:, :, :], d["cos"]), (sinT[:, :, :], d["sin"]), (iota[:, :], d["iota"].broadcast_to([128, 256])),
                                 (WP[:, :, :], d["w_proj3"]), (WK1[:, :, :, :], d["wk1_const"])):
                    sp.dma_start(dst, src).then_inc(s["ld"], 16)

            @block.gpsimd
            def _(pool):
                nc.gpsimd.memset(ones[:, :], 1.0).then_inc(s["ready"], 1)
                nc.gpsimd.memset(mean[:, :], 1.0 / N).then_inc(s["ready"], 1)
                nc.gpsimd.memset(cu[:, :, 0:8], 0.0).then_inc(s["ready"], 1)
                pool.wait_ge(s["ld"], 128)
                with pool.Fori(0, B) as b:
                    with pool.Fori(0, NQ) as g:
                        q = b * NQ + g
                        pool.wait_ge(s["prepared"], q + 1)
                        for dst, src in ((WQ[:, :], d["wq3"][bass.ds(g * QR_, QR_), :]),
                                         (WKW[:, :], d["wkw"][bass.ds(g * C, C), :]),
                                         (WKS[:, :], d["wks"][bass.ds(g * C, C), :]),
                                         (WV[:, :], d["wv"][bass.ds(g * KR_, KR_), :]),
                                         (WVW[:, :], d["wvw"][bass.ds(g * C, C), :]),
                                         (WVS[:, :], d["wvs"][bass.ds(g * C, C), :]),
                                         (WK1[0:KR_, :, 0, 0:32], d["wk1"][bass.ds(g * KR_, KR_), :].rearrange("p (h c) -> p h c", h=QUAD)),
                                         (WK1[0:KR_, :, 1, 0:32], d["wk1"][bass.ds(g * KR_, KR_), :].rearrange("p (h c) -> p h c", h=QUAD))):
                            pool.dma_start(dst, src).then_inc(s["wk_ld"], 16)
                        for k in range(NG):
                            pool.wait_ge(s["rope"], q * NG + k + 1)
                            ra, rb = [x[:, k % 2, :, :, :].rearrange("p a h c -> p (a h) c")[:, :, None, :]
                                      .broadcast_to([128, 2 * QUAD, 2, VD]) for x in (RA, RB)]
                            nc.gpsimd.tensor_tensor(TM[:, k % 2, :, :, 32:], ra, rb, ALU.add)\
                                .then_inc(s["rope_added"], 1)

            @block.tensor
            def _(pe):
                def group(q, k):
                    kind, g = groups[k]
                    if k >= 2:
                        pe.wait_ge(s["a_copied"], q * NG + k - 1)
                    src, w = {"q": (CQF, WQ), "w": (XC, WKW), "s": (XS, WKS)}[kind]
                    for j in range(2):
                        c = (2 * g + j) * 128
                        last = nc.tensor.matmul(P[k % 2][:, j * 256:(j + 1) * 256], src[:, c:c + 128], w[:, :],
                                                start=True, stop=True)
                    last.then_inc(s["a_ready"], 1)

                def plain_product(q, k):
                    kind, x, half = plain[k]
                    bank = P[6 + k % 2]
                    if k >= 2:
                        if k - 2 < nk1:
                            pe.wait_ge(s["b_split"], q * nk1 + k - 1)
                        else:
                            pe.wait_ge(s["v_copied"], q * 5 + k - nk1 - 1)
                    if kind == "k1":
                        last = nc.tensor.matmul(bank, WK1[:, x, :, :].rearrange("p r c -> p (r c)"),
                                                CKF[:, half * HALF:(half + 1) * HALF], start=True, stop=True)
                    else:
                        src, w, nt = {"v1": (CKF[0:KR_, :], WV, 4), "vw": (XC[:, :], WVW, 4), "vs": (XS[:, :], WVS, 2)}[kind]
                        for t in range(nt):
                            c = (4 * x + t) * 128
                            last = nc.tensor.matmul(bank[:, t * 128:(t + 1) * 128], src[:, c:c + 128], w[:, :],
                                                    start=True, stop=True)
                    last.then_inc(s["b_ready"], 1)

                def turn_group(q, k):
                    pe.wait_ge(s["rope_added"], q * NG + k + 1)
                    for j in range(2):
                        u = 2 * k + j
                        if u >= 4:
                            pe.wait_ge(s["tr_split"], q * 2 * NG + u - 3)
                        for h in range(QUAD):
                            last = nc.tensor.transpose(P[2 + u % 4][:, h * 128:(h + 1) * 128],
                                                       TM[:, k % 2, j * QUAD + h, :, :].rearrange("p r c -> p (r c)"), ident[:, :])
                        last.then_inc(s["tr_ready"], 1)

                def scores_full(q, n):
                    i, h = units[n]
                    S = slot(n)
                    w = (i + 1) * 128
                    qh, ql = QH[:, h, i * 128:(i + 1) * 128], QL[:, h, i * 128:(i + 1) * 128]
                    if n >= 2:
                        pe.wait_ge(s["exp1"], q * NU + n - 1)
                    for c0 in range(0, w, HALF):
                        c1 = min(w, c0 + HALF)
                        nc.tensor.matmul(S[:, c0:c1], qh, K1[:, h, c0:c1], start=True, stop=False)
                        last = nc.tensor.matmul(S[:, c0:c1], ql, K1[:, h, c0:c1], start=False, stop=c1 < w)
                    nc.tensor.matmul(S[:, w - 128:w], identb[:, :], masks[:, 0, :], start=False, stop=True)\
                        .then_inc(s["s1_ready"], 1)

                def scores_short(q, n):
                    i, h = units[n]
                    qh, ql = QH[:, h, i * 128:(i + 1) * 128], QL[:, h, i * 128:(i + 1) * 128]
                    if n >= 1:
                        pe.wait_ge(s["exp23"], q * NU + n)
                    k0, c = max(0, i - 1) * 128, HALF - win(i)
                    nc.tensor.matmul(S23[:, 0:KEEP3], qh, KS[:, h, :], start=True, stop=False)
                    nc.tensor.matmul(S23[:, 0:KEEP3], ql, KS[:, h, :], start=False, stop=False)
                    nc.tensor.matmul(S23[:, c:], qh, KW[:, h, k0:(i + 1) * 128], start=False, stop=False)
                    nc.tensor.matmul(S23[:, c:], ql, KW[:, h, k0:(i + 1) * 128], start=False, stop=False)
                    nc.tensor.matmul(S23[:, c:], identb[:, :], masks[:, 1 if i else 2:3, :].rearrange("p a n -> p (a n)"),
                                     start=False, stop=True).then_inc(s["s23_ready"], 1)

                def transposes(q, n):
                    pe.wait_ge(s["prob_ready"], q * NU + n + 1)
                    for k in range(first_bank[n], first_bank[n + 1]):
                        if k >= 2:
                            pe.wait_ge(s["pt_copied"], q * NB + k - 1)
                        _, j0, m = banks[k]
                        for j in range(m):
                            last = nc.tensor.transpose(P[5 + k % 2][:, j * 128:(j + 1) * 128],
                                                       PR[:, n % 2, (j0 + j) * 128:(j0 + j + 1) * 128], ident[:, :])
                        last.then_inc(s["pt_ready"], 1)

                def values(q, i):
                    pe.wait_ge(s["pt_copied"], q * NB + first_bank[QUAD * (i + 1)])
                    if i >= 1:
                        pe.wait_ge(s["added"], q * NT + i)
                    src = [V1[:, j, :] for j in range(i + 1)] + [VS[:, 0, :], VS[:, 1, :]] + \
                          [VW[:, j, :] for j in range(max(0, i - 1), i + 1)]
                    for j, v in enumerate(src):
                        for h in range(QUAD):
                            last = nc.tensor.matmul(P[7][h * VD:(h + 1) * VD, 0:128], v[:, h * VD:(h + 1) * VD],
                                                    PT[:, i % 2, h, j * 128:(j + 1) * 128],
                                                    start=(j == 0), stop=(j == len(src) - 1))
                    last.then_inc(s["pv_ready"], 1)

                def project(q, g, i):
                    pe.wait_ge(s["yt_copied"], q * NT + i + 1)
                    nc.tensor.matmul(P[7][:, 128:256], YT[:, i % 2, :], WP[:, bass.ds(g, 1), :].rearrange("p a c -> p (a c)"),
                                     start=True, stop=True).then_inc(s["proj_ready"], 1)

                pe.wait_ge(s["ready"], 4)
                with pe.Fori(0, B) as b:
                    norm_tensor(nc, pe, s, b, P, XN, ident)
                    pe.wait_ge(s["xc_ready"], b * 2 + 2)
                    for half in range(2):
                        nc.tensor.matmul(P[4 + half], wimpr[:, :], XC[:, half * HALF:(half + 1) * HALF],
                                         start=True, stop=True).then_inc(s["row_ready"], 1)
                    for half in range(2):
                        for t in range(4):
                            c = (4 * half + t) * 128
                            last = nc.tensor.matmul(P[2 + half][:, t * 128:t * 128 + SMALL], XC[:, c:c + 128], WS[:, :],
                                                    start=True, stop=True)
                        last.then_inc(s["sm_ready"], 1)
                    pe.wait_ge(s["gsum"], b + 1)
                    nc.tensor.matmul(P[6][:, 0:3], mean[:, :], gs[:, 0, :], start=True, stop=True).then_inc(s["gmean"], 1)
                    pe.wait_ge(s["latent"], b + 1)
                    for half in range(2):
                        for t in range(4):
                            last = nc.tensor.transpose(P[4 + half][0:KR_ + VD + QR_, t * 128:(t + 1) * 128],
                                                       CK[:, 4 * half + t, :], ident[:, :])
                        last.then_inc(s["lt_ready"], 1)
                    pe.wait_ge(s["sel"], b * 5 + 1)
                    nc.tensor.matmul(P[7][:, 0:NT], tri[:, :], rk["rank"][:, :], start=True, stop=True)
                    nc.tensor.matmul(P[7][:, NT:2 * NT], ones[:, :], rk["rank"][:, :], start=True, stop=True)\
                        .then_inc(s["selt_ready"], 1)
                    pe.wait_ge(s["onehot"], b + 1)
                    for t in range(NT):
                        last = nc.tensor.matmul(P[6][:, 0:KEEP3], XN[:, t, :], SEL[:, t, :], start=(t == 0), stop=(t == NT - 1))
                    last.then_inc(s["xs_ready"], 1)
                    with pe.Fori(0, NQ) as g:
                        q = b * NQ + g
                        pe.wait_ge(s["lt_copied"], b * 2 + 2)
                        pe.wait_ge(s["xs_copied"], b + 1)
                        pe.wait_ge(s["wk_ld"], q * 128 + 128)
                        for a, bs, t in plan:
                            if a is not None:
                                group(q, a)
                            for k in bs:
                                plain_product(q, k)
                            if t is not None:
                                turn_group(q, t)
                        pe.wait_ge(s["tr_split"], q * 2 * NG + 2 * NG)
                        pe.wait_ge(s["b_split"], q * nk1 + nk1)
                        pe.wait_ge(s["v_copied"], q * 5 + 5)
                        scores_full(q, 0)
                        scores_short(q, 0)
                        for n, (i, h) in enumerate(units):
                            if n + 1 < NU:
                                scores_full(q, n + 1)
                            if h == 3 and i > 0:
                                project(q, g, i - 1)
                            if n >= 1:
                                transposes(q, n - 1)
                            if n + 1 < NU:
                                scores_short(q, n + 1)
                            if h == 1 and i > 0:
                                values(q, i - 1)
                        transposes(q, NU - 1)
                        values(q, NT - 1)
                        project(q, g, NT - 1)
                        pe.wait_ge(s["added"], q * NT + NT)

            @block.scalar
            def _(act):
                def copy_banks(q, n):
                    i, h = units[n]
                    if h == 0 and i >= 2:
                        act.wait_ge(s["pv_ready"], q * NT + i - 1)
                    for k in range(first_bank[n], first_bank[n + 1]):
                        _, j0, m = banks[k]
                        act.wait_ge(s["pt_ready"], q * NB + k + 1)
                        nc.scalar.activation(PT[:, i % 2, h, j0 * 128:(j0 + m) * 128], P[5 + k % 2][:, 0:m * 128],
                                             ACT.Copy).then_inc(s["pt_copied"], 1)

                with act.Fori(0, B) as b:
                    norm_scalar(nc, act, s, b, P, XC, ln)
                    for half in range(2):
                        act.wait_ge(s["row_ready"], b * 2 + half + 1)
                        nc.scalar.activation(rk["row"][:, half * HALF:(half + 1) * HALF], P[4 + half], ACT.Copy)\
                            .then_inc(s["row_copied"], 1)
                    for half in range(2):
                        act.wait_ge(s["sm_ready"], b * 2 + half + 1)
                        nc.scalar.activation(SM[:, 4 * half:4 * half + 4, :],
                                             P[2 + half].rearrange("p (t c) -> p t c", t=4)[:, :, 0:SMALL], ACT.Copy)\
                            .then_inc(s["sm_copied"], 1)
                    act.wait_ge(s["rms"], b * 5 + 4)
                    nc.scalar.activation(ms[:, 1, :, :], ms[:, 0, :, :], ACT.Sqrt).then_inc(s["rms_std"], 1)
                    act.wait_ge(s["gsub"], b + 1)
                    nc.scalar.activation(gs[:, 3, :], gs[:, 2, :], ACT.Exp).then_inc(s["gexp"], 1)
                    for half in range(2):
                        act.wait_ge(s["lt_ready"], b * 2 + half + 1)
                        nc.scalar.activation(CF[:, half * HALF:(half + 1) * HALF], P[4 + half][0:KR_ + VD + QR_, :], ACT.Copy)\
                            .then_inc(s["lt_copied"], 1)
                    act.wait_ge(s["xs_ready"], b + 1)
                    nc.scalar.activation(XS[:, :], P[6][:, 0:KEEP3], ACT.Copy).then_inc(s["xs_copied"], 1)
                    with act.Fori(0, NQ) as g:
                        q = b * NQ + g
                        for a, bs, t in plan:
                            if a is not None:
                                act.wait_ge(s["a_ready"], q * NG + a + 1)
                                if a >= 2:
                                    act.wait_ge(s["tr_ready"], q * 2 * NG + 2 * (a - 1))
                                nc.scalar.activation(TM[:, a % 2, :, :, :],
                                                     P[a % 2].rearrange("p (a c) -> p a c", c=DH)[:, :, None, :]
                                                     .broadcast_to([128, 2 * QUAD, 2, DH]), ACT.Copy)\
                                    .then_inc(s["a_copied"], 1)
                            for k in bs:
                                kind, x, half = plain[k]
                                act.wait_ge(s["b_ready"], q * len(plain) + k + 1)
                                if kind == "k1":
                                    if k >= 2:
                                        act.wait_ge(s["b_split"], q * nk1 + k - 1)
                                    nc.scalar.activation(R[:, k % 2, :], P[6 + k % 2], ACT.Copy).then_inc(s["b_round"], 1)
                                else:
                                    dst, nt = {"v1": (V1, 4), "vw": (VW, 4), "vs": (VS, 2)}[kind]
                                    nc.scalar.activation(dst[:, 4 * x:4 * x + nt, :].rearrange("p t c -> p (t c)"),
                                                         P[6 + k % 2][:, 0:nt * 128], ACT.Copy).then_inc(s["v_copied"], 1)
                            if t is not None:
                                kind, g4 = groups[t]
                                for j in range(2):
                                    u, c = 2 * t + j, (2 * g4 + j) * 128
                                    dst = {"q": QH, "w": KW, "s": KS}[kind]
                                    act.wait_ge(s["tr_ready"], q * 2 * NG + u + 1)
                                    nc.scalar.activation(dst[:, :, c:c + 128], P[2 + u % 4].rearrange("p (h c) -> p h c", h=QUAD),
                                                         ACT.Copy, scale=0.125 if kind == "q" else 1.0).then_inc(s["tr_round"], 1)
                        for n, (i, h) in enumerate(units):
                            w, m = (i + 1) * 128, n % 2
                            act.wait_ge(s["max1"], q * NU + n + 1)
                            if n >= 2:
                                act.wait_ge(s["pt_ready"], q * NB + first_bank[n - 1])
                            nc.scalar.activation(PR[:, m, 0:w], slot(n)[:, 0:w], ACT.Exp, bias=NM[:, m, 0:1],
                                                 accum_out=L[:, m, 0:1]).then_inc(s["exp1"], 1)
                            act.wait_ge(s["max23"], q * NU + n + 1)
                            nc.scalar.activation(PR[:, m, w:w + KEEP3], S23[:, 0:KEEP3], ACT.Exp, bias=NM[:, m, 1:2],
                                                 accum_out=L[:, m, 1:2])
                            nc.scalar.activation(PR[:, m, w + KEEP3:w + KEEP3 + win(i)], S23[:, HALF - win(i):], ACT.Exp,
                                                 bias=NM[:, m, 2:3], accum_out=L[:, m, 2:3]).then_inc(s["exp23"], 1)
                            if n >= 1:
                                copy_banks(q, n - 1)
                        copy_banks(q, NU - 1)

            @block.vector
            def _(dve):
                def max_full(q, n):
                    i, h = units[n]
                    m = n % 2
                    dve.wait_ge(s["s1_ready"], q * NU + n + 1)
                    if n >= 2:
                        dve.wait_ge(s["exp1"], q * NU + n - 1)
                    nc.vector.tensor_reduce(NM[:, m, 0:1], slot(n)[:, 0:(i + 1) * 128], AX.X, ALU.max,
                                            negate=True).then_inc(s["max1"], 1)

                def max_short(q, n):
                    i, h = units[n]
                    m = n % 2
                    if n >= 2:
                        dve.wait_ge(s["exp23"], q * NU + n - 1)
                    dve.wait_ge(s["s23_ready"], q * NU + n + 1)
                    if i:
                        ins = nc.vector.tensor_reduce(NM[:, m, 1:3], S23.rearrange("p (a n) -> p a n", a=2), AX.X, ALU.max,
                                                      negate=True)
                    else:
                        nc.vector.tensor_reduce(NM[:, m, 1:2], S23[:, 0:KEEP3], AX.X, ALU.max, negate=True)
                        ins = nc.vector.tensor_reduce(NM[:, m, 2:3], S23[:, HALF - 128:], AX.X, ALU.max, negate=True)
                    ins.then_inc(s["max23"], 1)

                def normalise(q, n):
                    i, h = units[n]
                    m, w = n % 2, (i + 1) * 128
                    dve.wait_ge(s["exp23"], q * NU + n + 1)
                    nc.vector.reciprocal(RL[:, m, :], L[:, m, :]).then_inc(s["rl"], 1)
                    dve.wait_ge(s["rl"], (q * NU + n) * 2 + 1)
                    nc.vector.tensor_tensor(RL[:, m, :], RL[:, m, :], gs[:, 5, :], ALU.mult).then_inc(s["rl"], 1)
                    dve.wait_ge(s["rl"], (q * NU + n) * 2 + 2)
                    for c0, c1, j in ((0, w, 0), (w, w + KEEP3, 1), (w + KEEP3, w + KEEP3 + win(i), 2)):
                        ins = nc.vector.tensor_scalar(PR[:, m, c0:c1], PR[:, m, c0:c1], RL[:, m, j:j + 1], None, ALU.mult)
                    ins.then_inc(s["prob_ready"], 1)

                def head_out(q, i):
                    dve.wait_ge(s["pv_ready"], q * NT + i + 1)
                    nc.vector.tensor_copy(YT[:, i % 2, :], P[7][:, 0:128]).then_inc(s["yt_copied"], 1)

                def residual(q, b, i):
                    dve.wait_ge(s["proj_ready"], q * NT + i + 1)
                    t = T[:, bass.ds(b * NT + i, 1), :].rearrange("p a c -> p (a c)")
                    nc.vector.tensor_tensor(t, t, P[7][:, 128:256], ALU.add).then_inc(s["added"], 1)

                def rotate(q, k):
                    kind, g = groups[k]
                    x = TM[:, k % 2, :, 0, 32:].rearrange("p (a h) c -> p a h c", a=2)
                    cos = cosT[:, 2 * g:2 * g + 2, None, :].broadcast_to([128, 2, QUAD, 32])
                    sin = sinT[:, 2 * g:2 * g + 2, None, :].broadcast_to([128, 2, QUAD, 32])
                    dve.wait_ge(s["a_copied"], q * NG + k + 1)
                    if k >= 2:
                        dve.wait_ge(s["rope_added"], q * NG + k - 1)
                    nc.vector.tensor_tensor(RA[:, k % 2, :, :, :], x, cos, ALU.mult)
                    nc.vector.tensor_tensor(RB[:, k % 2, :, :, 0:16], x[:, :, :, 16:], sin[:, :, :, 0:16], ALU.mult)
                    nc.vector.tensor_tensor(RB[:, k % 2, :, :, 16:], x[:, :, :, 0:16], sin[:, :, :, 16:], ALU.mult)\
                        .then_inc(s["rope"], 1)

                dve.wait_ge(s["ld"], 128)
                nc.vector.memset(rk["cnt"][:, 0, 0:1], 0.0).then_inc(s["prepared"], 1)
                nc.vector.tensor_copy(wimpr[:, :], wimp[:, 0:1].broadcast_to([C, 128])).then_inc(s["ready"], 1)
                with dve.Fori(0, B) as b:
                    norm_vector(nc, dve, s, b, T, XN, ln)
                    dve.wait_ge(s["sm_copied"], b * 2 + 2)
                    nc.vector.tensor_reduce(gs[:, 0, :], SM[:, :, SMALL - 3:].rearrange("p t c -> p c t"), AX.X, ALU.add)\
                        .then_inc(s["gsum"], 1)
                    nc.vector.tensor_tensor(SQ[:, :, :], SM[:, :, 0:QR_ + KR_], SM[:, :, 0:QR_ + KR_], ALU.mult).then_inc(s["rms"], 1)
                    dve.wait_ge(s["rms"], b * 5 + 1)
                    nc.vector.tensor_reduce(ms[:, 2, 0, :], SQ[:, :, 0:QR_], AX.X, ALU.add).then_inc(s["rms"], 1)
                    nc.vector.tensor_reduce(ms[:, 2, 1, :], SQ[:, :, QR_:], AX.X, ALU.add).then_inc(s["rms"], 1)
                    dve.wait_ge(s["rms"], b * 5 + 3)
                    nc.vector.tensor_scalar(ms[:, 0, 0, :], ms[:, 2, 0, :], 1.0 / QR_, 1e-6, ALU.mult, ALU.add)
                    nc.vector.tensor_scalar(ms[:, 0, 1, :], ms[:, 2, 1, :], 1.0 / KR_, 1e-6, ALU.mult, ALU.add).then_inc(s["rms"], 1)
                    kr = SM[:, :, QR_ + KR_:QR_ + KR_ + VD]
                    nc.vector.tensor_tensor(t1[:, :, :], kr, cosT[:, :, :], ALU.mult)
                    nc.vector.tensor_tensor(t2[:, :, 0:16], kr[:, :, 16:], sinT[:, :, 0:16], ALU.mult)
                    nc.vector.tensor_tensor(t2[:, :, 16:], kr[:, :, 0:16], sinT[:, :, 16:], ALU.mult)
                    dve.wait_ge(s["rms_std"], b + 1)
                    nc.vector.reciprocal(ms[:, 2, :, :], ms[:, 1, :, :]).then_inc(s["rms"], 1)
                    dve.wait_ge(s["rms"], b * 5 + 5)
                    nc.vector.tensor_tensor(t1[:, :, :], t1[:, :, :], t2[:, :, :], ALU.add)
                    nc.vector.tensor_tensor(CK[:, :, KR_ + VD:], SM[:, :, 0:QR_],
                                            ms[:, 2, 0, :, None].broadcast_to([128, NT, QR_]), ALU.mult)
                    nc.vector.tensor_tensor(CK[:, :, 0:KR_], SM[:, :, QR_:QR_ + KR_],
                                            ms[:, 2, 1, :, None].broadcast_to([128, NT, KR_]), ALU.mult).then_inc(s["gate"], 1)
                    dve.wait_ge(s["gate"], b * 5 + 1)
                    nc.vector.tensor_scalar(CK[:, :, KR_:KR_ + VD], t1[:, :, :], 1.0 / H3, None, ALU.mult)
                    nc.vector.tensor_tensor(CK[:, :, KR_ + VD:], CK[:, :, KR_ + VD:],
                                            nw[:, None, 0:QR_].broadcast_to([128, NT, QR_]), ALU.mult)
                    nc.vector.tensor_tensor(CK[:, :, 0:KR_], CK[:, :, 0:KR_],
                                            nw[:, None, QR_:].broadcast_to([128, NT, KR_]), ALU.mult).then_inc(s["latent"], 1)
                    dve.wait_ge(s["gmean"], b + 1)
                    nc.vector.tensor_reduce(gs[:, 1, 0:1], P[6][:, 0:3], AX.X, ALU.max).then_inc(s["gate"], 1)
                    dve.wait_ge(s["gate"], b * 5 + 2)
                    nc.vector.tensor_scalar(gs[:, 2, :], P[6][:, 0:3], gs[:, 1, 0:1], None, ALU.subtract).then_inc(s["gsub"], 1)
                    dve.wait_ge(s["row_copied"], b * 2 + 2)
                    rank_vector(nc, dve, s, b, rk, ident, below, 5)
                    nc.vector.tensor_scalar(rk["rank"][:, :], rk["rank"][:, :], float(KEEP3), None, ALU.is_lt).then_inc(s["sel"], 1)
                    dve.wait_ge(s["gexp"], b + 1)
                    nc.vector.tensor_reduce(gs[:, 4, 0:1], gs[:, 3, :], AX.X, ALU.add).then_inc(s["gate"], 1)
                    dve.wait_ge(s["gate"], b * 5 + 3)
                    nc.vector.reciprocal(gs[:, 4, 1:2], gs[:, 4, 0:1]).then_inc(s["gate"], 1)
                    dve.wait_ge(s["gate"], b * 5 + 4)
                    nc.vector.tensor_scalar(gs[:, 5, :], gs[:, 3, :], gs[:, 4, 1:2], None, ALU.mult).then_inc(s["gate"], 1)
                    dve.wait_ge(s["selt_ready"], b + 1)
                    nc.vector.tensor_copy(cu[:, 0, 8:], P[7][:, NT:2 * NT]).then_inc(s["sel"], 1)
                    for k, sh in enumerate((1, 2, 4)):
                        dve.wait_ge(s["sel"], b * 5 + 2 + k)
                        nc.vector.tensor_tensor(cu[:, (k + 1) % 2, 8:], cu[:, k % 2, 8:], cu[:, k % 2, 8 - sh:8 + NT - sh], ALU.add)\
                            .then_inc(s["sel"], 1)
                    dve.wait_ge(s["sel"], b * 5 + 5)
                    link = dve.wait_ge
                    nc.vector.tensor_tensor(posn[:, :], P[7][:, 0:NT], cu[:, 1, 7:7 + NT], ALU.add).then_inc(s["pos"], 1)
                    link(s["pos"], b * 3 + 1)
                    nc.vector.tensor_tensor(posn[:, :], posn[:, :], rk["rank"][:, :], ALU.mult).then_inc(s["pos"], 1)
                    link(s["pos"], b * 3 + 2)
                    nc.vector.tensor_scalar(posn[:, :], posn[:, :], -1.0, None, ALU.add).then_inc(s["pos"], 1)
                    link(s["pos"], b * 3 + 3)
                    for t in range(NT):
                        ins = nc.vector.tensor_scalar(SEL[:, t, :], iota[:, :], posn[:, t:t + 1], None, ALU.is_equal)
                    ins.then_inc(s["onehot"], 1)
                    with dve.Fori(0, NQ) as g:
                        q = b * NQ + g
                        for a, bs, t in plan:
                            if a is not None:
                                rotate(q, a)
                            for k in bs:
                                kind, x, half = plain[k]
                                if kind == "k1":
                                    dve.wait_ge(s["b_round"], q * nk1 + k + 1)
                                    nc.vector.scalar_tensor_tensor(out=K1[:, x, half * HALF:(half + 1) * HALF],
                                                                   in0=R[:, k % 2, :].bitcast(F32), scalar=lohi[:, 0:1],
                                                                   in1=P[6 + k % 2], op0=ALU.mult, op1=ALU.add)\
                                        .then_inc(s["b_split"], 1)
                            if t is not None:
                                kind, g4 = groups[t]
                                for j in range(2):
                                    u, c = 2 * t + j, (2 * g4 + j) * 128
                                    dve.wait_ge(s["tr_round"], q * 2 * NG + u + 1)
                                    bank = P[2 + u % 4].rearrange("p (h c) -> p h c", h=QUAD)
                                    if kind == "q":
                                        ins = nc.vector.scalar_tensor_tensor(
                                            out=QL[:, :, c:c + 128], in0=bank, scalar=0.125,
                                            in1=QH[:, :, c:c + 128].bitcast(F32), op0=ALU.mult, op1=ALU.subtract)
                                    else:
                                        K = {"w": KW, "s": KS}[kind][:, :, c:c + 128]
                                        ins = nc.vector.scalar_tensor_tensor(out=K, in0=K.bitcast(F32), scalar=lohi[:, 0:1],
                                                                             in1=bank, op0=ALU.mult, op1=ALU.add)
                                    ins.then_inc(s["tr_split"], 1)
                        dve.wait_ge(s["tr_split"], q * 2 * NG + 2 * NG)
                        dve.wait_ge(s["v_copied"], q * 5 + 5)
                        nc.vector.memset(NM[:, 0, 0:1], 0.0).then_inc(s["prepared"], 1)
                        dve.wait_ge(s["prepared"], q + 2)
                        max_full(q, 0)
                        max_short(q, 0)
                        for n, (i, h) in enumerate(units):
                            if n + 1 < NU:
                                max_full(q, n + 1)
                            if h == 2 and i > 0:
                                head_out(q, i - 1)
                            normalise(q, n)
                            if n + 1 < NU:
                                max_short(q, n + 1)
                            if h == 3 and i > 0:
                                residual(q, b, i - 1)
                        head_out(q, NT - 1)
                        residual(q, b, NT - 1)
                        dve.wait_ge(s["added"], q * NT + NT)


def program(nc, d, out, upto=99):
    with ExitStack() as ctx:
        def sb(name, shape, dt=F32):
            return ctx.enter_context(nc.sbuf_tensor(name, shape, dt))

        PS = ctx.enter_context(nc.psum_tensor("PS", [128, 8, HALF], F32))
        P = [PS[:, i, :] for i in range(8)]
        T = sb("T", [128, TT, C])
        ident, lohi = sb("ident", [128, 128]), sb("lohi", [128, 3])
        below, tri = sb("below", [128, 128]), sb("tri", [128, 128])
        maskf = sb("maskf", [128, 3, 128])
        identb, masks = sb("identb", [128, 128], BF16), sb("masks", [128, 3, 128], BF16)
        ld_c, stored, conv_c = [ctx.enter_context(nc.semaphore(n)) for n in ("ld_c", "stored", "conv_c")]
        with nc.Block() as block:
            @block.sync
            def _(sp):
                sp.dma_start(ident[:, :], d["ident"]).then_inc(ld_c, 16)
                sp.dma_start(lohi[:, :], d["lohi"]).then_inc(ld_c, 16)
                sp.dma_start(tri[:, :], d["tri"]).then_inc(ld_c, 16)
                sp.dma_start(below[:, :], d["below"]).then_inc(ld_c, 16)
                sp.dma_start(maskf[:, :, :], d["masks"]).then_inc(ld_c, 16)

            @block.vector
            def _(dve):
                dve.wait_ge(ld_c, 80)
                nc.vector.tensor_copy(identb[:, :], ident[:, :]).then_inc(conv_c, 1)
                nc.vector.tensor_copy(masks[:, :, :], maskf[:, :, :]).then_inc(conv_c, 1)
                dve.wait_ge(conv_c, 2)
        if upto not in (100, 101, 102, 103):
            keep = Semaphores(nc)
            stage_conv(nc, keep, P, T, ident, d)
            keep.release()
        else:
            with nc.Block() as block:
                @block.sync
                def _(sp):
                    sp.dma_start(T[:, :, :], d["T0"]).then_inc(stored, 16)
                    sp.wait_ge(stored, 16)
        if upto in (99, 100):
            keep = Semaphores(nc)
            stage_attn2(nc, keep, PS, P, T, ident, identb, masks[:, 0, :], lohi, d)
            keep.release()
        if upto in (99, 101):
            keep = Semaphores(nc)
            stage_ffn2(nc, keep, PS, P, T, ident, below, d)
            keep.release()
        if upto in (99, 102):
            keep = Semaphores(nc)
            stage_attn3(nc, keep, PS, P, T, ident, identb, masks, lohi, below, tri, d)
            keep.release()
        if upto in (99, 103):
            keep = Semaphores(nc)
            stage_ffn3(nc, keep, PS, P, T, ident, tri, d)
            keep.release()
        with nc.Block() as block:
            @block.sync
            def _(sp):
                sp.dma_start(out, T[:, :, :]).then_inc(stored, 16)
                sp.wait_ge(stored, 16 + 16 * (upto >= 100))


def host_arrays(i):
    a = {k: np.asarray(v) for k, v in i.items()}
    f = np.float32
    m = np.cos((2.0 * np.arange(16)[:, None] + 1.0) * np.arange(4)[None, :] * np.pi / 32.0) / 16.0
    dct = np.einsum("hi,wj->hwij", m, m).reshape(2, 128, 16).transpose(1, 0, 2) / 4.0
    p = np.arange(128)
    lohi = np.zeros((128, 3))
    lohi[p >= 64, 0] = -1.0
    lohi[(p // 32) % 2 == 1, 1] = -1.0
    q, c = p[:, None], p[None, :]
    masks = np.stack([np.where(c <= q, 0.0, -1e30),
                      np.where(c - q > 64, 0.0, -1e30),
                      np.where((c <= q) & (q - c < 64), 0.0, -1e30)], 1)
    wh = lambda w, cols: w.reshape(w.shape[0], H3 // QUAD, QUAD * cols).transpose(1, 0, 2).reshape(-1, QUAD * cols)
    ang = np.outer(np.arange(N, dtype=f), 1.0 / 10000.0 ** (np.arange(0, 32, 2, dtype=f) / 32)).astype(f)
    cos, sin = [x.reshape(NT, 128, 16).transpose(1, 0, 2) for x in (np.cos(ang), np.sin(ang))]
    wk1c = np.zeros((64, QUAD, 2, DH), f)
    wk1c[32:, :, :, 32:] = np.eye(32, dtype=f)[:, None, None, :]
    nope, rope = a["L3_attn_Wq_nope"].reshape(48, H3, 32), a["L3_attn_Wq_rope"].reshape(48, H3, 32)
    return {
        "w_small": np.concatenate([a["L3_attn_Wcq"], a["L3_attn_Wckv"], a["L3_attn_Wk_rope"], a["L3_attn_Wgate"]], 1),
        "w_imp": a["L3_attn_W_imp"],
        "norm_w": np.concatenate([a["L3_attn_q_norm_w"], a["L3_attn_kv_norm_w"]])[None, :],
        "cos": np.concatenate([cos, cos], 2), "sin": np.concatenate([-sin, sin], 2),
        "iota": np.arange(256, dtype=f)[None, :], "w_proj3": a["L3_attn_Wproj"].reshape(4, 128, C).transpose(1, 0, 2),
        "wk1_const": wk1c, "wq3": wh(np.concatenate([nope, rope], 2).reshape(48, H3 * DH), DH),
        "wkw": wh(a["L3_attn_Wwin_k"], DH), "wks": wh(a["L3_attn_Wsel_k"], DH), "wv": wh(a["L3_attn_Wv"], VD),
        "wvw": wh(a["L3_attn_Wwin_v"], VD), "wvs": wh(a["L3_attn_Wsel_v"], VD), "wk1": wh(a["L3_attn_Wk_nope"], 32),
        "below": (c < q).astype(f), "tri": (q <= c).astype(f),
        "gate_w": a["L3_ffn_gate_w"], "gate_b": a["L3_ffn_gate_b"][None, :],
        "ecol": np.arange(E3, 0, -1, dtype=f)[None, :], "eslot": (np.arange(E3, dtype=f) * CAP - 1)[None, :],
        "tok": (SLOTS + np.arange(TT)[None, :] * 128 + p[:, None]).astype(f),
        "w1e": a["L3_ffn_w1"].reshape(E3 * C, F3), "b1e": a["L3_ffn_b1"].reshape(E3, 4, 128).transpose(0, 2, 1).reshape(E3 * 128, 4),
        "w2e": a["L3_ffn_w2"].reshape(E3, 4, 128, C).transpose(0, 2, 1, 3).reshape(E3 * 128, 4 * C),
        "b2e": a["L3_ffn_b2"],
        "wr": a["L2_ffn_wr"], "br": a["L2_ffn_br"][None, :], "w1": a["L2_ffn_w1"],
        "b1": a["L2_ffn_b1"].reshape(4, 128).T, "w2": a["L2_ffn_w2"].reshape(4, 128, C).transpose(1, 0, 2),
        "b2": a["L2_ffn_b2"][None, :],
        "lohi": lohi.astype(f), "masks": masks.astype(f),
        "W_attn": a["L2_attn_W_attn"], "W_proj2": a["L2_attn_W_proj"],
        "x": a["x"].reshape(B, C, N).transpose(1, 0, 2).reshape(C, B * N),
        "pg_w": np.concatenate([a["L0_conv_phi_w"].T, a["L0_conv_g_w"].T], 1),
        "pg_b": np.concatenate([a["L0_conv_phi_b"], a["L0_conv_g_b"]])[None, :],
        "theta_w": a["L0_conv_theta_w"], "theta_b": a["L0_conv_theta_b"][:, None],
        "w_wT": a["L0_conv_w_w"].T,
        "vec": np.stack([a["L0_conv_w_b"], a["L0_conv_gamma"], a["L0_conv_beta"]], 1),
        "experts": a["L1_conv_experts"].transpose(2, 0, 3, 4, 1).reshape(C, 8 * 9 * C),
        "w_f1": a["L1_conv_w_f1"], "b_f1": a["L1_conv_b_f1"][:, None], "w_f2": a["L1_conv_w_f2"],
        "b_f2": a["L1_conv_b_f2"][None, :], "w_r1": a["L1_conv_w_r1"], "b_r1": a["L1_conv_b_r1"][:, None],
        "w_r2": a["L1_conv_w_r2"], "b_r2": a["L1_conv_b_r2"][None, :],
        "ident": np.eye(128, dtype=f), "blk4": np.kron(np.eye(32), np.full((4, 4), 0.25)).astype(f),
        "dct": dct.astype(f),
    }


def kernel(**inputs):
    import numpy as _np
    import concourse.bacc as _bacc
    from concourse import mybir as _mybir
    from concourse.bass_utils import run_bass_kernel_spmd as _run

    nc = _bacc.Bacc("TRN2", target_bir_lowering=False, num_devices=1)
    arrays, aps = {}, {}
    for name, a in host_arrays(inputs).items():
        a = _np.ascontiguousarray(a)
        arrays["in_" + name] = a
        aps[name] = nc.dram_tensor("in_" + name, a.shape, _mybir.dt.from_np(a.dtype), kind="ExternalInput").ap()
    out = nc.dram_tensor("out_tokens", (128, TT, C), F32, kind="ExternalOutput").ap()
    program(nc, aps, out)
    r = _run(nc, [arrays], core_ids=[0])
    got = _np.asarray(r.results[0]["out_tokens"])
    return got.transpose(1, 0, 2).reshape(B, N, C).transpose(0, 2, 1).reshape(B, C, HW, HW)
```

```python
import numpy as np
import concourse.bass as bass
from concourse import mybir
from contextlib import ExitStack

F32 = mybir.dt.float32
F32R = mybir.dt.float32r
BF16 = mybir.dt.bfloat16
U32 = mybir.dt.uint32
ALU = mybir.AluOpType
ACT = mybir.ActivationFunctionType
AX = mybir.AxisListType

B, C, HW, N = 4, 128, 32, 1024
NT = N // 128
TT = B * NT
HALF = 512
CI = 64
E1 = 8
GH = 32
LOW = 16
PADW = HW + 2
TAPS = 9


class Semaphores:

    def __init__(self, nc):
        self.nc, self.stack, self.taken = nc, ExitStack(), []

    def enter_context(self, manager):
        self.taken.append(self.stack.enter_context(manager))
        return self.taken[-1]

    def release(self):
        numbers = sorted(sem.num for sem in self.taken)
        with self.nc.Block() as block:
            @block.gpsimd
            def _(pool):
                start = end = numbers[0]
                for n in numbers + [None]:
                    if n is not None and n <= end:
                        end = n + 1
                        continue
                    pool.sem_clear(range(start, end))
                    start, end = n, (n or 0) + 1
        self.stack.close()


class Chain:

    def __init__(self, eng, sem):
        self.eng, self.sem, self.n = eng, sem, 0

    def __call__(self, ins):
        self.n += 1
        ins.then_inc(self.sem, 1)
        self.eng.wait_ge(self.sem, self.n)


def stage_conv(nc, keep, P, T, ident, d):
    with ExitStack() as ctx:
        def sb(name, shape, dt=F32):
            return ctx.enter_context(nc.sbuf_tensor("c_" + name, shape, dt))

        def sem(name):
            return keep.enter_context(nc.semaphore(name))

        X = sb("X", [C, B * N])
        WY = sb("WY", [C, B * N])
        PG = sb("PG", [C, 2 * CI])
        PGb = sb("PGb", [128, 2 * CI])
        thw = sb("thw", [CI, C])
        thb = sb("thb", [CI, 1])
        wwT = sb("wwT", [CI, C])
        vec = sb("vec", [C, 3])
        PT = sb("PT", [128, NT, 2 * CI])
        KVT = sb("KVT", [CI, CI])
        M = sb("M", [CI, C])
        WE = sb("WE", [C, C])
        be = sb("be", [C, 1])
        st = sb("st", [C, B * 2, 6])
        mv = sb("mv", [C, 2])
        sc = sb("sc", [C, 4])
        gst = sb("gst", [C, B * 2, 6])
        gmv = sb("gmv", [C, B, 2])
        gq = sb("gq", [C, B])
        gg = sb("gg", [C, B, 2])
        gr = sb("gr", [C, B])
        blk4 = sb("blk4", [C, C])
        XP = sb("XP", [C, B, PADW, PADW])
        pr = sb("pr", [C, B, HW // 2, HW])
        pp = sb("pp", [C, B, 256])
        ppT = sb("ppT", [128, 2, B, C])
        dct = sb("dct", [128, 2, LOW])
        fq = sb("fq", [LOW, B * C])
        wf1 = sb("wf1", [LOW, GH])
        bf1 = sb("bf1", [GH, 1])
        h1 = sb("h1", [GH, B * C])
        wf2 = sb("wf2", [GH, 1])
        bf2 = sb("bf2", [C, 1])
        fs = sb("fs", [C, B])
        wr1 = sb("wr1", [C, GH])
        br1 = sb("br1", [GH, 1])
        rh = sb("rh", [GH, B])
        rhb = sb("rhb", [GH, B, C])
        wr2 = sb("wr2", [GH, E1])
        br2 = sb("br2", [C, E1])
        lg = sb("lg", [C, B, E1])
        lm = sb("lm", [C, B])
        EX = sb("EX", [C, E1, TAPS * C])
        KD = sb("KD", [C, 2, TAPS * C])
        XPH, XPL = sb("XPH", [C, B, PADW, PADW], F32R), sb("XPL", [C, B, PADW, PADW], F32R)
        KDH, KDL = sb("KDH", [C, 2, TAPS * C], F32R), sb("KDL", [C, 2, TAPS * C], F32R)

        ld_x = [sem(f"ld_x{b}") for b in range(B)]
        ld_first, ld_w, ld_e, zeroed = sem("ld_first"), sem("ld_w"), sem("ld_e"), sem("zeroed")
        pg_ready, pg_biased = sem("pg_ready"), sem("pg_biased")
        kvt_ready, kvt_copied = sem("kvt_ready"), sem("kvt_copied")
        m_ready, m_copied = sem("m_ready"), sem("m_copied")
        we_ready, we_copied, be_ready = sem("we_ready"), sem("we_copied"), sem("be_ready")
        wy_ready, wy_copied = sem("wy_ready"), sem("wy_copied")
        var_ready, std_ready, bn_scale = sem("var_ready"), sem("std_ready"), sem("bn_scale")
        bn_done, dch = sem("bn_done"), sem("dch")
        gstat, ggrp, gvar, gstd = sem("gstat"), sem("ggrp"), sem("gvar"), sem("gstd")

        nld = 8
        with nc.Block() as block:
            @block.sync
            def _(sp):
                for dst, src in ((PG, d["pg_w"]), (PGb, d["pg_b"].broadcast_to([128, 2 * CI])), (thw, d["theta_w"]),
                                 (thb, d["theta_b"]), (wwT, d["w_wT"]), (vec, d["vec"])):
                    sp.dma_start(dst[:, :], src).then_inc(ld_first, 16)
                for b in range(B):
                    sp.dma_start(X[:, b * N:(b + 1) * N], d["x"][:, b * N:(b + 1) * N]).then_inc(ld_x[b], 16)
                sp.dma_start(EX[:, :, :].rearrange("p e n -> p (e n)"), d["experts"]).then_inc(ld_e, 16)

            @block.scalar
            def _(act):
                for dst, src in ((blk4, d["blk4"]),
                                 (wf1, d["w_f1"]), (bf1, d["b_f1"]), (wf2, d["w_f2"]),
                                 (bf2, d["b_f2"].broadcast_to([128, 1])), (wr1, d["w_r1"]), (br1, d["b_r1"]),
                                 (wr2, d["w_r2"])):
                    act.dma_start(dst[:, :], src).then_inc(ld_w, 16)
                for b in range(B):
                    act.wait_ge(we_ready, b + 1)
                    nc.scalar.activation(WE[:, :], P[4][:, 0:C], ACT.Copy).then_inc(we_copied, 1)
                    act.wait_ge(be_ready, b + 1)
                    for h in range(2):
                        act.wait_ge(wy_ready, 2 * b + h + 1)
                        nc.scalar.activation(WY[:, b * N + h * HALF:b * N + (h + 1) * HALF], P[6 + h][:, :],
                                             ACT.Identity, bias=be[:, 0:1]).then_inc(wy_copied, 1)
                act.wait_ge(var_ready, 1)
                nc.scalar.activation(sc[:, 1:2], sc[:, 0:1], ACT.Sqrt).then_inc(std_ready, 1)
                act.wait_ge(gvar, 1)
                nc.scalar.activation(gr[:, :], gq[:, :], ACT.Sqrt).then_inc(gstd, 1)

            @block.gpsimd
            def _(pool):
                nc.gpsimd.memset(XP[:, :, :, :], 0.0).then_inc(zeroed, 1)

            @block.tensor
            def _(pe):
                pe.wait_ge(ld_first, 16 * 6)
                for b in range(B):
                    pe.wait_ge(ld_x[b], 16)
                    for h in range(2):
                        for t in range(4):
                            k = b * N + (4 * h + t) * 128
                            last = nc.tensor.matmul(P[h][:, t * 128:(t + 1) * 128], X[:, k:k + 128], PG[:, :],
                                                    start=True, stop=True)
                        last.then_inc(pg_ready, 1)
                    pe.wait_ge(pg_biased, 2 * b + 2)
                    for t in range(NT):
                        last = nc.tensor.matmul(P[2][0:CI, 0:CI], PT[:, t, CI:], PT[:, t, 0:CI],
                                                start=(t == 0), stop=(t == NT - 1))
                    last.then_inc(kvt_ready, 1)
                    pe.wait_ge(kvt_copied, b + 1)
                    nc.tensor.matmul(P[3][0:CI, 0:C], KVT[:, :], wwT[:, :], start=True, stop=True).then_inc(m_ready, 1)
                    pe.wait_ge(m_copied, b + 1)
                    nc.tensor.matmul(P[5][:, 0:1], M[:, :], thb[:, :], start=True, stop=True)
                    nc.tensor.matmul(P[4][:, 0:C], thw[:, :], M[:, :], start=True, stop=True).then_inc(we_ready, 1)
                    pe.wait_ge(we_copied, b + 1)
                    for h in range(2):
                        k = b * N + h * HALF
                        nc.tensor.matmul(P[6 + h][:, :], WE[:, :], X[:, k:k + HALF],
                                         start=True, stop=True).then_inc(wy_ready, 1)
                    pe.wait_ge(wy_copied, 2 * b + 2)
                pe.wait_ge(ld_w, 16 * nld)
                pe.wait_ge(gstat, 1)
                nc.tensor.matmul(P[2][:, 0:2 * B], blk4[:, :], gg[:, :, :].rearrange("p b s -> p (b s)"),
                                 start=True, stop=True).then_inc(ggrp, 1)

            @block.vector
            def _(dve):
                link = Chain(dve, dch)
                dve.wait_ge(ld_first, 16 * 6)
                for b in range(B):
                    for h in range(2):
                        dve.wait_ge(pg_ready, 2 * b + h + 1)
                        nc.vector.tensor_tensor(PT[:, 4 * h:4 * h + 4, :],
                                                P[h][:, :].rearrange("p (t n) -> p t n", t=4),
                                                PGb[:, None, :].broadcast_to([128, 4, 2 * CI]), ALU.add)\
                            .then_inc(pg_biased, 1)
                    dve.wait_ge(kvt_ready, b + 1)
                    nc.vector.tensor_copy(KVT[:, :], P[2][0:CI, 0:CI]).then_inc(kvt_copied, 1)
                    dve.wait_ge(m_ready, b + 1)
                    nc.vector.tensor_scalar(M[:, :], P[3][0:CI, 0:C], 1.0 / N, None, ALU.mult).then_inc(m_copied, 1)
                    dve.wait_ge(we_ready, b + 1)
                    nc.vector.tensor_tensor(be[:, :], P[5][:, 0:1], vec[:, 0:1], ALU.add).then_inc(be_ready, 1)
                    for h in range(2):
                        k = b * N + h * HALF
                        dve.wait_ge(wy_copied, 2 * b + h + 1)
                        ins = nc.vector.bn_stats(st[:, 2 * b + h, :], WY[:, k:k + HALF])
                link(ins)
                link(nc.vector.bn_aggr(mv[:, :], st[:, :, :].rearrange("p a s -> p (a s)")))
                nc.vector.tensor_scalar(sc[:, 0:1], mv[:, 1:2], 1e-5, None, ALU.add).then_inc(var_ready, 1)
                dve.wait_ge(std_ready, 1)
                link(nc.vector.reciprocal(sc[:, 2:3], sc[:, 1:2]))
                link(nc.vector.tensor_tensor(sc[:, 0:1], sc[:, 2:3], vec[:, 1:2], ALU.mult))
                link(nc.vector.tensor_tensor(sc[:, 1:2], mv[:, 0:1], sc[:, 0:1], ALU.mult))
                link(nc.vector.tensor_tensor(sc[:, 3:4], vec[:, 2:3], sc[:, 1:2], ALU.subtract))
                for k in range(0, B * N, N):
                    nc.vector.tensor_scalar(WY[:, k:k + N], WY[:, k:k + N], sc[:, 0:1], sc[:, 3:4],
                                            ALU.mult, ALU.add).then_inc(bn_done, 1)
                for i, k in enumerate(range(0, B * N, N)):
                    dve.wait_ge(bn_done, i + 1)
                    nc.vector.tensor_tensor(X[:, k:k + N], X[:, k:k + N], WY[:, k:k + N], ALU.add).then_inc(bn_done, 1)
                dve.wait_ge(bn_done, 2 * B)
                for j in range(2 * B):
                    ins = nc.vector.bn_stats(gst[:, j, :], X[:, j * HALF:(j + 1) * HALF])
                link(ins)
                for b in range(B):
                    ins = nc.vector.bn_aggr(gmv[:, b, :], gst[:, 2 * b:2 * b + 2, :].rearrange("p a s -> p (a s)"))
                link(ins)
                link(nc.vector.tensor_tensor(gq[:, :], gmv[:, :, 0], gmv[:, :, 0], ALU.mult))
                link(nc.vector.tensor_copy(gg[:, :, 0], gmv[:, :, 0]))
                nc.vector.tensor_tensor(gg[:, :, 1], gmv[:, :, 1], gq[:, :], ALU.add).then_inc(gstat, 1)
                dve.wait_ge(ggrp, 1)
                link(nc.vector.tensor_copy(gg[:, :, :].rearrange("p b s -> p (b s)"), P[2][:, 0:2 * B]))
                link(nc.vector.tensor_tensor(gr[:, :], gg[:, :, 0], gg[:, :, 0], ALU.mult))
                link(nc.vector.tensor_tensor(gq[:, :], gg[:, :, 1], gr[:, :], ALU.subtract))
                link(nc.vector.tensor_scalar(gq[:, :], gq[:, :], 1e-5, None, ALU.add))
                nc.vector.tensor_copy(gmv[:, :, 0], gg[:, :, 0]).then_inc(gvar, 1)
                dve.wait_ge(gstd, 1)
                link(nc.vector.reciprocal(gq[:, :], gr[:, :]))
                dve.wait_ge(zeroed, 1)
                for b in range(B):
                    ins = nc.vector.tensor_scalar(XP[:, b, 1:1 + HW, 1:1 + HW],
                                                  X[:, b * N:(b + 1) * N].rearrange("p (h w) -> p h w", h=HW),
                                                  gmv[:, b, 0:1], gq[:, b:b + 1], ALU.subtract, ALU.mult)
                link(ins)

        pooled, pT_ready, pT_copied = sem("pooled"), sem("pT_ready"), sem("pT_copied")
        fq_ready, fq_copied, h1_ready, h1_done = sem("fq_ready"), sem("fq_copied"), sem("h1_ready"), sem("h1_done")
        f_ready, f_done, rh_ready, rh_done = sem("f_ready"), sem("f_done"), sem("rh_ready"), sem("rh_done")
        rhb_done, lg_ready, lsub, lexp = sem("rhb_done"), sem("lg_ready"), sem("lsub"), sem("lexp")
        mixed, conv_ready, conv_added, dch2 = sem("mixed"), sem("conv_ready"), sem("conv_added"), sem("dch2")
        image_high, image_low, kernel_high, kernel_low = sem("image_high"), sem("image_low"), sem("kernel_high"), sem("kernel_low")
        t_ready, t_copied, ld_r = sem("t_ready"), sem("t_copied"), sem("ld_r")

        with nc.Block() as block:
            @block.sync
            def _(sp):
                sp.dma_start(dct[:, :, :], d["dct"]).then_inc(ld_r, 16)
                sp.dma_start(br2[:, :], d["b_r2"].broadcast_to([128, E1])).then_inc(ld_r, 16)

            @block.tensor
            def _(pe):
                for b in range(B):
                    pe.wait_ge(pooled, b + 1)
                    for j in range(2):
                        last = nc.tensor.transpose(P[j][:, b * 128:(b + 1) * 128], pp[:, b, j * 128:(j + 1) * 128],
                                                   ident[:, :])
                last.then_inc(pT_ready, 1)
                pe.wait_ge(pT_copied, 2)
                pe.wait_ge(ld_r, 32)
                for j in range(2):
                    last = nc.tensor.matmul(P[2][0:LOW, :], dct[:, j, :], ppT[:, j, :, :].rearrange("p b c -> p (b c)"),
                                            start=(j == 0), stop=(j == 1))
                last.then_inc(fq_ready, 1)
                pe.wait_ge(fq_copied, 1)
                nc.tensor.matmul(P[3][0:GH, :], wf1[:, :], fq[:, :], start=True, stop=True).then_inc(h1_ready, 1)
                pe.wait_ge(h1_done, 1)
                for b in range(B):
                    last = nc.tensor.matmul(P[4][:, b:b + 1], h1[:, b * C:(b + 1) * C], wf2[:, :], start=True, stop=True)
                last.then_inc(f_ready, 1)
                pe.wait_ge(f_done, 1)
                nc.tensor.matmul(P[5][0:GH, 0:B], wr1[:, :], fs[:, :], start=True, stop=True).then_inc(rh_ready, 1)
                pe.wait_ge(rhb_done, 1)
                for b in range(B):
                    last = nc.tensor.matmul(P[6][:, b * E1:(b + 1) * E1], rhb[:, b, :], wr2[:, :], start=True, stop=True)
                last.then_inc(lg_ready, 1)
                for b in range(B):
                    pe.wait_ge(image_low, b + 1)
                    pe.wait_ge(kernel_low, b + 1)
                    for h in range(2):
                        if b > 1:
                            pe.wait_ge(conv_added, 2 * (b - 2) + h + 1)
                        for tap in range(TAPS):
                            dy, dx = divmod(tap, 3)
                            for part, (kernel, image) in enumerate(((KDH, XPH), (KDH, XPL), (KDL, XPH))):
                                last = nc.tensor.matmul(P[2 * (b % 2) + h][:, :], kernel[:, b % 2, tap * C:(tap + 1) * C],
                                                        image[:, b, 16 * h + dy:16 * h + dy + 16, dx:dx + HW],
                                                        start=(tap == 0 and part == 0), stop=(tap == TAPS - 1 and part == 2))
                        last.then_inc(conv_ready, 1)
                for u in range(2 * B):
                    pe.wait_ge(conv_added, u + 1)
                    if u >= 2:
                        pe.wait_ge(t_copied, u - 1)
                    for t in range(4):
                        k = (4 * u + t) * 128
                        last = nc.tensor.transpose(P[4 + u % 2][:, t * 128:(t + 1) * 128], X[:, k:k + 128], ident[:, :])
                    last.then_inc(t_ready, 1)

            @block.gpsimd
            def _(pool):
                flat = lambda x, b: x[:, b, :, :].rearrange("p h w -> p (h w)")
                for b in range(B):
                    pool.wait_ge(image_high, b + 1)
                    nc.gpsimd.tensor_tensor(flat(XPL, b), flat(XP, b), flat(XPH, b).bitcast(F32), ALU.subtract)\
                        .then_inc(image_low, 1)
                for b in range(B):
                    pool.wait_ge(kernel_high, b + 1)
                    if b >= 2:
                        pool.wait_ge(conv_ready, 2 * (b - 1))
                    nc.gpsimd.tensor_tensor(KDL[:, b % 2, :], KD[:, b % 2, :], KDH[:, b % 2, :].bitcast(F32), ALU.subtract)\
                        .then_inc(kernel_low, 1)

            @block.scalar
            def _(act):
                for b in range(B):
                    nc.scalar.activation(XPH[:, b, :, :], XP[:, b, :, :], ACT.Copy).then_inc(image_high, 1)
                act.wait_ge(pT_ready, 1)
                for j in range(2):
                    nc.scalar.activation(ppT[:, j, :, :].rearrange("p b c -> p (b c)"), P[j][:, :], ACT.Copy)\
                        .then_inc(pT_copied, 1)
                act.wait_ge(fq_ready, 1)
                nc.scalar.activation(fq[:, :], P[2][0:LOW, :], ACT.Copy).then_inc(fq_copied, 1)
                act.wait_ge(h1_ready, 1)
                nc.scalar.activation(h1[:, :], P[3][0:GH, :], ACT.Relu, bias=bf1[:, 0:1]).then_inc(h1_done, 1)
                act.wait_ge(f_ready, 1)
                nc.scalar.activation(fs[:, :], P[4][:, 0:B], ACT.Sigmoid, bias=bf2[:, 0:1]).then_inc(f_done, 1)
                act.wait_ge(rh_ready, 1)
                nc.scalar.activation(rh[:, :], P[5][0:GH, 0:B], ACT.Relu, bias=br1[:, 0:1]).then_inc(rh_done, 1)
                act.wait_ge(lsub, 1)
                nc.scalar.activation(lg[:, :, :], lg[:, :, :], ACT.Exp).then_inc(lexp, 1)
                for b in range(B):
                    act.wait_ge(mixed, b + 1)
                    if b >= 2:
                        act.wait_ge(conv_ready, 2 * (b - 1))
                    nc.scalar.activation(KDH[:, b % 2, :], KD[:, b % 2, :], ACT.Copy).then_inc(kernel_high, 1)
                for u in range(2 * B):
                    act.wait_ge(t_ready, u + 1)
                    nc.scalar.activation(T[:, 4 * u:4 * u + 4, :], P[4 + u % 2][:, :].rearrange("p (t c) -> p t c", t=4),
                                         ACT.Copy).then_inc(t_copied, 1)

            def add_conv(nc, dve, b):
                for h in range(2):
                    k = b * N + h * HALF
                    dve.wait_ge(conv_ready, 2 * b + h + 1)
                    nc.vector.tensor_tensor(X[:, k:k + HALF], X[:, k:k + HALF], P[2 * (b % 2) + h][:, :], ALU.add)\
                        .then_inc(conv_added, 1)

            @block.vector
            def _(dve):
                link = Chain(dve, dch2)
                for b in range(B):
                    link(nc.vector.tensor_tensor(pr[:, b, :, :], XP[:, b, 1:1 + HW:2, 1:1 + HW],
                                                 XP[:, b, 2:2 + HW:2, 1:1 + HW], ALU.add))
                    nc.vector.tensor_tensor(pp[:, b, :].rearrange("p (h w) -> p h w", h=16), pr[:, b, :, 0::2],
                                            pr[:, b, :, 1::2], ALU.add).then_inc(pooled, 1)
                dve.wait_ge(rh_done, 1)
                nc.vector.tensor_copy(rhb[:, :, :], rh[:, :, None].broadcast_to([GH, B, C])).then_inc(rhb_done, 1)
                dve.wait_ge(lg_ready, 1)
                dve.wait_ge(ld_r, 32)
                link(nc.vector.tensor_tensor(lg[:, :, :], P[6][:, 0:B * E1].rearrange("p (b e) -> p b e", b=B),
                                             br2[:, None, :].broadcast_to([C, B, E1]), ALU.add))
                link(nc.vector.tensor_reduce(lm[:, :], lg[:, :, :], AX.X, ALU.max))
                nc.vector.tensor_tensor(lg[:, :, :], lg[:, :, :], lm[:, :, None].broadcast_to([C, B, E1]),
                                        ALU.subtract).then_inc(lsub, 1)
                dve.wait_ge(lexp, 1)
                link(nc.vector.tensor_reduce(lm[:, :], lg[:, :, :], AX.X, ALU.add))
                link(nc.vector.reciprocal(lm[:, :], lm[:, :]))
                link(nc.vector.tensor_tensor(lg[:, :, :], lg[:, :, :], lm[:, :, None].broadcast_to([C, B, E1]), ALU.mult))
                dve.wait_ge(ld_e, 16)
                for b in range(B):
                    if b >= 2:
                        dve.wait_ge(kernel_low, b - 1)
                    link(nc.vector.tensor_scalar(KD[:, b % 2, :], EX[:, 0, :], lg[:, b, 0:1], None, ALU.mult))
                    for e in range(1, E1):
                        ins = nc.vector.scalar_tensor_tensor(out=KD[:, b % 2, :], in0=EX[:, e, :], scalar=lg[:, b, e:e + 1],
                                                             in1=KD[:, b % 2, :], op0=ALU.mult, op1=ALU.add)
                        if e < E1 - 1:
                            link(ins)
                    ins.then_inc(mixed, 1)
                    if b >= 2:
                        add_conv(nc, dve, b - 2)
                add_conv(nc, dve, B - 2)
                add_conv(nc, dve, B - 1)


def norm_vector(nc, dve, s, b, T, XN, ln):
    for t in range(NT):
        ins = nc.vector.bn_stats(ln["st"][:, t, :], T[:, bass.ds(b * NT + t, 1), :].rearrange("p a c -> p (a c)"))
    ins.then_inc(s["ln_stat"], 1)
    st, va, tmp = ln["st"], ln["va"], ln["tmp"]
    dve.wait_ge(s["ln_stat"], b * 3 + 1)
    nc.vector.tensor_tensor(tmp[:, 0, :], st[:, :, 1], st[:, :, 4], ALU.add)
    nc.vector.tensor_tensor(tmp[:, 1, :], st[:, :, 1], st[:, :, 4], ALU.subtract)
    nc.vector.tensor_tensor(tmp[:, 2, :], st[:, :, 2], st[:, :, 5], ALU.add).then_inc(s["ln_stat"], 1)
    dve.wait_ge(s["ln_stat"], b * 3 + 2)
    nc.vector.tensor_scalar(ln["mv"][:, :], tmp[:, 0, :], 0.5, None, ALU.mult)
    nc.vector.scalar_tensor_tensor(out=tmp[:, 3, :], in0=tmp[:, 1, :], scalar=0.25, in1=tmp[:, 1, :],
                                   op0=ALU.mult, op1=ALU.mult)
    nc.vector.tensor_scalar(va[:, :], tmp[:, 2, :], 1.0 / C, 1e-5, ALU.mult, ALU.add).then_inc(s["ln_stat"], 1)
    dve.wait_ge(s["ln_stat"], b * 3 + 3)
    nc.vector.tensor_tensor(va[:, :], va[:, :], tmp[:, 3, :], ALU.add).then_inc(s["ln_var"], 1)
    dve.wait_ge(s["ln_std"], b + 1)
    nc.vector.reciprocal(ln["rs"][:, :], ln["sd"][:, :]).then_inc(s["ln_rs"], 1)
    dve.wait_ge(s["ln_rs"], b + 1)
    for t in range(NT):
        ins = nc.vector.tensor_scalar(XN[:, t, :], T[:, bass.ds(b * NT + t, 1), :].rearrange("p a c -> p (a c)"),
                                      ln["mv"][:, t:t + 1], ln["rs"][:, t:t + 1], ALU.subtract, ALU.mult)
        if t % 4 == 3:
            ins.then_inc(s["ln_done"], 1)


def norm_scalar(nc, act, s, b, P, XC, ln):
    act.wait_ge(s["ln_var"], b + 1)
    nc.scalar.activation(ln["sd"][:, :], ln["va"][:, :], ACT.Sqrt).then_inc(s["ln_std"], 1)
    for h in range(2):
        act.wait_ge(s["xt_ready"], b * 2 + h + 1)
        nc.scalar.activation(XC[:, h * HALF:(h + 1) * HALF], P[h], ACT.Copy).then_inc(s["xc_ready"], 1)


def norm_tensor(nc, pe, s, b, P, XN, ident):
    for h in range(2):
        pe.wait_ge(s["ln_done"], b * 2 + h + 1)
        for t in range(4):
            last = nc.tensor.transpose(P[h][:, t * 128:(t + 1) * 128], XN[:, 4 * h + t, :], ident[:, :])
        last.then_inc(s["xt_ready"], 1)


def norm_tiles(sb):
    return {"st": sb("ln_st", [128, NT, 6]), "mv": sb("ln_mv", [128, NT]), "tmp": sb("ln_tmp", [128, 4, NT]), "va": sb("ln_va", [128, NT]),
            "sd": sb("ln_sd", [128, NT]), "rs": sb("ln_rs_t", [128, NT])}


NORM_SEMS = ("ln_stat", "ln_var", "ln_std", "ln_rs", "ln_done", "xt_ready", "xc_ready")


H2 = 4
D2 = C // H2
UNITS = NT * H2


def stage_attn2(nc, keep, PS, P, T, ident, identb, cmask, lohi, d):
    with ExitStack() as ctx:
        def sb(name, shape, dt=F32):
            return ctx.enter_context(nc.sbuf_tensor("a2_" + name, shape, dt))

        ln = norm_tiles(sb)
        XN = sb("XN", [128, NT, C])
        XC = sb("XC", [C, N])
        WA = sb("WA", [C, 3 * C])
        WR = sb("WR", [C, 2, H2, 4, D2])
        WP = sb("WP", [C, C])
        R = sb("R", [128, 4, HALF], F32R)
        QS = sb("QS", [128, H2, N], F32R)
        KS = sb("KS", [128, H2, N], F32R)
        V = sb("V", [128, NT, C])
        NM = sb("NM", [128, 2])
        L = sb("L", [128, 2])
        RL = sb("RL", [128, 2])
        PR = sb("PR", [128, 3, N])
        PT = sb("PT", [128, 2, H2, N])
        YT = sb("YT", [C, N])
        names = NORM_SEMS + ("ld", "wr_ready", "qk_ready", "qk_round", "qk_split", "v_ready", "v_copied",
                             "score_ready", "max_ready", "exp_done", "rl_ready", "prob_ready", "pt_ready", "pt_copied",
                             "pv_ready", "yt_copied", "proj_ready", "added")
        s = {n: keep.enter_context(nc.semaphore("a2_" + n)) for n in names}
        job_bank = lambda k: P[(2, 3, 6, 7)[k % 4]]
        jobs = [(w, h, half) for w in range(2) for h in range(H2) for half in range(2)]
        units = [(i, h) for i in range(NT) for h in range(H2)]
        width = lambda i: (i + 1) * 128
        banks = []
        first_bank = []
        for n, (i, h) in enumerate(units):
            first_bank.append(len(banks))
            banks += [(n, j, min(4, i + 1 - j)) for j in range(0, i + 1, 4)]
        first_bank.append(len(banks))
        NB = len(banks)
        slot = lambda n: PS[:, 2 * (n % 2):2 * (n % 2) + 2, :].rearrange("p a n -> p (a n)")

        with nc.Block() as block:
            @block.sync
            def _(sp):
                sp.dma_start(WA[:, :], d["W_attn"]).then_inc(s["ld"], 16)
                sp.dma_start(WP[:, :], d["W_proj2"]).then_inc(s["ld"], 16)

            @block.tensor
            def _(pe):
                def scores(b, n):
                    i, h = units[n]
                    if n >= 2:
                        pe.wait_ge(s["exp_done"], b * UNITS + n - 1)
                    S = slot(n)
                    w = width(i)
                    for c0 in range(0, w, HALF):
                        c1 = min(w, c0 + HALF)
                        diag = c1 == w
                        last = nc.tensor.matmul(S[:, c0:c1], QS[:, h, i * 128:(i + 1) * 128], KS[:, h, c0:c1],
                                                start=True, stop=not diag)
                    last = nc.tensor.matmul(S[:, w - 128:w], identb[:, :], cmask[:, :], start=False, stop=True)
                    last.then_inc(s["score_ready"], 1)

                def transposes(b, n):
                    i, h = units[n]
                    pe.wait_ge(s["prob_ready"], b * UNITS + n + 1)
                    for k in range(first_bank[n], first_bank[n + 1]):
                        if k >= 2:
                            pe.wait_ge(s["pt_copied"], b * NB + k - 1)
                        _, j0, m = banks[k]
                        for j in range(m):
                            last = nc.tensor.transpose(P[4 + k % 2][:, j * 128:(j + 1) * 128],
                                                       PR[:, n % 3, (j0 + j) * 128:(j0 + j + 1) * 128], ident[:, :])
                        last.then_inc(s["pt_ready"], 1)

                def values(b, i):
                    pe.wait_ge(s["pt_copied"], b * NB + first_bank[H2 * (i + 1)])
                    if i >= 2:
                        pe.wait_ge(s["added"], b * NT + i - 1)
                    for j in range(i + 1):
                        for h in range(H2):
                            last = nc.tensor.matmul(P[6 + i % 2][h * D2:(h + 1) * D2, 0:128],
                                                    V[:, j, h * D2:(h + 1) * D2], PT[:, i % 2, h, j * 128:(j + 1) * 128],
                                                    start=(j == 0), stop=(j == i))
                    last.then_inc(s["pv_ready"], 1)

                def project(b, i):
                    pe.wait_ge(s["yt_copied"], b * NT + i + 1)
                    nc.tensor.matmul(P[6 + i % 2][:, 128:256], YT[:, i * 128:(i + 1) * 128], WP[:, :],
                                     start=True, stop=True).then_inc(s["proj_ready"], 1)

                pe.wait_ge(s["wr_ready"], 1)
                with pe.Fori(0, B) as b:
                    norm_tensor(nc, pe, s, b, P, XN, ident)
                    pe.wait_ge(s["xc_ready"], b * 2 + 2)
                    for k, (w, h, half) in enumerate(jobs):
                        if k >= 4:
                            pe.wait_ge(s["qk_split"], b * 16 + k - 3)
                        nc.tensor.matmul(job_bank(k), WR[:, w, h, :, :].rearrange("p r c -> p (r c)"),
                                         XC[:, half * HALF:(half + 1) * HALF], start=True, stop=True)\
                            .then_inc(s["qk_ready"], 1)
                    for half in range(2):
                        for t in range(4):
                            k = (4 * half + t) * 128
                            last = nc.tensor.matmul(P[4 + half][:, t * 128:(t + 1) * 128], XC[:, k:k + 128],
                                                    WA[:, 2 * C:], start=True, stop=True)
                        last.then_inc(s["v_ready"], 1)
                    pe.wait_ge(s["qk_split"], b * 16 + 16)
                    pe.wait_ge(s["v_copied"], b * 2 + 2)
                    scores(b, 0)
                    for n, (i, h) in enumerate(units):
                        if n + 1 < UNITS:
                            scores(b, n + 1)
                        if n >= 2:
                            transposes(b, n - 2)
                        if h == 2 and i > 0:
                            values(b, i - 1)
                        if h == 3 and i > 0:
                            project(b, i - 1)
                    transposes(b, UNITS - 2)
                    transposes(b, UNITS - 1)
                    values(b, NT - 1)
                    project(b, NT - 1)

            @block.scalar
            def _(act):
                def copy_banks(b, n):
                    i, h = units[n]
                    if h == 0 and i >= 2:
                        act.wait_ge(s["pv_ready"], b * NT + i - 1)
                    for k in range(first_bank[n], first_bank[n + 1]):
                        _, j0, m = banks[k]
                        act.wait_ge(s["pt_ready"], b * NB + k + 1)
                        nc.scalar.activation(PT[:, i % 2, h, j0 * 128:(j0 + m) * 128], P[4 + k % 2][:, 0:m * 128],
                                             ACT.Copy).then_inc(s["pt_copied"], 1)

                with act.Fori(0, B) as b:
                    norm_scalar(nc, act, s, b, P, XC, ln)
                    for k, (w, h, half) in enumerate(jobs):
                        act.wait_ge(s["qk_ready"], b * 16 + k + 1)
                        if k >= 4:
                            act.wait_ge(s["qk_split"], b * 16 + k - 3)
                        nc.scalar.activation(R[:, k % 4, :], job_bank(k), ACT.Copy).then_inc(s["qk_round"], 1)
                    for half in range(2):
                        act.wait_ge(s["v_ready"], b * 2 + half + 1)
                        nc.scalar.activation(V[:, 4 * half:4 * half + 4, :], P[4 + half].rearrange("p (t c) -> p t c", t=4),
                                             ACT.Copy).then_inc(s["v_copied"], 1)
                    for n, (i, h) in enumerate(units):
                        act.wait_ge(s["max_ready"], b * UNITS + n + 1)
                        if n >= 3:
                            act.wait_ge(s["pt_ready"], b * NB + first_bank[n - 2])
                        nc.scalar.activation(PR[:, n % 3, 0:width(i)], slot(n)[:, 0:width(i)], ACT.Exp,
                                             bias=NM[:, n % 2:n % 2 + 1], accum_out=L[:, n % 2:n % 2 + 1])\
                            .then_inc(s["exp_done"], 1)
                        if n >= 2:
                            copy_banks(b, n - 2)
                    copy_banks(b, UNITS - 2)
                    copy_banks(b, UNITS - 1)

            @block.vector
            def _(dve):
                def row_max(b, n):
                    dve.wait_ge(s["score_ready"], b * UNITS + n + 1)
                    if n >= 2:
                        dve.wait_ge(s["exp_done"], b * UNITS + n - 1)
                    nc.vector.tensor_reduce(NM[:, n % 2:n % 2 + 1], slot(n)[:, 0:width(units[n][0])], AX.X, ALU.max,
                                            negate=True).then_inc(s["max_ready"], 1)

                def normalise(b, n):
                    i, h = units[n]
                    dve.wait_ge(s["exp_done"], b * UNITS + n + 1)
                    nc.vector.reciprocal(RL[:, n % 2:n % 2 + 1], L[:, n % 2:n % 2 + 1]).then_inc(s["rl_ready"], 1)
                    dve.wait_ge(s["rl_ready"], b * UNITS + n + 1)
                    nc.vector.tensor_scalar(PR[:, n % 3, 0:width(i)], PR[:, n % 3, 0:width(i)], RL[:, n % 2:n % 2 + 1],
                                            None, ALU.mult).then_inc(s["prob_ready"], 1)

                def head_out(b, i):
                    dve.wait_ge(s["pv_ready"], b * NT + i + 1)
                    nc.vector.tensor_copy(YT[:, i * 128:(i + 1) * 128], P[6 + i % 2][:, 0:128]).then_inc(s["yt_copied"], 1)

                def residual(b, i):
                    dve.wait_ge(s["proj_ready"], b * NT + i + 1)
                    t = T[:, bass.ds(b * NT + i, 1), :].rearrange("p a c -> p (a c)")
                    nc.vector.tensor_tensor(t, t, P[6 + i % 2][:, 128:256], ALU.add).then_inc(s["added"], 1)

                dve.wait_ge(s["ld"], 32)
                for w in range(2):
                    for r in range(4):
                        ins = nc.vector.tensor_scalar(WR[:, w, :, r, :],
                                                      WA[:, w * C:(w + 1) * C].rearrange("p (h c) -> p h c", h=H2),
                                                      1.0 if w else float(1.0 / np.sqrt(np.float32(D2))), None, ALU.mult)
                ins.then_inc(s["wr_ready"], 1)
                with dve.Fori(0, B) as b:
                    norm_vector(nc, dve, s, b, T, XN, ln)
                    for k, (w, h, half) in enumerate(jobs):
                        dve.wait_ge(s["qk_round"], b * 16 + k + 1)
                        nc.vector.scalar_tensor_tensor(out=(QS, KS)[w][:, h, half * HALF:(half + 1) * HALF],
                                                       in0=R[:, k % 4, :].bitcast(F32), scalar=lohi[:, w:w + 1],
                                                       in1=job_bank(k), op0=ALU.mult, op1=ALU.add)\
                            .then_inc(s["qk_split"], 1)
                    row_max(b, 0)
                    for n, (i, h) in enumerate(units):
                        if n + 1 < UNITS:
                            row_max(b, n + 1)
                        if h == 3 and i > 0:
                            head_out(b, i - 1)
                        normalise(b, n)
                        if h == 0 and i > 1:
                            residual(b, i - 2)
                    residual(b, NT - 2)
                    head_out(b, NT - 1)
                    residual(b, NT - 1)
                    dve.wait_ge(s["added"], b * NT + NT)


F = 4 * C
KEEP2 = N // 2 - 1


def rank_tiles(sb):
    return {"row": sb("rk_row", [128, N]), "ex": sb("rk_ex", [128, NT, 128]), "col": sb("rk_col", [128, NT]),
            "cnt": sb("rk_cnt", [128, 3, NT]), "junk": sb("rk_junk", [128, NT, N + 128], BF16), "rank": sb("rk_rank", [128, NT])}


def rank_vector(nc, dve, s, b, rk, ident, below, steps):
    row, col, cnt, junk = rk["row"], rk["col"], rk["cnt"], rk["junk"]
    nc.vector.tensor_tensor(rk["ex"][:, :, :], row[:, :].rearrange("p (t c) -> p t c", t=NT),
                            ident[:, None, :].broadcast_to([128, NT, 128]), ALU.mult).then_inc(s["rk"], 1)
    dve.wait_ge(s["rk"], b * steps + 1)
    nc.vector.tensor_reduce(col[:, :], rk["ex"][:, :, :], AX.X, ALU.add).then_inc(s["rk"], 1)
    dve.wait_ge(s["rk"], b * steps + 2)
    for t in range(NT):
        c = col[:, t:t + 1]
        if t:
            nc.vector.tensor_scalar(junk[:, t, 0:128 * t], row[:, 0:128 * t], c, 0.0, ALU.is_ge, ALU.add,
                                    accum_out=cnt[:, 0, t:t + 1])
        nc.vector.tensor_scalar(junk[:, t, 128 * t:N], row[:, 128 * t:N], c, 0.0, ALU.is_gt, ALU.add,
                                accum_out=cnt[:, 1, t:t + 1])
        ins = nc.vector.scalar_tensor_tensor(out=junk[:, t, N:], in0=row[:, 128 * t:128 * t + 128], scalar=c,
                                             in1=below[:, :], op0=ALU.is_equal, op1=ALU.mult,
                                             accum_out=cnt[:, 2, t:t + 1])
    ins.then_inc(s["rk"], 1)
    dve.wait_ge(s["rk"], b * steps + 3)
    nc.vector.tensor_tensor(rk["rank"][:, :], cnt[:, 0, :], cnt[:, 1, :], ALU.add).then_inc(s["rk"], 1)
    dve.wait_ge(s["rk"], b * steps + 4)
    nc.vector.tensor_tensor(rk["rank"][:, :], rk["rank"][:, :], cnt[:, 2, :], ALU.add).then_inc(s["rk"], 1)
    dve.wait_ge(s["rk"], b * steps + 5)


def stage_ffn2(nc, keep, PS, P, T, ident, below, d):
    with ExitStack() as ctx:
        def sb(name, shape, dt=F32):
            return ctx.enter_context(nc.sbuf_tensor("f2_" + name, shape, dt))

        ln, rk = norm_tiles(sb), rank_tiles(sb)
        XN = sb("XN", [128, NT, C])
        XC = sb("XC", [C, N])
        wr = sb("wr", [C, 1])
        wrr = sb("wrr", [C, 128])
        br = sb("br", [128, 1])
        w1 = sb("w1", [C, F])
        b1 = sb("b1", [128, 4])
        w2 = sb("w2", [128, 4, C])
        b2 = sb("b2", [128, C])
        H = sb("H", [128, 4, N])
        Y = sb("Y", [128, NT, C])
        gate = sb("gate", [128, NT])
        names = NORM_SEMS + ("ld", "wrr_ready", "row_ready", "row_copied", "rk", "gated", "h_ready", "h_done",
                             "y_ready", "y_scaled", "t_plus_x", "t_done")
        s = {n: keep.enter_context(nc.semaphore("f2_" + n)) for n in names}
        jobs = [(m, half) for half in range(2) for m in range(4)]
        with nc.Block() as block:
            @block.sync
            def _(sp):
                for dst, src in ((wr[:, :], d["wr"]), (br[:, :], d["br"].broadcast_to([128, 1])), (w1[:, :], d["w1"]),
                                 (b1[:, :], d["b1"]), (w2[:, :, :], d["w2"]), (b2[:, :], d["b2"].broadcast_to([128, C]))):
                    sp.dma_start(dst, src).then_inc(s["ld"], 16)

            @block.tensor
            def _(pe):
                pe.wait_ge(s["ld"], 96)
                pe.wait_ge(s["wrr_ready"], 1)
                with pe.Fori(0, B) as b:
                    norm_tensor(nc, pe, s, b, P, XN, ident)
                    pe.wait_ge(s["xc_ready"], b * 2 + 2)
                    for h in range(2):
                        nc.tensor.matmul(P[2 + h], wrr[:, :], XC[:, h * HALF:(h + 1) * HALF], start=True, stop=True)\
                            .then_inc(s["row_ready"], 1)
                    for k, (m, half) in enumerate(jobs):
                        if k >= 2:
                            pe.wait_ge(s["h_done"], b * 8 + k - 1)
                        nc.tensor.matmul(P[4 + k % 2], w1[:, m * 128:(m + 1) * 128], XC[:, half * HALF:(half + 1) * HALF],
                                         start=True, stop=True).then_inc(s["h_ready"], 1)
                    for g in range(2):
                        pe.wait_ge(s["h_done"], b * 8 + 4 * g + 4)
                        for t in range(4):
                            for m in range(4):
                                k = (4 * g + t) * 128
                                last = nc.tensor.matmul(P[6 + g][:, t * 128:(t + 1) * 128], H[:, m, k:k + 128],
                                                        w2[:, m, :], start=(m == 0), stop=(m == 3))
                        last.then_inc(s["y_ready"], 1)

            @block.scalar
            def _(act):
                with act.Fori(0, B) as b:
                    norm_scalar(nc, act, s, b, P, XC, ln)
                    for h in range(2):
                        act.wait_ge(s["row_ready"], b * 2 + h + 1)
                        nc.scalar.activation(rk["row"][:, h * HALF:(h + 1) * HALF], P[2 + h], ACT.Identity,
                                             bias=br[:, 0:1]).then_inc(s["row_copied"], 1)
                    for k, (m, half) in enumerate(jobs):
                        act.wait_ge(s["h_ready"], b * 8 + k + 1)
                        nc.scalar.activation(H[:, m, half * HALF:(half + 1) * HALF], P[4 + k % 2], ACT.Gelu_apprx_tanh,
                                             bias=b1[:, m:m + 1]).then_inc(s["h_done"], 1)

            @block.gpsimd
            def _(pool):
                with pool.Fori(0, B) as b:
                    for g in range(2):
                        pool.wait_ge(s["ln_done"], b * 2 + g + 1)
                        t = T[:, bass.ds(b * NT + 4 * g, 4), :]
                        nc.gpsimd.tensor_tensor(t, t, XN[:, 4 * g:4 * g + 4, :], ALU.add).then_inc(s["t_plus_x"], 1)

            @block.vector
            def _(dve):
                dve.wait_ge(s["ld"], 96)
                nc.vector.memset(rk["cnt"][:, 0, 0:1], 0.0)
                nc.vector.tensor_copy(wrr[:, :], wr[:, 0:1].broadcast_to([C, 128])).then_inc(s["wrr_ready"], 1)
                with dve.Fori(0, B) as b:
                    norm_vector(nc, dve, s, b, T, XN, ln)
                    dve.wait_ge(s["row_copied"], b * 2 + 2)
                    rank_vector(nc, dve, s, b, rk, ident, below, 6)
                    nc.vector.tensor_scalar(rk["rank"][:, :], rk["rank"][:, :], float(KEEP2), None, ALU.is_lt)\
                        .then_inc(s["rk"], 1)
                    dve.wait_ge(s["rk"], b * 6 + 6)
                    nc.vector.tensor_tensor(gate[:, :], rk["rank"][:, :], rk["col"][:, :], ALU.mult).then_inc(s["gated"], 1)
                    dve.wait_ge(s["gated"], b + 1)
                    for g in range(2):
                        y = Y[:, 4 * g:4 * g + 4, :]
                        dve.wait_ge(s["y_ready"], b * 2 + g + 1)
                        nc.vector.tensor_tensor(y, P[6 + g].rearrange("p (t c) -> p t c", t=4),
                                                b2[:, None, :].broadcast_to([128, 4, C]), ALU.add).then_inc(s["y_scaled"], 1)
                    for g in range(2):
                        y = Y[:, 4 * g:4 * g + 4, :]
                        dve.wait_ge(s["y_scaled"], b * 4 + g + 1)
                        nc.vector.tensor_tensor(y, y, gate[:, 4 * g:4 * g + 4, None].broadcast_to([128, 4, C]), ALU.mult)\
                            .then_inc(s["y_scaled"], 1)
                    dve.wait_ge(s["t_plus_x"], b * 2 + 2)
                    for g in range(2):
                        dve.wait_ge(s["y_scaled"], b * 4 + g + 3)
                        t = T[:, bass.ds(b * NT + 4 * g, 4), :]
                        nc.vector.tensor_tensor(t, t, Y[:, 4 * g:4 * g + 4, :], ALU.add).then_inc(s["t_done"], 1)


E3 = 8
CAP = -(-5 * B * N // (4 * E3))
SLOTS = E3 * CAP
CT = CAP // 128
F3 = 4 * C


def stage_ffn3(nc, keep, PS, P, T, ident, upto_tri, d, out, stored):
    with ExitStack() as ctx:
        def sb(name, shape, dt=F32):
            return ctx.enter_context(nc.sbuf_tensor("f3_" + name, shape, dt))

        buf = nc.dram_tensor("slots_in", [SLOTS + B * N, C], F32, kind="Internal").ap()
        ybuf = nc.dram_tensor("slots_out", [SLOTS, C], F32, kind="Internal").ap()
        ln = norm_tiles(sb)
        XN = sb("XN", [128, NT, C])
        XA = sb("XA", [128, TT, C])
        XC = sb("XC", [C, N])
        ZR = sb("ZR", [128, 8 * C])
        gw = sb("gw", [C, E3])
        gb = sb("gb", [128, E3])
        LG = sb("LG", [128, TT, E3])
        A1, A2 = sb("A1", [128, TT, E3]), sb("A2", [128, TT, E3])
        OH = sb("OH", [128, TT, E3])
        RX = sb("RX", [128, 8, TT])
        CU = sb("CU", [128, 2, TT + 16, E3])
        ecol, eslot = sb("ecol", [128, E3]), sb("eslot", [128, E3])
        ones = sb("ones", [128, 128])
        SC, SG = sb("SC", [128, TT], U32), sb("SG", [128, TT], U32)
        tok = sb("tok", [128, TT])
        W1 = sb("W1", [C, 2, F3])
        B1 = sb("B1", [128, 2, 4])
        W2 = sb("W2", [128, 2, 4, C])
        B2 = sb("B2", [128, 2, C])
        XB = sb("XB", [128, 2, CT, C])
        XT = sb("XT", [C, 2, CAP])
        H = sb("H", [128, 2, 4, CAP])
        YB = sb("YB", [128, 2, CT, C])
        YG = sb("YG", [128, TT, C])
        bad = sb("bad", [128, 8, C], U32)
        clamp = sb("clamp", [128, 3, 8 * C])
        names = NORM_SEMS + ("ld", "zero", "zeroed", "kept_x", "lg_ready", "lg_copied", "st", "sub", "exp", "tri_ready",
                             "scattered", "slot_ready", "xt3_ready", "xt3_copied", "h_ready", "h_done",
                             "y_ready", "y_done", "fin", "cl")
        s = {n: keep.enter_context(nc.semaphore("f3_" + n)) for n in names}

        with nc.Block() as block:
            @block.sync
            def _(sp):
                for dst, src in ((gw[:, :], d["gate_w"]), (gb[:, :], d["gate_b"].broadcast_to([128, E3])),
                                 (ecol[:, :], d["ecol"].broadcast_to([128, E3])),
                                 (eslot[:, :], d["eslot"].broadcast_to([128, E3])),
                                 (tok[:, :], d["tok"])):
                    sp.dma_start(dst, src).then_inc(s["ld"], 16)
                sp.wait_ge(s["zero"], 1)
                for k in range(CT):
                    sp.dma_start(buf[k * 8 * 128:(k + 1) * 8 * 128, :].rearrange("(p r) c -> p (r c)", r=8), ZR[:, :])\
                        .then_inc(s["zeroed"], 16)

            @block.gpsimd
            def _(pool):
                nc.gpsimd.memset(ZR[:, :], 0.0).then_inc(s["zero"], 1)
                nc.gpsimd.memset(ones[:, :], 1.0)
                nc.gpsimd.memset(CU[:, :, 0:16, :], 0.0).then_inc(s["zero"], 1)
                pool.wait_ge(s["zeroed"], 16 * CT)
                pool.wait_ge(s["kept_x"], 2 * B)
                pool.wait_ge(s["slot_ready"], 1)
                for t in range(TT):
                    nc.gpsimd.indirect_dma_start(out=buf, out_offset=bass.IndirectOffsetOnAxis(ap=SC[:, t:t + 1], axis=0),
                                                 in_=XA[:, t, :], in_offset=None).then_inc(s["scattered"], 16)
                pool.wait_ge(s["scattered"], 16 * TT)

            @block.tensor
            def _(pe):
                pe.wait_ge(s["ld"], 80)
                with pe.Fori(0, B) as b:
                    norm_tensor(nc, pe, s, b, P, XN, ident)
                    pe.wait_ge(s["xc_ready"], b * 2 + 2)
                    for t in range(NT):
                        last = nc.tensor.matmul(P[2][:, t * E3:(t + 1) * E3], XC[:, t * 128:(t + 1) * 128], gw[:, :],
                                                start=True, stop=True)
                    last.then_inc(s["lg_ready"], 1)
                pe.wait_ge(s["st"], 6)
                pe.wait_ge(s["zero"], 2)
                oh = OH[:, :, :].rearrange("p t e -> p (t e)")
                nc.tensor.matmul(P[3][:, 0:TT * E3], upto_tri[:, :], oh, start=True, stop=True)
                nc.tensor.matmul(P[4][:, 0:TT * E3], ones[:, :], oh, start=True, stop=True).then_inc(s["tri_ready"], 1)

            @block.scalar
            def _(act):
                with act.Fori(0, B) as b:
                    norm_scalar(nc, act, s, b, P, XC, ln)
                    for g in range(2):
                        act.wait_ge(s["ln_done"], b * 2 + g + 1)
                        nc.scalar.activation(XA[:, bass.ds(b * NT + 4 * g, 4), :], XN[:, 4 * g:4 * g + 4, :], ACT.Copy)\
                            .then_inc(s["kept_x"], 1)
                act.wait_ge(s["st"], 1)
                nc.scalar.activation(A1[:, :, :], LG[:, :, :], ACT.Exp).then_inc(s["exp"], 1)

            @block.vector
            def _(dve):
                dve.wait_ge(s["ld"], 80)
                with dve.Fori(0, B) as b:
                    norm_vector(nc, dve, s, b, T, XN, ln)
                    dve.wait_ge(s["lg_ready"], b + 1)
                    nc.vector.tensor_tensor(LG[:, bass.ds(b * NT, NT), :], P[2][:, 0:NT * E3].rearrange("p (t e) -> p t e", e=E3),
                                            gb[:, None, :].broadcast_to([128, NT, E3]), ALU.add).then_inc(s["lg_copied"], 1)
                    dve.wait_ge(s["kept_x"], b * 2 + 2)
                link = Chain(dve, s["sub"])
                bc = lambda a: a[:, :, None].broadcast_to([128, TT, E3])
                dve.wait_ge(s["lg_copied"], B)
                link(nc.vector.tensor_reduce(RX[:, 0, :], LG[:, :, :], AX.X, ALU.max))
                nc.vector.tensor_tensor(LG[:, :, :], LG[:, :, :], bc(RX[:, 0, :]), ALU.subtract).then_inc(s["st"], 1)
                dve.wait_ge(s["exp"], 1)
                nc.vector.tensor_reduce(RX[:, 1, :], A1[:, :, :], AX.X, ALU.add).then_inc(s["st"], 1)
                nc.vector.tensor_reduce(RX[:, 0, :], A1[:, :, :], AX.X, ALU.max).then_inc(s["st"], 1)
                dve.wait_ge(s["st"], 3)
                nc.vector.reciprocal(RX[:, 2, :], RX[:, 1, :])
                link(nc.vector.tensor_tensor(A2[:, :, :], A1[:, :, :], bc(RX[:, 0, :]), ALU.is_ge))
                nc.vector.tensor_tensor(A2[:, :, :], A2[:, :, :], ecol[:, None, :].broadcast_to([128, TT, E3]), ALU.mult)\
                    .then_inc(s["st"], 1)
                dve.wait_ge(s["st"], 4)
                nc.vector.tensor_reduce(RX[:, 3, :], A2[:, :, :], AX.X, ALU.max).then_inc(s["st"], 1)
                dve.wait_ge(s["st"], 5)
                nc.vector.tensor_tensor(OH[:, :, :], A2[:, :, :], bc(RX[:, 3, :]), ALU.is_ge).then_inc(s["st"], 1)
                dve.wait_ge(s["tri_ready"], 1)
                dve.wait_ge(s["zero"], 2)
                n4 = P[4][:, 0:TT * E3].rearrange("p (t e) -> p t e", e=E3)
                link(nc.vector.tensor_copy(CU[:, 0, 16:, :], n4))
                for k, sh in enumerate((1, 2, 4, 8, 16)):
                    a, z = k % 2, (k + 1) % 2
                    link(nc.vector.tensor_tensor(CU[:, z, 16:, :], CU[:, a, 16:, :], CU[:, a, 16 - sh:16 + TT - sh, :], ALU.add))
                link(nc.vector.tensor_tensor(A1[:, :, :], P[3][:, 0:TT * E3].rearrange("p (t e) -> p t e", e=E3),
                                             CU[:, 1, 15:15 + TT, :], ALU.add))
                link(nc.vector.tensor_tensor(A1[:, :, :], A1[:, :, :], OH[:, :, :], ALU.mult))
                link(nc.vector.tensor_reduce(RX[:, 3, :], A1[:, :, :], AX.X, ALU.add))
                link(nc.vector.tensor_tensor(A2[:, :, :], OH[:, :, :], eslot[:, None, :].broadcast_to([128, TT, E3]), ALU.mult))
                link(nc.vector.tensor_reduce(RX[:, 4, :], A2[:, :, :], AX.X, ALU.add))
                link(nc.vector.tensor_scalar(RX[:, 5, :], RX[:, 3, :], float(CAP), None, ALU.is_le))
                link(nc.vector.tensor_scalar(RX[:, 6, :], RX[:, 3, :], float(CAP), None, ALU.min))
                link(nc.vector.tensor_tensor(RX[:, 6, :], RX[:, 6, :], RX[:, 4, :], ALU.add))
                link(nc.vector.tensor_copy(SG[:, :], RX[:, 6, :]))
                link(nc.vector.tensor_tensor(RX[:, 6, :], RX[:, 6, :], tok[:, :], ALU.subtract))
                link(nc.vector.tensor_tensor(RX[:, 6, :], RX[:, 6, :], RX[:, 5, :], ALU.mult))
                link(nc.vector.tensor_tensor(RX[:, 6, :], RX[:, 6, :], tok[:, :], ALU.add))
                link(nc.vector.tensor_tensor(RX[:, 7, :], RX[:, 5, :], RX[:, 2, :], ALU.mult))
                nc.vector.tensor_copy(SC[:, :], RX[:, 6, :]).then_inc(s["slot_ready"], 1)

        w_ld, x_ld, y_stored = [[keep.enter_context(nc.semaphore(f"f3_{n}{k}")) for k in range(2)]
                                for n in ("w_ld", "x_ld", "y_stored")]
        gathered = [keep.enter_context(nc.semaphore(f"f3_gathered{k}")) for k in range(TT // 8)]
        sub = 2
        cols = CAP // sub
        with nc.Block() as block:
            @block.sync
            def _(sp):
                for t in range(0, TT, 8):
                    sp.wait_ge(s["fin"], t + 8)
                    sp.dma_start(out[:, t:t + 8, :], T[:, t:t + 8, :]).then_inc(stored, 16)
                sp.wait_ge(stored, 16 * TT // 8)

            @block.gpsimd
            def _(pool):
                def load_weights(e, k):
                    for dst, src in ((W1[:, k, :], d["w1e"][bass.ds(e * C, C), :]),
                                     (W2[:, k, :, :].rearrange("p m c -> p (m c)"), d["w2e"][bass.ds(e * 128, 128), :]),
                                     (B1[:, k, :], d["b1e"][bass.ds(e * 128, 128), :]),
                                     (B2[:, k, :], d["b2e"][bass.ds(e, 1), :].broadcast_to([128, C]))):
                        pool.dma_start(dst, src).then_inc(w_ld[k], 16)

                def load_tokens(e, k):
                    pool.dma_start(XB[:, k, :, :], buf[bass.ds(e * CAP, CAP), :].rearrange("(t p) c -> p t c", p=128))\
                        .then_inc(x_ld[k], 16)

                for k in range(2):
                    load_tokens(k, k)
                    load_weights(k, k)
                with pool.Fori(0, E3 // 2 - 1) as h:
                    for k in range(2):
                        pool.wait_ge(s["xt3_ready"], h * 2 + k + 1)
                        load_tokens(h * 2 + 2 + k, k)
                    for k in range(2):
                        pool.wait_ge(s["y_done"], (h * 2 + k) * 2 + 3)
                        load_weights(h * 2 + 2 + k, k)
                for k in range(2):
                    pool.wait_ge(y_stored[k], 16 * (E3 // 2) + 1)
                for t in range(TT):
                    nc.gpsimd.indirect_dma_start(out=YG[:, t, :], out_offset=None, in_=ybuf,
                                                 in_offset=bass.IndirectOffsetOnAxis(ap=SG[:, t:t + 1], axis=0))\
                        .then_inc(gathered[t // 8], 16)
                for g in range(TT // 8):
                    pool.wait_ge(gathered[g], 16 * 8)

            @block.tensor
            def _(pe):
                def turn_tokens(e, k, turn):
                    pe.wait_ge(x_ld[k], turn * 16 + 16)
                    for t in range(CT):
                        last = nc.tensor.transpose(P[t // 4][:, (t % 4) * 128:(t % 4 + 1) * 128], XB[:, k, t, :], ident[:, :])
                    last.then_inc(s["xt3_ready"], 1)

                def hidden(e, k, turn):
                    pe.wait_ge(w_ld[k], turn * 64 + 64)
                    pe.wait_ge(s["xt3_copied"], (e + k) * 2 + 2)
                    for j in range(4 * sub):
                        m, c = divmod(j, sub)
                        if j >= 4:
                            pe.wait_ge(s["h_done"], (e + k) * 4 * sub + j - 3)
                        nc.tensor.matmul(P[2 + j % 4][:, 0:cols], W1[:, k, m * 128:(m + 1) * 128],
                                         XT[:, k, c * cols:(c + 1) * cols], start=True, stop=True).then_inc(s["h_ready"], 1)

                def out(e, k):
                    pe.wait_ge(s["h_done"], (e + k + 1) * 4 * sub)
                    pe.wait_ge(s["y_done"], (e + k) * 2 + 1)
                    for t in range(CT):
                        for m in range(4):
                            last = nc.tensor.matmul(P[6 + t // 4][:, (t % 4) * 128:(t % 4 + 1) * 128],
                                                    H[:, k, m, t * 128:(t + 1) * 128], W2[:, k, m, :],
                                                    start=(m == 0), stop=(m == 3))
                    last.then_inc(s["y_ready"], 1)

                turn_tokens(0, 0, 0)
                with pe.Fori(0, E3 // 2 - 1) as turn:
                    e = turn * 2
                    hidden(e, 0, turn)
                    turn_tokens(e, 1, turn)
                    out(e, 0)
                    hidden(e, 1, turn)
                    turn_tokens(e + 2, 0, turn + 1)
                    out(e, 1)
                hidden(E3 - 2, 0, E3 // 2 - 1)
                turn_tokens(E3 - 2, 1, E3 // 2 - 1)
                out(E3 - 2, 0)
                hidden(E3 - 2, 1, E3 // 2 - 1)
                out(E3 - 2, 1)

            @block.scalar
            def _(act):
                with act.Fori(0, E3 // 2) as turn:
                    e = turn * 2
                    for k in range(2):
                        for j in range(4 * sub):
                            m, c = divmod(j, sub)
                            act.wait_ge(s["h_ready"], (e + k) * 4 * sub + j + 1)
                            nc.scalar.activation(H[:, k, m, c * cols:(c + 1) * cols], P[2 + j % 4][:, 0:cols], ACT.Relu,
                                                 bias=B1[:, k, m:m + 1])\
                                .then_inc(s["h_done"], 1)
                        act.wait_ge(s["y_done"], (e + k) * 2 + 3)
                        act.dma_start(ybuf[bass.ds((e + k) * CAP, CAP), :].rearrange("(t p) c -> p t c", p=128),
                                      YB[:, k, :, :]).then_inc(y_stored[k], 16)

            @block.vector
            def _(dve):
                nc.vector.memset(clamp[:, 0, 0:1], 0.0).then_inc(s["y_done"], 1)
                dve.wait_ge(s["y_done"], 1)
                for j, v in enumerate((0.0, 1e4, -1e4)):
                    ins = nc.vector.memset(clamp[:, j, :], v)
                    if j < 2:
                        ins.then_inc(y_stored[j], 1)
                ins.then_inc(s["cl"], 1)

                def tokens_turned(e, k):
                    dve.wait_ge(s["xt3_ready"], e + k + 1 if k else e + 1)
                    nc.vector.tensor_copy(XT[:, k, 0:HALF], P[0]).then_inc(s["xt3_copied"], 1)
                    nc.vector.tensor_copy(XT[:, k, HALF:], P[1][:, 0:CAP - HALF]).then_inc(s["xt3_copied"], 1)

                def experts(turn, more):
                    e = turn * 2
                    for k in range(2):
                        if k == 0:
                            tokens_turned(e, 1)
                        elif more:
                            tokens_turned(e + 2, 0)
                        dve.wait_ge(s["y_ready"], e + k + 1)
                        dve.wait_ge(y_stored[k], turn * 16 + 1)
                        nc.vector.tensor_tensor(YB[:, k, 0:4, :], P[6].rearrange("p (t c) -> p t c", t=4),
                                                B2[:, k:k + 1, :].broadcast_to([128, 4, C]), ALU.add).then_inc(s["y_done"], 1)
                        nc.vector.tensor_tensor(YB[:, k, 4:, :], P[7][:, 0:CAP - HALF].rearrange("p (t c) -> p t c", c=C),
                                                B2[:, k:k + 1, :].broadcast_to([128, CT - 4, C]), ALU.add).then_inc(s["y_done"], 1)

                tokens_turned(0, 0)
                with dve.Fori(0, E3 // 2 - 1) as turn:
                    experts(turn, True)
                experts(E3 // 2 - 1, False)
                dve.wait_ge(s["cl"], 1)
                link = Chain(dve, s["fin"])
                for t in range(0, TT, 8):
                    dve.wait_ge(gathered[t // 8], 16 * 8)
                    y = YG[:, t:t + 8, :]
                    link(nc.vector.tensor_tensor(y, y, RX[:, 7, t:t + 8, None].broadcast_to([128, 8, C]), ALU.mult))
                    big = float(np.finfo(np.float32).max)
                    for j in range(3):
                        if j == 0:
                            link(nc.vector.tensor_tensor(bad[:, :, :], y, y, ALU.not_equal))
                        else:
                            link(nc.vector.tensor_scalar(bad[:, :, :], y, big if j == 1 else -big, None,
                                                         ALU.is_gt if j == 1 else ALU.is_lt))
                        link(nc.vector.copy_predicated(y, bad[:, :, :], clamp[:, j, :].rearrange("p (a c) -> p a c", a=8)))
                    link(nc.vector.tensor_tensor(T[:, t:t + 8, :], T[:, t:t + 8, :], y, ALU.add))


H3 = 16
QUAD = 4
NQ = H3 // QUAD
DH = 64
VD = 32
QR_, KR_ = 48, 32
KEEP3 = 256
SMALL = QR_ + KR_ + VD + 3
PAIR = 256
RING = 6


def stage_attn3(nc, keep, PS, P, T, ident, identb, masks, lohi, below, tri, d):
    with ExitStack() as ctx:
        def sb(name, shape, dt=F32):
            return ctx.enter_context(nc.sbuf_tensor("a3_" + name, shape, dt))

        ln = norm_tiles(sb)
        XC = sb("XC", [C, N])
        with ExitStack() as early:
            def scratch(name, shape, dt=F32):
                return early.enter_context(nc.sbuf_tensor("a3_" + name, shape, dt))

            XN, SEL = scratch("XN", [128, NT, C]), scratch("SEL", [128, NT, KEEP3])
            row, ex = scratch("rk_row", [128, N]), scratch("rk_ex", [128, NT, 128])
            junk = scratch("rk_junk", [128, NT, N + 128], BF16)
            SQ, CK = scratch("SQ", [128, NT, QR_ + KR_]), scratch("CK", [128, NT, KR_ + VD + QR_])
            SM = scratch("SM", [128, NT, SMALL])
            CK2 = scratch("CK2", [128, NT, 2, KR_ + VD])
            t1, t2 = scratch("t1", [128, NT, VD]), scratch("t2", [128, NT, VD])
        QH, QL = sb("QH", [128, QUAD, N], F32R), sb("QL", [128, QUAD, N], F32R)
        K1, KW = sb("K1", [128, QUAD, N], F32R), sb("KW", [128, QUAD, N], F32R)
        rk = {"row": row, "ex": ex, "junk": junk,
              "col": sb("rk_col", [128, NT]), "cnt": sb("rk_cnt", [128, 3, NT]), "rank": sb("rk_rank", [128, NT])}
        WS = sb("WS", [C, SMALL])
        wimp = sb("wimp", [C, 1])
        wimpr = sb("wimpr", [C, 128])
        ms = sb("ms", [128, 3, 2, NT])
        nw = sb("nw", [128, QR_ + KR_])
        gs = sb("gs", [128, 6, 3])
        mean = sb("mean", [128, 128])
        ones = sb("ones", [128, 128])
        iota = sb("iota", [128, KEEP3])
        posn = sb("posn", [128, NT])
        cu = sb("cu", [128, 2, NT + 8])
        cosT, sinT = sb("cosT", [128, NT, VD]), sb("sinT", [128, NT, VD])
        CF = sb("CF", [KR_ + VD + QR_, N])
        CKF, CQF = CF[0:KR_ + VD, :], CF[KR_ + VD:, :]
        XS = sb("XS", [C, KEEP3])
        WQ = sb("WQ", [KR_ + VD + QR_, QUAD * DH])[KR_ + VD:, :]
        WKW, WKS = sb("WKW", [C, QUAD * DH]), sb("WKS", [C, QUAD * DH])
        CKS = sb("CKS", [128, N], F32R)
        WK1 = sb("WK1", [128, QUAD, 2, DH])
        WKH, WKL = sb("WKH", [128, QUAD, 2, DH], F32R), sb("WKL", [KR_ + VD, QUAD, 2, DH], F32R)
        WV = sb("WV", [KR_, QUAD * VD])
        WVW, WVS = sb("WVW", [C, QUAD * VD]), sb("WVS", [C, QUAD * VD])
        WP = sb("WP", [128, NQ, C])
        KS = sb("KS", [128, QUAD, KEEP3], F32R)
        K1B, KWB = sb("K1B", [128, QUAD, N], F32R), sb("KWB", [128, QUAD, N], F32R)
        KSB = sb("KSB", [128, QUAD, KEEP3], F32R)
        V1, VW, VS = sb("V1", [128, NT, 128]), sb("VW", [128, NT, 128]), sb("VS", [128, 2, 128])
        identr = sb("identr", [128, 128], F32R)
        NM = sb("NM", [128, 2, DH + 3 * QUAD], F32R)
        PT = sb("PT", [128, RING, QUAD * PAIR])
        TM = PT[:, 0:2, :].rearrange("p k (u r c) -> p k u r c", u=2 * QUAD, r=2)
        rot = PT[:, 2, :].rearrange("p (x k a h c) -> p x k a h c", x=2, k=2, a=2, h=QUAD)
        RA, RB = rot[:, 0, :, :, :, :], rot[:, 1, :, :, :, :]
        R = PT[:, 3, :].rearrange("p (k n) -> p k n", k=2).bitcast(F32R)
        RL, YB = sb("RL", [128, 2, PAIR]), sb("YB", [128, 3, PAIR])
        SV = sb("SV", [128, 2, PAIR])
        KT = sb("KT", [128, 2, QUAD, PAIR])
        YT = sb("YT", [128, 2, PAIR])
        names = NORM_SEMS + (
            "ld", "ready", "sm_ready", "sm_copied", "row_ready", "row_copied", "rk", "sel", "selt_ready", "gsum", "gmean", "gsub",
            "gexp", "gate", "rms", "rms_std", "latent", "lt_ready", "lt_copied", "onehot", "xs_ready", "xs_copied",
            "wk_ld", "prepared", "a_ready", "a_copied", "rope", "rope_added", "tr_ready", "tr_round", "tr_split",
            "b_ready", "b_round", "b_split", "v_copied", "s1_ready", "s23_ready", "max1", "max23", "doubled", "pos",
            "ck_twice", "ckt_ready", "ckt_round", "ckt_split", "wk_round", "wk_split", "zeroed", "rows", "filled", "taken", "weighed", "summed_pool", "summed_dve", "sum_ready", "inverted", "weights_copied", "added", "scaled", "yt_ready", "proj_ready")
        s = {n: keep.enter_context(nc.semaphore("a3_" + n)) for n in names}

        groups = [("s", 0), ("w", 0), ("q", 0)] + [("w", g) for g in range(1, 4)] + [("q", g) for g in range(1, 4)]
        NG = len(groups)
        plain = [("k1", h, half) for h in range(QUAD) for half in range(2)] + \
                [("v1", 0, 0), ("v1", 1, 0), ("vw", 0, 0), ("vw", 1, 0), ("vs", 0, 0)]
        nk1 = 2 * QUAD
        plain_bank = lambda k: P[6 + k % 2] if k < nk1 else P[5]
        LAG = 2
        plan = []
        left = list(range(len(plain)))
        for k in range(NG + LAG):
            early = {5: [0], 6: [1], 7: [2], 8: [3, 4], 9: [5, 6], 10: [7]}.get(k, [])
            products = [left.pop(0) for _ in range(2 if k < nk1 // 2 else 1) if left]
            plan.append((k if k < NG else None, products, k - LAG if k >= LAG else None, early))
        assert not left and sum((step[3] for step in plan), []) == list(range(2 * QUAD))

        units = [(i, h) for i in range(NT) for h in range(QUAD)]
        NU = len(units)
        win = lambda i: 256 if i else 128
        tiles = []
        for p in range(NT // 2):
            t = [(0, j * 128, 0, PAIR, {}) for j in range(2 * p)]
            t += [(0, 2 * p * 128, 0, PAIR, {0: 0}), (0, (2 * p + 1) * 128, 128, 128, {128: 0})]
            t += [(1, 0, 0, PAIR, {}), (1, 128, 0, PAIR, {})]
            t += [(2, 2 * p * 128, 0, PAIR, {0: 2, 128: 1})]
            t += [(2, (2 * p - 1) * 128, 0, 128, {0: 1})] if p else []
            t += [(2, (2 * p + 1) * 128, 128, 128, {128: 2})]
            tiles.append(t)
        NPAIR = len(tiles)
        flat = [(p, j) for p in range(NPAIR) for j in range(len(tiles[p]))]
        first_tile = [flat.index((p, 0)) for p in range(NPAIR)]
        NK = len(flat)
        LV = 2
        LD = 2
        steps = [("turn", 0), ("turn", 1)]
        for p in range(NPAIR):
            count = len(tiles[p])
            for j in range(count):
                steps.append(("score", first_tile[p] + j))
                if p + 1 < NPAIR:
                    steps += [("max", 2 * QUAD * (p + 1) + m) for m in range(2 * QUAD) if j == m * (count - 1) // (2 * QUAD)]
                if j >= LV:
                    steps.append(("value", first_tile[p] + j - LV))
            if p + 1 < NPAIR:
                steps += [("turn", 2 * p + 2), ("turn", 2 * p + 3)]
            steps += [("value", first_tile[p] + j) for j in range(count - LV, count)]

        def branch_edge(k, side):
            p, j = flat[k]
            return not 0 <= j + side < len(tiles[p]) or tiles[p][j + side][0] != tiles[p][j][0]

        def branch(k):
            return 3 * flat[k][0] + tiles[flat[k][0]][flat[k][1]][0]

        ends = [k for k in range(NK) if branch_edge(k, 1)]
        late = []
        for z, k in enumerate(ends):
            late.append((k + (LD + 1 if z == 3 * NPAIR - 2 else LD), ("sum", z)))
            if z % 3 == 2:
                late.append((k + LD + 2, ("project", z // 3)))
        for k, step in sorted(late, key=lambda x: x[0], reverse=True):
            place = steps.index(("value", k)) + 1 if k < NK else len(steps)
            steps.insert(place, step)
        tail = steps.index(("value", NK - 1)) + 1
        steps[tail:] = sorted(steps[tail:], key=lambda st: (st[1] if st[0] == "sum" else 3 * st[1] + 3, st[0] != "sum"))
        uses, act_steps = [], []
        for what, k in steps:
            new = []
            if what == "turn":
                new = [(what, k, 0)]
            elif what == "score":
                new = [(what, k, part) for part in range(2 if tiles[flat[k][0]][flat[k][1]][3] == PAIR else 1)]
            uses += new
            act_steps += new
            if what == "value" and branch_edge(k, 1):
                act_steps.append((what, k, 0))
        NE = len(uses)
        turning = lambda e: P[3 + e % 3]
        taken_after = lambda k: max(e for e, use in enumerate(uses) if use[:2] == ("score", k)) + 1
        additions = []
        for z in range(3 * NPAIR):
            k0 = next(k for k in range(NK) if branch(k) == z)
            begun = set()
            for k in range(k0 + 1, ends[z] + 1):
                q0, w = tiles[flat[k][0]][flat[k][1]][2:4]
                mine = {0, 128} if w == PAIR else {q0}
                additions.append((z, k, q0, w, None if mine & begun else k0, k))
                begun |= mine
            additions += [(z, ends[z], at, 128, k0, None) for at in (0, 128) if at not in begun]
        share_of = lambda z: "dve" if z in (3 * NPAIR - 3, 3 * NPAIR - 1) else "pool"
        share = {who: [a for a in additions if share_of(a[0]) == who] for who in ("pool", "dve")}
        summed = lambda who: s["summed_" + who]

        def last_use(k=None, z=None):
            who = share_of(branch(k) if z is None else z)
            return who, max(n for n, a in enumerate(share[who]) if (k in a[4:] if z is None else a[0] == z)) + 1

        def addition(eng, who, q, n):
            z, k, q0, w, one, other = share[who][n]
            total = KT[:, z % 2, :, q0:q0 + w]
            eng.wait_ge(s["taken"], q * NE + taken_after(k))
            if z >= 2 and (n == 0 or share[who][n - 1][0] != z):
                eng.wait_ge(s["sum_ready"], q * 3 * NPAIR + z - 1)
            if one is None:
                eng.wait_ge(summed(who), q * len(share[who]) + n)
            one_in = total if one is None else heads(one, PAIR)[:, :, q0:q0 + w]
            other_in = cu[:, 0, 0:1, None].broadcast_to([128, QUAD, w]) if other is None else heads(other, w)
            return total, one_in, other_in

        heads = lambda k, w: PT[:, k % RING, 0:QUAD * w].rearrange("p (h c) -> p h c", h=QUAD)
        last_bank = [st for st in steps if st[0] in ("sum", "project") and st != ("sum", 3 * NPAIR - 1)]
        sum_bank = lambda z: P[2] if z == 3 * NPAIR - 1 else P[7]
        q_scores = lambda n: (P[6], P[7]) if n < 2 * QUAD else (PS[:, 0:2, :].rearrange("p a n -> p (a n)"), P[2])
        keys, upper, vals = (K1, KS, KW), (K1B, KSB, KWB), (V1, VS, VW)

        NLD = 9
        WARM1, WARM2 = 28, 6
        ND = 5 + QUAD

        with nc.Block() as block:
            @block.sync
            def _(sp):
                for dst, src in ((WS[:, :], d["w_small"]), (wimp[:, :], d["w_imp"]), (nw[:, :], d["norm_w"].broadcast_to([128, 80])),
                                 (cosT[:, :, :], d["cos"]), (sinT[:, :, :], d["sin"]), (iota[:, :], d["iota"].broadcast_to([128, 256])),
                                 (WP[:, :, :], d["w_proj3"]), (WK1[0:KR_ + VD, :, :, :], d["wk1_const"]),
                                 (WK1[KR_ + VD:, :, :, :], d["wk1_const"])):
                    sp.dma_start(dst, src).then_inc(s["ld"], 16)

            @block.gpsimd
            def _(pool):
                nc.gpsimd.memset(ones[:, :], 1.0).then_inc(s["ready"], 1)
                nc.gpsimd.memset(mean[:, :], 1.0 / N).then_inc(s["ready"], 1)
                nc.gpsimd.memset(cu[:, :, 0:8], 0.0).then_inc(s["ready"], 1)
                pool.wait_ge(s["zeroed"], 4)
                for x, t in enumerate(upper):
                    pool.dma_start(t[DH:DH + 3, :, :].rearrange("p h n -> p (h n)"),
                                   d["branch_rows"][:, x, 0:QUAD * t.shape[2]]).then_inc(s["rows"], 16)
                pool.wait_ge(s["ld"], 16 * NLD)
                pool.wait_ge(s["rows"], 48)

                def double(q, k):
                    kind, g = groups[k]
                    if kind != "q":
                        c, x = 256 * g, {"w": 2, "s": 1}[kind]
                        pool.dma_start(upper[x][0:DH, :, c:c + 256], keys[x][0:DH, :, c:c + 256].bitcast(F32))\
                            .then_inc(s["doubled"], 16)

                def load_weights(g):
                    for dst, src in ((WQ[:, :], d["wq3"][bass.ds(g * QR_, QR_), :]),
                                     (WKW[:, :], d["wkw"][bass.ds(g * C, C), :]),
                                     (WKS[:, :], d["wks"][bass.ds(g * C, C), :]),
                                     (WV[:, :], d["wv"][bass.ds(g * KR_, KR_), :]),
                                     (WVW[:, :], d["wvw"][bass.ds(g * C, C), :]),
                                     (WVS[:, :], d["wvs"][bass.ds(g * C, C), :]),
                                     *((WK1[low:low + KR_, :, r, 0:32],
                                        d["wk1"][bass.ds(g * KR_, KR_), :].rearrange("p (h c) -> p h c", h=QUAD))
                                       for low in (0, KR_ + VD) for r in range(2))):
                        pool.dma_start(dst, src).then_inc(s["wk_ld"], 16)

                load_weights(0)
                with pool.Fori(0, B) as b:
                    with pool.Fori(0, NQ) as g:
                        q = b * NQ + g
                        for k in range(NG):
                            if k >= 3:
                                pool.wait_ge(s["tr_split"], q * 2 * NG + 2 * (k - 3) + 2)
                            if k == 7:
                                pool.wait_ge(s["b_split"], q * nk1 + nk1)
                            pool.wait_ge(s["rope"], q * NG + k + 1)
                            ra, rb = [x[:, k % 2, :, :, :].rearrange("p a h c -> p (a h) c")[:, :, None, :]
                                      .broadcast_to([128, 2 * QUAD, 2, VD]) for x in (RA, RB)]
                            nc.gpsimd.tensor_tensor(TM[:, k % 2, :, :, 32:], ra, rb, ALU.add)\
                                .then_inc(s["rope_added"], 1)
                            if k >= 3:
                                double(q, k - 3)
                            if k == 7:
                                for h in range(QUAD):
                                    pool.dma_start(K1B[0:DH, h, :], K1[0:DH, h, :].bitcast(F32)).then_inc(s["doubled"], 16)
                        pool.wait_ge(s["prepared"], q + 2)
                        load_weights(g + 1)
                        for n in range(len(share["pool"])):
                            total, one, other = addition(pool, "pool", q, n)
                            nc.gpsimd.tensor_tensor(total, one, other, ALU.add).then_inc(s["summed_pool"], 1)
                pool.wait_ge(s["wk_ld"], 160 * (B * NQ + 1))

            @block.tensor
            def _(pe):
                def group(q, k):
                    kind, g = groups[k]
                    if k >= 2:
                        pe.wait_ge(s["a_copied"], q * NG + k - 1)
                    src, w = {"q": (CQF, WQ), "w": (XC, WKW), "s": (XS, WKS)}[kind]
                    for j in range(2):
                        c = (2 * g + j) * 128
                        last = nc.tensor.matmul(P[k % 2][:, j * 256:(j + 1) * 256], src[:, c:c + 128], w[:, :],
                                                start=True, stop=True)
                    last.then_inc(s["a_ready"], 1)

                def plain_product(q, k):
                    kind, x, half = plain[k]
                    bank = plain_bank(k)
                    if 2 <= k < nk1:
                        pe.wait_ge(s["b_split"], q * nk1 + k - 1)
                    elif k > nk1:
                        pe.wait_ge(s["v_copied"], q * 5 + k - nk1)
                    if kind == "k1":
                        if k == 0:
                            pe.wait_ge(s["wk_split"], q + 1)
                        cols = slice(half * HALF, (half + 1) * HALF)
                        nc.tensor.matmul(bank, WKH[:, x, :, :].rearrange("p r c -> p (r c)"), CKS[:, cols], start=True, stop=False)
                        last = nc.tensor.matmul(bank, WKL[:, x, :, :].rearrange("p r c -> p (r c)"), CKS[0:KR_ + VD, cols],
                                                start=False, stop=True)
                    else:
                        src, w, nt = {"v1": (CKF[0:KR_, :], WV, 4), "vw": (XC[:, :], WVW, 4), "vs": (XS[:, :], WVS, 2)}[kind]
                        for t in range(nt):
                            c = (4 * x + t) * 128
                            last = nc.tensor.matmul(bank[:, t * 128:(t + 1) * 128], src[:, c:c + 128], w[:, :],
                                                    start=True, stop=True)
                    last.then_inc(s["b_ready"], 1)

                def turn_group(q, k):
                    pe.wait_ge(s["rope_added"], q * NG + k + 1)
                    for j in range(2):
                        u = 2 * k + j
                        if u >= 3:
                            pe.wait_ge(s["tr_split"], q * 2 * NG + u - 2)
                        for h in range(QUAD):
                            last = nc.tensor.transpose(P[2 + u % 3][:, h * 128:(h + 1) * 128],
                                                       TM[:, k % 2, j * QUAD + h, :, :].rearrange("p r c -> p (r c)"), ident[:, :])
                        last.then_inc(s["tr_ready"], 1)

                def query_major(q, n):
                    i, h = units[n]
                    S1, S23 = q_scores(n)
                    w, qh = (i + 1) * 128, QH[:, h, i * 128:(i + 1) * 128]
                    if n >= 1:
                        pe.wait_ge(s["max1"], q * NU + n)
                    for c0 in range(0, w, HALF):
                        c1 = min(w, c0 + HALF)
                        nc.tensor.matmul(S1[:, c0:c1], qh, K1[:, h, c0:c1], start=True, stop=c1 < w)
                    nc.tensor.matmul(S1[:, w - 128:w], identb[:, :], masks[:, 0, :], start=False, stop=True)\
                        .then_inc(s["s1_ready"], 1)
                    if n >= 1:
                        pe.wait_ge(s["max23"], q * NU + n)
                    k0, c = max(0, i - 1) * 128, HALF - win(i)
                    nc.tensor.matmul(S23[:, 0:KEEP3], qh, KS[:, h, :], start=True, stop=True)
                    nc.tensor.matmul(S23[:, c:], qh, KW[:, h, k0:(i + 1) * 128], start=True, stop=False)
                    nc.tensor.matmul(S23[:, c:], identb[:, :], masks[:, 1 if i else 2:3, :].rearrange("p a n -> p (a n)"),
                                     start=False, stop=True).then_inc(s["s23_ready"], 1)

                def turn_maxima(q, i):
                    e = uses.index(("turn", i, 0))
                    pe.wait_ge(s["max23"], q * NU + QUAD * (i + 1))
                    if e >= 3:
                        pe.wait_ge(s["taken"], q * NE + e - 2)
                    for h in range(QUAD):
                        last = nc.tensor.matmul(turning(e)[0:DH + 3, h * 128:(h + 1) * 128], NM[:, i % 2, 3 * h:3 * h + DH + 3], identr[:, :],
                                                start=True, stop=True)
                    last.then_inc(s["filled"], 1)

                def key_major(q, k):
                    p, j = flat[k]
                    x, c, q0, w, mask = tiles[p][j]
                    each = HALF // w
                    for part in range(QUAD // each):
                        e = uses.index(("score", k, part))
                        if j == 0 and part == 0:
                            pe.wait_ge(s["taken"], q * NE + e)
                        elif e >= 3:
                            pe.wait_ge(s["taken"], q * NE + e - 2)
                        for m in range(each):
                            h, start = part * each + m, p * PAIR + q0
                            out = turning(e)[:, m * w:(m + 1) * w]
                            nc.tensor.matmul(out, keys[x][:, h, c:c + 128], QH[:, h, start:start + w], start=True, stop=False)
                            last = nc.tensor.matmul(out, upper[x][:, h, c:c + 128], QL[:, h, start:start + w],
                                                    start=False, stop=not mask)
                            for at, which in mask.items():
                                last = nc.tensor.matmul(out[:, at - q0:at - q0 + 128], masks[:, which, :], identb[:, :],
                                                        start=False, stop=at == max(mask))
                        last.then_inc(s["filled"], 1)

                def values(q, k):
                    p, j = flat[k]
                    z, (x, c, q0, w, _) = branch(k), tiles[p][j]
                    pe.wait_ge(s["taken"], q * NE + taken_after(k))
                    first, final = branch_edge(k, -1), branch_edge(k, 1)
                    if first and z:
                        pe.wait_ge(s["weights_copied"], q * 3 * NPAIR + z)
                    for h in range(QUAD):
                        last = nc.tensor.matmul(P[6][h * VD:(h + 1) * VD, q0:q0 + w], vals[x][:, c // 128, h * VD:(h + 1) * VD],
                                                PT[:, k % RING, h * w:(h + 1) * w], start=first, stop=final)
                    last.then_inc(s["weighed"], 1)

                def last_bank_free(q, step):
                    u = last_bank.index(step)
                    if u:
                        what, k = last_bank[u - 1]
                        pe.wait_ge(s["inverted"] if what == "sum" else s["added"],
                                   q * (3 * NPAIR if what == "sum" else NPAIR) + k + 1)

                def denominators(q, z):
                    if z < 3 * NPAIR - 1:
                        last_bank_free(q, ("sum", z))
                    who, count = last_use(z=z)
                    pe.wait_ge(summed(who), q * len(share[who]) + count)
                    for h in range(QUAD):
                        last = nc.tensor.matmul(sum_bank(z)[h * VD:(h + 1) * VD, 0:PAIR], ones[:, h * VD:(h + 1) * VD],
                                                KT[:, z % 2, h, :], start=True, stop=True)
                    last.then_inc(s["sum_ready"], 1)

                def stay_warm(count):
                    for _ in range(count):
                        nc.tensor.matmul(P[0][:, 0:3 * 128], identb[:, :], masks[:, :, :].rearrange("p a n -> p (a n)"),
                                         start=True, stop=True)

                def project(q, g, p):
                    last_bank_free(q, ("project", p))
                    pe.wait_ge(s["yt_ready"], (q * NPAIR + p) * 2 + 2)
                    for j in range(2):
                        last = nc.tensor.matmul(P[7][:, j * 128:(j + 1) * 128], YT[:, p % 2, j * 128:(j + 1) * 128],
                                                WP[:, bass.ds(g, 1), :].rearrange("p a c -> p (a c)"), start=True, stop=True)
                    last.then_inc(s["proj_ready"], 1)

                pe.wait_ge(s["ready"], 5)
                pe.wait_ge(s["zeroed"], 4)
                with pe.Fori(0, B) as b:
                    norm_tensor(nc, pe, s, b, P, XN, ident)
                    pe.wait_ge(s["xc_ready"], b * 2 + 2)
                    for half in range(2):
                        nc.tensor.matmul(P[4 + half], wimpr[:, :], XC[:, half * HALF:(half + 1) * HALF],
                                         start=True, stop=True).then_inc(s["row_ready"], 1)
                    for half in range(2):
                        for t in range(4):
                            c = (4 * half + t) * 128
                            last = nc.tensor.matmul(P[2 + half][:, t * 128:t * 128 + SMALL], XC[:, c:c + 128], WS[:, :],
                                                    start=True, stop=True)
                        last.then_inc(s["sm_ready"], 1)
                    pe.wait_ge(s["gsum"], b + 1)
                    nc.tensor.matmul(P[6][:, 0:3], mean[:, :], gs[:, 0, :], start=True, stop=True).then_inc(s["gmean"], 1)
                    pe.wait_ge(s["latent"], b + 1)
                    for half in range(2):
                        for t in range(4):
                            last = nc.tensor.transpose(P[4 + half][0:KR_ + VD + QR_, t * 128:(t + 1) * 128],
                                                       CK[:, 4 * half + t, :], ident[:, :])
                        last.then_inc(s["lt_ready"], 1)
                    pe.wait_ge(s["ck_twice"], b + 1)
                    pe.wait_ge(s["sm_copied"], b * 2 + 2)
                    for half in range(2):
                        for t in range(4):
                            last = nc.tensor.transpose(P[2 + half][:, t * 128:(t + 1) * 128],
                                                       CK2[:, 4 * half + t, :, :].rearrange("p r c -> p (r c)"), ident[:, :])
                        last.then_inc(s["ckt_ready"], 1)
                    pe.wait_ge(s["sel"], b * 5 + 1)
                    nc.tensor.matmul(P[7][:, 0:NT], tri[:, :], rk["rank"][:, :], start=True, stop=True)
                    nc.tensor.matmul(P[7][:, NT:2 * NT], ones[:, :], rk["rank"][:, :], start=True, stop=True)\
                        .then_inc(s["selt_ready"], 1)
                    pe.wait_ge(s["onehot"], b + 1)
                    for t in range(NT):
                        last = nc.tensor.matmul(P[6][:, 0:KEEP3], XN[:, t, :], SEL[:, t, :], start=(t == 0), stop=(t == NT - 1))
                    last.then_inc(s["xs_ready"], 1)
                    with pe.Fori(0, NQ) as g:
                        q = b * NQ + g
                        pe.wait_ge(s["lt_copied"], b * 2 + 2)
                        pe.wait_ge(s["ckt_split"], b * 2 + 2)
                        pe.wait_ge(s["xs_copied"], b + 1)
                        pe.wait_ge(s["wk_ld"], q * 160 + 160)
                        for a, bs, t, early in plan:
                            if t is not None:
                                turn_group(q, t)
                            if a is not None:
                                group(q, a)
                            for k in bs:
                                plain_product(q, k)
                            for n in early:
                                if n == 0:
                                    pe.wait_ge(s["tr_split"], q * 2 * NG + 2 * 3)
                                    pe.wait_ge(s["b_split"], q * nk1 + nk1)
                                query_major(q, n)
                        pe.wait_ge(s["tr_split"], q * 2 * NG + 2 * NG)
                        pe.wait_ge(s["b_split"], q * nk1 + nk1)
                        pe.wait_ge(s["v_copied"], q * 5 + 5)
                        for what, k in steps:
                            if what == "max":
                                query_major(q, k)
                            elif what == "turn":
                                turn_maxima(q, k)
                            elif what == "score":
                                if k == 0:
                                    pe.wait_ge(s["doubled"], q * 16 * ND + 16 * ND)
                                key_major(q, k)
                            elif what == "value":
                                values(q, k)
                            elif what == "sum":
                                denominators(q, k)
                            else:
                                if k == NPAIR - 1:
                                    stay_warm(WARM1)
                                project(q, g, k)
                        stay_warm(WARM2)
                        pe.wait_ge(s["added"], q * NPAIR + NPAIR)

            @block.scalar
            def _(act):
                with act.Fori(0, B) as b:
                    norm_scalar(nc, act, s, b, P, XC, ln)
                    for half in range(2):
                        act.wait_ge(s["row_ready"], b * 2 + half + 1)
                        nc.scalar.activation(rk["row"][:, half * HALF:(half + 1) * HALF], P[4 + half], ACT.Copy)\
                            .then_inc(s["row_copied"], 1)
                    for half in range(2):
                        act.wait_ge(s["sm_ready"], b * 2 + half + 1)
                        nc.scalar.activation(SM[:, 4 * half:4 * half + 4, :],
                                             P[2 + half].rearrange("p (t c) -> p t c", t=4)[:, :, 0:SMALL], ACT.Copy)\
                            .then_inc(s["sm_copied"], 1)
                    act.wait_ge(s["rms"], b * 5 + 4)
                    nc.scalar.activation(ms[:, 1, :, :], ms[:, 0, :, :], ACT.Sqrt).then_inc(s["rms_std"], 1)
                    act.wait_ge(s["gsub"], b + 1)
                    nc.scalar.activation(gs[:, 3, :], gs[:, 2, :], ACT.Exp).then_inc(s["gexp"], 1)
                    act.wait_ge(s["latent"], b + 1)
                    nc.scalar.activation(CK2[:, :, :, :], CK[:, :, None, 0:KR_ + VD].broadcast_to([128, NT, 2, KR_ + VD]), ACT.Copy)\
                        .then_inc(s["ck_twice"], 1)
                    for half in range(2):
                        act.wait_ge(s["lt_ready"], b * 2 + half + 1)
                        nc.scalar.activation(CF[:, half * HALF:(half + 1) * HALF], P[4 + half][0:KR_ + VD + QR_, :], ACT.Copy)\
                            .then_inc(s["lt_copied"], 1)
                    for half in range(2):
                        act.wait_ge(s["ckt_ready"], b * 2 + half + 1)
                        nc.scalar.activation(CKS[:, half * HALF:(half + 1) * HALF], P[2 + half], ACT.Copy)\
                            .then_inc(s["ckt_round"], 1)
                    act.wait_ge(s["xs_ready"], b + 1)
                    nc.scalar.activation(XS[:, :], P[6][:, 0:KEEP3], ACT.Copy).then_inc(s["xs_copied"], 1)
                    act.wait_ge(s["gate"], b * 5 + 5)
                    with act.Fori(0, NQ) as g:
                        q = b * NQ + g
                        act.wait_ge(s["wk_ld"], q * 160 + 160)
                        nc.scalar.activation(WKH[:, :, :, :], WK1[:, :, :, :], ACT.Copy).then_inc(s["wk_round"], 1)
                        for a, bs, t, _ in plan:
                            if t is not None:
                                kind, g4 = groups[t]
                                for j in range(2):
                                    u, c = 2 * t + j, (2 * g4 + j) * 128
                                    dst = {"q": QH, "w": KW, "s": KS}[kind]
                                    act.wait_ge(s["tr_ready"], q * 2 * NG + u + 1)
                                    nc.scalar.activation(dst[:, :, c:c + 128], P[2 + u % 3].rearrange("p (h c) -> p h c", h=QUAD),
                                                         ACT.Copy, scale=0.125 if kind == "q" else 1.0).then_inc(s["tr_round"], 1)
                            if a is not None:
                                act.wait_ge(s["a_ready"], q * NG + a + 1)
                                if a >= 2:
                                    act.wait_ge(s["tr_ready"], q * 2 * NG + 2 * (a - 1))
                                nc.scalar.activation(TM[:, a % 2, :, :, :],
                                                     P[a % 2].rearrange("p (a c) -> p a c", c=DH)[:, :, None, :]
                                                     .broadcast_to([128, 2 * QUAD, 2, DH]), ACT.Copy)\
                                    .then_inc(s["a_copied"], 1)
                            for k in bs:
                                kind, x, half = plain[k]
                                act.wait_ge(s["b_ready"], q * len(plain) + k + 1)
                                if kind == "k1":
                                    if k >= 2:
                                        act.wait_ge(s["b_split"], q * nk1 + k - 1)
                                    nc.scalar.activation(R[:, k % 2, :], plain_bank(k), ACT.Copy).then_inc(s["b_round"], 1)
                                else:
                                    dst, nt = {"v1": (V1, 4), "vw": (VW, 4), "vs": (VS, 2)}[kind]
                                    g_of = {"v1": 0, "vs": 1, "vw": 2}
                                    nc.scalar.activation(dst[:, 4 * x:4 * x + nt, :].rearrange("p t c -> p (t c)"),
                                                         plain_bank(k)[:, 0:nt * 128], ACT.Identity,
                                                         scale=gs[:, 5, g_of[kind]:g_of[kind] + 1]).then_inc(s["v_copied"], 1)
                        e = -1
                        for what, k, part in act_steps:
                            if what == "value":
                                z = branch(k)
                                act.wait_ge(s["weighed"], q * NK + k + 1)
                                if z >= 2:
                                    act.wait_ge(s["scaled"], q * 3 * NPAIR + z - 1)
                                nc.scalar.activation(SV[:, z % 2, :], P[6][:, 0:PAIR], ACT.Copy)\
                                    .then_inc(s["weights_copied"], 1)
                                continue
                            e += 1
                            act.wait_ge(s["filled"], q * NE + e + 1)
                            if what == "turn":
                                nc.scalar.activation(QL[DH:DH + 3, :, k * 128:(k + 1) * 128],
                                                     turning(e)[DH:DH + 3, :].rearrange("p (h c) -> p h c", h=QUAD),
                                                     ACT.Copy).then_inc(s["taken"], 1)
                            else:
                                if part == 0 and k >= RING:
                                    act.wait_ge(s["weighed"], q * NK + k - RING + 1)
                                    who, count = last_use(k=k - RING)
                                    act.wait_ge(summed(who), q * len(share[who]) + count)
                                nc.scalar.activation(PT[:, k % RING, part * HALF:(part + 1) * HALF], turning(e),
                                                     ACT.Exp).then_inc(s["taken"], 1)

            @block.vector
            def _(dve):
                def maxima(q, n):
                    i, h = units[n]
                    S1, S23 = q_scores(n)
                    NMh = NM[:, i % 2, DH + 3 * h:DH + 3 * h + 3]
                    dve.wait_ge(s["s1_ready"], q * NU + n + 1)
                    nc.vector.tensor_reduce(NMh[:, 0:1], S1[:, 0:(i + 1) * 128], AX.X, ALU.max, negate=True)\
                        .then_inc(s["max1"], 1)
                    dve.wait_ge(s["s23_ready"], q * NU + n + 1)
                    if i:
                        ins = nc.vector.tensor_reduce(NMh[:, 1:3], S23.rearrange("p (a n) -> p a n", a=2), AX.X, ALU.max,
                                                      negate=True)
                    else:
                        nc.vector.tensor_reduce(NMh[:, 1:2], S23[:, 0:KEEP3], AX.X, ALU.max, negate=True)
                        ins = nc.vector.tensor_reduce(NMh[:, 2:3], S23[:, HALF - 128:], AX.X, ALU.max, negate=True)
                    ins.then_inc(s["max23"], 1)

                def normalise(q, z):
                    p, x = z // 3, z % 3
                    dve.wait_ge(s["sum_ready"], q * 3 * NPAIR + z + 1)
                    nc.vector.reciprocal(RL[:, z % 2, :], sum_bank(z)[:, 0:PAIR]).then_inc(s["inverted"], 1)
                    dve.wait_ge(s["weights_copied"], q * 3 * NPAIR + z + 1)
                    dve.wait_ge(s["inverted"], q * 3 * NPAIR + z + 1)
                    nc.vector.tensor_tensor(YB[:, x, :], SV[:, z % 2, :], RL[:, z % 2, :], ALU.mult).then_inc(s["scaled"], 1)
                    if x == 2:
                        dve.wait_ge(s["scaled"], q * 3 * NPAIR + z + 1)
                        nc.vector.tensor_tensor(YT[:, p % 2, :], YB[:, 0, :], YB[:, 1, :], ALU.add).then_inc(s["yt_ready"], 1)
                        dve.wait_ge(s["yt_ready"], (q * NPAIR + p) * 2 + 1)
                        nc.vector.tensor_tensor(YT[:, p % 2, :], YT[:, p % 2, :], YB[:, 2, :], ALU.add).then_inc(s["yt_ready"], 1)
                        dve.wait_ge(s["yt_ready"], (q * NPAIR + p) * 2 + 2)

                def residual(q, b, p):
                    dve.wait_ge(s["proj_ready"], q * NPAIR + p + 1)
                    t = T[:, bass.ds(b * NT + 2 * p, 2), :].rearrange("p a c -> p (a c)")
                    nc.vector.tensor_tensor(t, t, P[7][:, 0:PAIR], ALU.add).then_inc(s["added"], 1)

                def rotate(q, k):
                    kind, g = groups[k]
                    x = TM[:, k % 2, :, 0, 32:].rearrange("p (a h) c -> p a h c", a=2)
                    cos = cosT[:, 2 * g:2 * g + 2, None, :].broadcast_to([128, 2, QUAD, 32])
                    sin = sinT[:, 2 * g:2 * g + 2, None, :].broadcast_to([128, 2, QUAD, 32])
                    dve.wait_ge(s["a_copied"], q * NG + k + 1)
                    if k >= 2:
                        dve.wait_ge(s["rope_added"], q * NG + k - 1)
                    nc.vector.tensor_tensor(RA[:, k % 2, :, :, :], x, cos, ALU.mult)
                    nc.vector.tensor_tensor(RB[:, k % 2, :, :, 0:16], x[:, :, :, 16:], sin[:, :, :, 0:16], ALU.mult)
                    nc.vector.tensor_tensor(RB[:, k % 2, :, :, 16:], x[:, :, :, 0:16], sin[:, :, :, 16:], ALU.mult)\
                        .then_inc(s["rope"], 1)

                nc.vector.memset(NM[:, :, :].bitcast(F32), 0.0).then_inc(s["zeroed"], 1)
                for t in upper:
                    nc.vector.memset(t[DH:, :, :].bitcast(F32), 0.0).then_inc(s["zeroed"], 1)
                dve.wait_ge(s["ld"], 16 * NLD)
                nc.vector.memset(rk["cnt"][:, 0, 0:1], 0.0).then_inc(s["prepared"], 1)
                nc.vector.tensor_copy(wimpr[:, :], wimp[:, 0:1].broadcast_to([C, 128])).then_inc(s["ready"], 1)
                nc.vector.tensor_copy(identr[:, :], ident[:, :]).then_inc(s["ready"], 1)
                with dve.Fori(0, B) as b:
                    norm_vector(nc, dve, s, b, T, XN, ln)
                    dve.wait_ge(s["sm_copied"], b * 2 + 2)
                    nc.vector.tensor_reduce(gs[:, 0, :], SM[:, :, SMALL - 3:].rearrange("p t c -> p c t"), AX.X, ALU.add)\
                        .then_inc(s["gsum"], 1)
                    nc.vector.tensor_tensor(SQ[:, :, :], SM[:, :, 0:QR_ + KR_], SM[:, :, 0:QR_ + KR_], ALU.mult).then_inc(s["rms"], 1)
                    dve.wait_ge(s["rms"], b * 5 + 1)
                    nc.vector.tensor_reduce(ms[:, 2, 0, :], SQ[:, :, 0:QR_], AX.X, ALU.add).then_inc(s["rms"], 1)
                    nc.vector.tensor_reduce(ms[:, 2, 1, :], SQ[:, :, QR_:], AX.X, ALU.add).then_inc(s["rms"], 1)
                    dve.wait_ge(s["rms"], b * 5 + 3)
                    nc.vector.tensor_scalar(ms[:, 0, 0, :], ms[:, 2, 0, :], 1.0 / QR_, 1e-6, ALU.mult, ALU.add)
                    nc.vector.tensor_scalar(ms[:, 0, 1, :], ms[:, 2, 1, :], 1.0 / KR_, 1e-6, ALU.mult, ALU.add).then_inc(s["rms"], 1)
                    kr = SM[:, :, QR_ + KR_:QR_ + KR_ + VD]
                    nc.vector.tensor_tensor(t1[:, :, :], kr, cosT[:, :, :], ALU.mult)
                    nc.vector.tensor_tensor(t2[:, :, 0:16], kr[:, :, 16:], sinT[:, :, 0:16], ALU.mult)
                    nc.vector.tensor_tensor(t2[:, :, 16:], kr[:, :, 0:16], sinT[:, :, 16:], ALU.mult)
                    dve.wait_ge(s["rms_std"], b + 1)
                    nc.vector.reciprocal(ms[:, 2, :, :], ms[:, 1, :, :]).then_inc(s["rms"], 1)
                    dve.wait_ge(s["rms"], b * 5 + 5)
                    nc.vector.tensor_tensor(t1[:, :, :], t1[:, :, :], t2[:, :, :], ALU.add)
                    nc.vector.tensor_tensor(CK[:, :, KR_ + VD:], SM[:, :, 0:QR_],
                                            ms[:, 2, 0, :, None].broadcast_to([128, NT, QR_]), ALU.mult)
                    nc.vector.tensor_tensor(CK[:, :, 0:KR_], SM[:, :, QR_:QR_ + KR_],
                                            ms[:, 2, 1, :, None].broadcast_to([128, NT, KR_]), ALU.mult).then_inc(s["gate"], 1)
                    dve.wait_ge(s["gate"], b * 5 + 1)
                    nc.vector.tensor_scalar(CK[:, :, KR_:KR_ + VD], t1[:, :, :], 1.0 / H3, None, ALU.mult)
                    nc.vector.tensor_tensor(CK[:, :, KR_ + VD:], CK[:, :, KR_ + VD:],
                                            nw[:, None, 0:QR_].broadcast_to([128, NT, QR_]), ALU.mult)
                    nc.vector.tensor_tensor(CK[:, :, 0:KR_], CK[:, :, 0:KR_],
                                            nw[:, None, QR_:].broadcast_to([128, NT, KR_]), ALU.mult).then_inc(s["latent"], 1)
                    dve.wait_ge(s["gmean"], b + 1)
                    nc.vector.tensor_reduce(gs[:, 1, 0:1], P[6][:, 0:3], AX.X, ALU.max).then_inc(s["gate"], 1)
                    dve.wait_ge(s["gate"], b * 5 + 2)
                    nc.vector.tensor_scalar(gs[:, 2, :], P[6][:, 0:3], gs[:, 1, 0:1], None, ALU.subtract).then_inc(s["gsub"], 1)
                    dve.wait_ge(s["row_copied"], b * 2 + 2)
                    rank_vector(nc, dve, s, b, rk, ident, below, 5)
                    nc.vector.tensor_scalar(rk["rank"][:, :], rk["rank"][:, :], float(KEEP3), None, ALU.is_lt).then_inc(s["sel"], 1)
                    dve.wait_ge(s["gexp"], b + 1)
                    nc.vector.tensor_reduce(gs[:, 4, 0:1], gs[:, 3, :], AX.X, ALU.add).then_inc(s["gate"], 1)
                    dve.wait_ge(s["gate"], b * 5 + 3)
                    nc.vector.reciprocal(gs[:, 4, 1:2], gs[:, 4, 0:1]).then_inc(s["gate"], 1)
                    dve.wait_ge(s["gate"], b * 5 + 4)
                    nc.vector.tensor_scalar(gs[:, 5, :], gs[:, 3, :], gs[:, 4, 1:2], None, ALU.mult).then_inc(s["gate"], 1)
                    dve.wait_ge(s["selt_ready"], b + 1)
                    nc.vector.tensor_copy(cu[:, 0, 8:], P[7][:, NT:2 * NT]).then_inc(s["sel"], 1)
                    for k, sh in enumerate((1, 2, 4)):
                        dve.wait_ge(s["sel"], b * 5 + 2 + k)
                        nc.vector.tensor_tensor(cu[:, (k + 1) % 2, 8:], cu[:, k % 2, 8:], cu[:, k % 2, 8 - sh:8 + NT - sh], ALU.add)\
                            .then_inc(s["sel"], 1)
                    dve.wait_ge(s["sel"], b * 5 + 5)
                    link = dve.wait_ge
                    nc.vector.tensor_tensor(posn[:, :], P[7][:, 0:NT], cu[:, 1, 7:7 + NT], ALU.add).then_inc(s["pos"], 1)
                    link(s["pos"], b * 3 + 1)
                    nc.vector.tensor_tensor(posn[:, :], posn[:, :], rk["rank"][:, :], ALU.mult).then_inc(s["pos"], 1)
                    link(s["pos"], b * 3 + 2)
                    nc.vector.tensor_scalar(posn[:, :], posn[:, :], -1.0, None, ALU.add).then_inc(s["pos"], 1)
                    link(s["pos"], b * 3 + 3)
                    for t in range(NT):
                        ins = nc.vector.tensor_scalar(SEL[:, t, :], iota[:, :], posn[:, t:t + 1], None, ALU.is_equal)
                    ins.then_inc(s["onehot"], 1)
                    for half in range(2):
                        dve.wait_ge(s["ckt_round"], b * 2 + half + 1)
                        cks = CKS[:, half * HALF:(half + 1) * HALF]
                        nc.vector.scalar_tensor_tensor(out=cks, in0=cks.bitcast(F32), scalar=lohi[:, 0:1], in1=P[2 + half],
                                                       op0=ALU.mult, op1=ALU.add).then_inc(s["ckt_split"], 1)
                    with dve.Fori(0, NQ) as g:
                        q = b * NQ + g
                        dve.wait_ge(s["wk_round"], q + 1)
                        nc.vector.tensor_tensor(WKL[:, :, :, :], WK1[0:KR_ + VD, :, :, :], WKH[0:KR_ + VD, :, :, :].bitcast(F32),
                                                ALU.subtract).then_inc(s["wk_split"], 1)
                        for a, bs, t, early in plan:
                            if t is not None:
                                kind, g4 = groups[t]
                                for j in range(2):
                                    u, c = 2 * t + j, (2 * g4 + j) * 128
                                    dve.wait_ge(s["tr_round"], q * 2 * NG + u + 1)
                                    bank = P[2 + u % 3].rearrange("p (h c) -> p h c", h=QUAD)
                                    if kind == "q":
                                        ins = nc.vector.scalar_tensor_tensor(
                                            out=QL[:, :, c:c + 128], in0=bank, scalar=0.125,
                                            in1=QH[:, :, c:c + 128].bitcast(F32), op0=ALU.mult, op1=ALU.subtract)
                                    else:
                                        K = {"w": KW, "s": KS}[kind][:, :, c:c + 128]
                                        ins = nc.vector.scalar_tensor_tensor(out=K, in0=K.bitcast(F32), scalar=lohi[:, 0:1],
                                                                             in1=bank, op0=ALU.mult, op1=ALU.add)
                                    ins.then_inc(s["tr_split"], 1)
                            if a is not None:
                                rotate(q, a)
                            for k in bs:
                                kind, x, half = plain[k]
                                if kind == "k1":
                                    dve.wait_ge(s["b_round"], q * nk1 + k + 1)
                                    nc.vector.scalar_tensor_tensor(out=K1[:, x, half * HALF:(half + 1) * HALF],
                                                                   in0=R[:, k % 2, :].bitcast(F32), scalar=lohi[:, 0:1],
                                                                   in1=plain_bank(k), op0=ALU.mult, op1=ALU.add)\
                                        .then_inc(s["b_split"], 1)
                            for n in early:
                                maxima(q, n)
                        dve.wait_ge(s["tr_split"], q * 2 * NG + 2 * NG)
                        dve.wait_ge(s["v_copied"], q * 5 + 5)
                        nc.vector.memset(cu[:, 0, 0:1], 0.0).then_inc(s["prepared"], 1)
                        dve.wait_ge(s["prepared"], q + 2)
                        for what, k in steps:
                            if what == "max":
                                maxima(q, k)
                            elif what == "value":
                                for n, (_, last_tile, *_) in enumerate(share["dve"]):
                                    if last_tile == k:
                                        total, one, other = addition(dve, "dve", q, n)
                                        nc.vector.tensor_tensor(total, one, other, ALU.add).then_inc(s["summed_dve"], 1)
                            elif what == "sum":
                                normalise(q, k)
                            elif what == "project":
                                residual(q, b, k)
                        dve.wait_ge(s["added"], q * NPAIR + NPAIR)


def program(nc, d, out):
    with ExitStack() as ctx:
        def sb(name, shape, dt=F32):
            return ctx.enter_context(nc.sbuf_tensor(name, shape, dt))

        PS = ctx.enter_context(nc.psum_tensor("PS", [128, 8, HALF], F32))
        P = [PS[:, i, :] for i in range(8)]
        T = sb("T", [128, TT, C])
        ident, lohi = sb("ident", [128, 128]), sb("lohi", [128, 3])
        below, tri = sb("below", [128, 128]), sb("tri", [128, 128])
        maskf = sb("maskf", [128, 3, 128])
        identb, masks = sb("identb", [128, 128], BF16), sb("masks", [128, 3, 128], BF16)
        ld_c, stored, conv_c = [ctx.enter_context(nc.semaphore(n)) for n in ("ld_c", "stored", "conv_c")]
        with nc.Block() as block:
            @block.sync
            def _(sp):
                sp.dma_start(ident[:, :], d["ident"]).then_inc(ld_c, 16)
                sp.dma_start(lohi[:, :], d["lohi"]).then_inc(ld_c, 16)
                sp.dma_start(tri[:, :], d["tri"]).then_inc(ld_c, 16)
                sp.dma_start(below[:, :], d["below"]).then_inc(ld_c, 16)
                sp.dma_start(maskf[:, :, :], d["masks"]).then_inc(ld_c, 16)

            @block.vector
            def _(dve):
                dve.wait_ge(ld_c, 80)
                nc.vector.tensor_copy(identb[:, :], ident[:, :]).then_inc(conv_c, 1)
                nc.vector.tensor_copy(masks[:, :, :], maskf[:, :, :]).then_inc(conv_c, 1)
                dve.wait_ge(conv_c, 2)
        for stage, tiles in ((stage_conv, (P, T, ident, d)),
                             (stage_attn2, (PS, P, T, ident, identb, masks[:, 0, :], lohi, d)),
                             (stage_ffn2, (PS, P, T, ident, below, d)),
                             (stage_attn3, (PS, P, T, ident, identb, masks, lohi, below, tri, d)),
                             (stage_ffn3, (PS, P, T, ident, tri, d, out, stored))):
            keep = Semaphores(nc)
            stage(nc, keep, *tiles)
            keep.release()


def host_arrays(i):
    a = {k: np.asarray(v) for k, v in i.items()}
    f = np.float32
    m = np.cos((2.0 * np.arange(16)[:, None] + 1.0) * np.arange(4)[None, :] * np.pi / 32.0) / 16.0
    dct = np.einsum("hi,wj->hwij", m, m).reshape(2, 128, 16).transpose(1, 0, 2) / 4.0
    p = np.arange(128)
    lohi = np.zeros((128, 3))
    lohi[p >= 64, 0] = -1.0
    lohi[(p // 32) % 2 == 1, 1] = -1.0
    q, c = p[:, None], p[None, :]
    masks = np.stack([np.where(c <= q, 0.0, -1e30),
                      np.where(c - q > 64, 0.0, -1e30),
                      np.where((c <= q) & (q - c < 64), 0.0, -1e30)], 1)

    def wh(w, cols):
        w = w.reshape(w.shape[0], H3 // QUAD, QUAD * cols).transpose(1, 0, 2)
        return np.concatenate([w, w[0:1]]).reshape(-1, QUAD * cols)

    ang = np.outer(np.arange(N, dtype=f), 1.0 / 10000.0 ** (np.arange(0, 32, 2, dtype=f) / 32)).astype(f)
    cos, sin = [x.reshape(NT, 128, 16).transpose(1, 0, 2) for x in (np.cos(ang), np.sin(ang))]
    wk1c = np.zeros((64, QUAD, 2, DH), f)
    wk1c[32:, :, :, 32:] = np.eye(32, dtype=f)[:, None, None, :]
    nope, rope = a["L3_attn_Wq_nope"].reshape(48, H3, 32), a["L3_attn_Wq_rope"].reshape(48, H3, 32)
    return {
        "w_small": np.concatenate([a["L3_attn_Wcq"], a["L3_attn_Wckv"], a["L3_attn_Wk_rope"], a["L3_attn_Wgate"]], 1),
        "w_imp": a["L3_attn_W_imp"],
        "norm_w": np.concatenate([a["L3_attn_q_norm_w"], a["L3_attn_kv_norm_w"]])[None, :],
        "cos": np.concatenate([cos, cos], 2), "sin": np.concatenate([-sin, sin], 2),
        "branch_rows": np.repeat(np.eye(3, dtype=f)[:, :, None], 4 * 1024, 2),
        "iota": np.arange(256, dtype=f)[None, :], "w_proj3": a["L3_attn_Wproj"].reshape(4, 128, C).transpose(1, 0, 2),
        "wk1_const": wk1c, "wq3": wh(np.concatenate([nope, rope], 2).reshape(48, H3 * DH), DH),
        "wkw": wh(a["L3_attn_Wwin_k"], DH), "wks": wh(a["L3_attn_Wsel_k"], DH), "wv": wh(a["L3_attn_Wv"], VD),
        "wvw": wh(a["L3_attn_Wwin_v"], VD), "wvs": wh(a["L3_attn_Wsel_v"], VD), "wk1": wh(a["L3_attn_Wk_nope"], 32),
        "below": (c < q).astype(f), "tri": (q <= c).astype(f),
        "gate_w": a["L3_ffn_gate_w"], "gate_b": a["L3_ffn_gate_b"][None, :],
        "ecol": np.arange(E3, 0, -1, dtype=f)[None, :], "eslot": (np.arange(E3, dtype=f) * CAP - 1)[None, :],
        "tok": (SLOTS + np.arange(TT)[None, :] * 128 + p[:, None]).astype(f),
        "w1e": a["L3_ffn_w1"].reshape(E3 * C, F3), "b1e": a["L3_ffn_b1"].reshape(E3, 4, 128).transpose(0, 2, 1).reshape(E3 * 128, 4),
        "w2e": a["L3_ffn_w2"].reshape(E3, 4, 128, C).transpose(0, 2, 1, 3).reshape(E3 * 128, 4 * C),
        "b2e": a["L3_ffn_b2"],
        "wr": a["L2_ffn_wr"], "br": a["L2_ffn_br"][None, :], "w1": a["L2_ffn_w1"],
        "b1": a["L2_ffn_b1"].reshape(4, 128).T, "w2": a["L2_ffn_w2"].reshape(4, 128, C).transpose(1, 0, 2),
        "b2": a["L2_ffn_b2"][None, :],
        "lohi": lohi.astype(f), "masks": masks.astype(f),
        "W_attn": a["L2_attn_W_attn"], "W_proj2": a["L2_attn_W_proj"],
        "x": a["x"].reshape(B, C, N).transpose(1, 0, 2).reshape(C, B * N),
        "pg_w": np.concatenate([a["L0_conv_phi_w"].T, a["L0_conv_g_w"].T], 1),
        "pg_b": np.concatenate([a["L0_conv_phi_b"], a["L0_conv_g_b"]])[None, :],
        "theta_w": a["L0_conv_theta_w"], "theta_b": a["L0_conv_theta_b"][:, None],
        "w_wT": a["L0_conv_w_w"].T,
        "vec": np.stack([a["L0_conv_w_b"], a["L0_conv_gamma"], a["L0_conv_beta"]], 1),
        "experts": a["L1_conv_experts"].transpose(2, 0, 3, 4, 1).reshape(C, 8 * 9 * C),
        "w_f1": a["L1_conv_w_f1"], "b_f1": a["L1_conv_b_f1"][:, None], "w_f2": a["L1_conv_w_f2"],
        "b_f2": a["L1_conv_b_f2"][None, :], "w_r1": a["L1_conv_w_r1"], "b_r1": a["L1_conv_b_r1"][:, None],
        "w_r2": a["L1_conv_w_r2"], "b_r2": a["L1_conv_b_r2"][None, :],
        "ident": np.eye(128, dtype=f), "blk4": np.kron(np.eye(32), np.full((4, 4), 0.25)).astype(f),
        "dct": dct.astype(f),
    }


def kernel(**inputs):
    import numpy as _np
    import concourse.bacc as _bacc
    from concourse import mybir as _mybir
    from concourse.bass_utils import run_bass_kernel_spmd as _run

    nc = _bacc.Bacc("TRN2", target_bir_lowering=False, num_devices=1)
    arrays, aps = {}, {}
    for name, a in host_arrays(inputs).items():
        a = _np.ascontiguousarray(a)
        arrays["in_" + name] = a
        aps[name] = nc.dram_tensor("in_" + name, a.shape, _mybir.dt.from_np(a.dtype), kind="ExternalInput").ap()
    out = nc.dram_tensor("out_tokens", (128, TT, C), F32, kind="ExternalOutput").ap()
    program(nc, aps, out)
    r = _run(nc, [arrays], core_ids=[0])
    got = _np.asarray(r.results[0]["out_tokens"])
    return got.transpose(1, 0, 2).reshape(B, N, C).transpose(0, 2, 1).reshape(B, C, HW, HW)
```
